# Optimizing a Trainium2 kernel written in Bass

```python
import numpy as np
import jax
import jax.numpy as jnp

def _softmax(x, axis=-1):
    return jax.nn.softmax(x, axis=axis)

def _gelu(x):
    return jax.nn.gelu(x, approximate=True)

def _silu(x):
    return jax.nn.silu(x)

def _sigmoid(x):
    return jax.nn.sigmoid(x)

def _layernorm(x, axis=-1, eps=1e-05):
    m = jnp.mean(x, axis=axis, keepdims=True)
    v = jnp.var(x, axis=axis, keepdims=True)
    return (x - m) / jnp.sqrt(v + eps)

def _scatter_add(tgt, idx, src, axis=0):
    return tgt.at[idx].add(src)

def _segment_sum(src, seg, n):
    return jax.ops.segment_sum(src, seg, n)
kernel_name = 'mk_xattn_seq_d4_seqx_r8_b6ff55'

def setup_inputs(seed: int=0):
    np.random.seed(seed)
    _w = jnp.asarray

    def _rec_inputs():
        import jax
        import jax.numpy as jnp
        _rk = jax.random.key(seed)
        x = -0.000917 + 0.9994 * jax.random.normal(jax.random.fold_in(_rk, 1), (2, 512, 128), jnp.float32)
        _lenS = 512 - jax.random.randint(jax.random.fold_in(_rk, 7), (2,), 0, max(1, 512 // 4) + 1, jnp.int32)
        _lenS2 = 77 - jax.random.randint(jax.random.fold_in(_rk, 8), (2,), 0, max(1, 77 // 4) + 1, jnp.int32)
        _ctx_768P = jax.random.normal(jax.random.fold_in(_rk, 11), (2, 16, 96), jnp.float32)
        _ctx_768c = jax.random.dirichlet(jax.random.fold_in(_rk, 511), 0.3 * jnp.ones((16,), jnp.float32), (2, 77))
        _ctx_768t = jnp.einsum('bsk,bkd->bsd', _ctx_768c, _ctx_768P)
        _ctx_768t = _ctx_768t * jax.lax.rsqrt(jnp.mean(jnp.square(_ctx_768t)) + 1e-12) * 0.953939
        ctx_768 = 0.000947723 + 1.00027 * (_ctx_768t + 0.3 * jax.random.normal(jax.random.fold_in(_rk, 611), (2, 77, 96), jnp.float32))
        _validS = jnp.arange(512)[None, :] < _lenS[:, None]
        _validS2 = jnp.arange(77)[None, :] < _lenS2[:, None]
        _causal = jnp.tril(jnp.ones((512, 512), dtype=bool))
        mask_BxS_bf0 = jnp.logical_not(jnp.ones((2, 512), dtype=bool))
        mask_BxS2_bf0 = jnp.logical_not(jnp.ones((2, 77), dtype=bool))
        return (x, ctx_768, mask_BxS_bf0, mask_BxS2_bf0)
    x, ctx_768, mask_BxS_bf0, mask_BxS2_bf0 = _rec_inputs()

    def _L0_xattn_setup():
        import jax, jax.numpy as jnp
        import numpy as np
        D_DEC, D_ENC, H, D_MLP = (128, 96, 16, 512)
        HD = D_DEC // H

        def _layernorm(x, w, b, eps=1e-05):
            m = x.mean(-1, keepdims=True)
            v = ((x - m) ** 2).mean(-1, keepdims=True)
            return (x - m) / jnp.sqrt(v + eps) * w + b

        def _decoder_block(x, enc, tgt_mask, enc_mask, ln1_w, ln1_b, qkv_w, qkv_b, proj_w, proj_b, ln2_w, ln2_b, q_w, q_b, k_w, k_b, v_w, v_b, out_w, out_b, ln3_w, ln3_b, mlp1_w, mlp1_b, mlp2_w, mlp2_b):
            B, T, C = x.shape
            S = enc.shape[1]
            scale = HD ** (-0.5)
            neg = jnp.asarray(-jnp.inf, x.dtype)
            h = _layernorm(x, ln1_w, ln1_b)
            qkv = (h @ qkv_w + qkv_b).reshape(B, T, 3, H, HD)
            q, k, v = [qkv[:, :, i].transpose(0, 2, 1, 3) for i in range(3)]
            attn = jnp.einsum('bhtd,bhsd->bhts', q, k) * scale
            causal = jnp.triu(jnp.ones((T, T), bool), 1)
            attn = jnp.where(causal[None, None], neg, attn)
            attn = jnp.where(tgt_mask[:, None, None, :], neg, attn)
            attn = jax.nn.softmax(attn, axis=-1)
            sa = jnp.einsum('bhts,bhsd->bhtd', attn, v).transpose(0, 2, 1, 3).reshape(B, T, C)
            x = x + sa @ proj_w + proj_b
            h = _layernorm(x, ln2_w, ln2_b)
            q = (h @ q_w + q_b).reshape(B, T, H, HD).transpose(0, 2, 1, 3)
            k = (enc @ k_w + k_b).reshape(B, S, H, HD).transpose(0, 2, 1, 3)
            v = (enc @ v_w + v_b).reshape(B, S, H, HD).transpose(0, 2, 1, 3)
            attn = jnp.einsum('bhtd,bhsd->bhts', q, k) * scale
            attn = jnp.where(enc_mask[:, None, None, :], neg, attn)
            attn = jax.nn.softmax(attn, axis=-1)
            ca = jnp.einsum('bhts,bhsd->bhtd', attn, v).transpose(0, 2, 1, 3).reshape(B, T, C)
            x = x + ca @ out_w + out_b
            h = _layernorm(x, ln3_w, ln3_b)
            h = jax.nn.gelu(h @ mlp1_w + mlp1_b, approximate=False)
            x = x + h @ mlp2_w + mlp2_b
            return x
        key = jax.random.key(seed)
        ks = jax.random.split(key, 16)
        B, T, S = (4, 128, 72)

        def lin(k, din, dout):
            kw, kb = jax.random.split(k)
            bound = 1.0 / np.sqrt(din)
            W = jax.random.uniform(kw, (din, dout), jnp.float32, -bound, bound)
            b = jax.random.uniform(kb, (dout,), jnp.float32, -bound, bound)
            return (W, b)
        qkv_w, qkv_b = lin(ks[0], D_DEC, 3 * D_DEC)
        proj_w, proj_b = lin(ks[1], D_DEC, D_DEC)
        q_w, q_b = lin(ks[2], D_DEC, D_DEC)
        k_w, k_b = lin(ks[3], D_ENC, D_DEC)
        v_w, v_b = lin(ks[4], D_ENC, D_DEC)
        out_w, out_b = lin(ks[5], D_DEC, D_DEC)
        mlp1_w, mlp1_b = lin(ks[6], D_DEC, D_MLP)
        mlp2_w, mlp2_b = lin(ks[7], D_MLP, D_DEC)
        return {'x': jax.random.normal(ks[8], (B, T, D_DEC), jnp.float32), 'enc': jax.random.normal(ks[9], (B, S, D_ENC), jnp.float32), 'tgt_key_padding_mask': jnp.zeros((B, T), bool), 'enc_padding_mask': jnp.zeros((B, S), bool), 'ln1_w': jnp.ones((D_DEC,)), 'ln1_b': jnp.zeros((D_DEC,)), 'qkv_w': qkv_w, 'qkv_b': qkv_b, 'proj_w': proj_w, 'proj_b': proj_b, 'ln2_w': jnp.ones((D_DEC,)), 'ln2_b': jnp.zeros((D_DEC,)), 'q_w': q_w, 'q_b': q_b, 'k_w': k_w, 'k_b': k_b, 'v_w': v_w, 'v_b': v_b, 'out_w': out_w, 'out_b': out_b, 'ln3_w': jnp.ones((D_DEC,)), 'ln3_b': jnp.zeros((D_DEC,)), 'mlp1_w': mlp1_w, 'mlp1_b': mlp1_b, 'mlp2_w': mlp2_w, 'mlp2_b': mlp2_b}
    _L0_xattn_all = _L0_xattn_setup()
    _L0_xattn_in = {k: v for k, v in _L0_xattn_all.items() if k in ('ln1_w', 'ln1_b', 'qkv_w', 'qkv_b', 'proj_w', 'proj_b', 'ln2_w', 'ln2_b', 'q_w', 'q_b', 'k_w', 'k_b', 'v_w', 'v_b', 'out_w', 'out_b', 'ln3_w', 'ln3_b', 'mlp1_w', 'mlp1_b', 'mlp2_w', 'mlp2_b')}
    del _L0_xattn_all

    def _L1_xattn_setup():
        import jax, jax.numpy as jnp
        import numpy as np
        LATENT = 128
        TEXT = 96
        HEADS = 16
        HEAD_DIM = LATENT // HEADS
        SCALE = HEAD_DIM ** (-0.5)
        LN_EPS = 1e-05
        key = jax.random.key(seed)
        ks = jax.random.split(key, 16)
        B, Tx, Txf = (4, 512, 32)

        def lin(k, fan_in, fan_out):
            bound = 1.0 / np.sqrt(fan_in)
            kw, kb = jax.random.split(k)
            W = jax.random.uniform(kw, (fan_in, fan_out), jnp.float32, -bound, bound)
            b = jax.random.uniform(kb, (fan_out,), jnp.float32, -bound, bound)
            return (W, b)
        Wq, bq = lin(ks[0], LATENT, LATENT)
        Wk, bk = lin(ks[1], TEXT, LATENT)
        Wv, bv = lin(ks[2], TEXT, LATENT)
        Wo, bo = lin(ks[3], LATENT, LATENT)
        W1, b1 = lin(ks[4], LATENT, 4 * LATENT)
        W2, b2 = lin(ks[5], 4 * LATENT, LATENT)
        return {'x': jax.random.normal(ks[6], (B, Tx, LATENT), jnp.float32), 'xf': jax.random.normal(ks[7], (B, Txf, TEXT), jnp.float32), 'Wq': Wq, 'bq': bq, 'Wk': Wk, 'bk': bk, 'Wv': Wv, 'bv': bv, 'Wo': Wo, 'bo': bo, 'ln_g': jnp.ones((LATENT,), jnp.float32), 'ln_b': jnp.zeros((LATENT,), jnp.float32), 'W1': W1, 'b1': b1, 'W2': W2, 'b2': b2}
    _L1_xattn_all = _L1_xattn_setup()
    _L1_xattn_in = {k: v for k, v in _L1_xattn_all.items() if k in ('Wq', 'bq', 'Wk', 'bk', 'Wv', 'bv', 'Wo', 'bo', 'ln_g', 'ln_b', 'W1', 'b1', 'W2', 'b2')}
    del _L1_xattn_all

    def _L2_xattn_setup():
        import jax, jax.numpy as jnp
        import numpy as np
        D_MODEL = 128
        D_COND = 96
        N_HEADS = 16
        D_HEAD = 64
        D_ATTN = N_HEADS * D_HEAD
        D_FF = 4 * D_MODEL

        def _layernorm(x, g, b, eps=1e-05):
            mu = jnp.mean(x, axis=-1, keepdims=True)
            var = jnp.var(x, axis=-1, keepdims=True)
            return (x - mu) * jax.lax.rsqrt(var + eps) * g + b

        def _attention(xq, xkv, wq, wk, wv, wo, bo):
            B, S, _ = xq.shape
            T = xkv.shape[1]
            q = (xq @ wq).reshape(B, S, N_HEADS, D_HEAD)
            k = (xkv @ wk).reshape(B, T, N_HEADS, D_HEAD)
            v = (xkv @ wv).reshape(B, T, N_HEADS, D_HEAD)
            scale = D_HEAD ** (-0.5)
            attn = jnp.einsum('bihd,bjhd->bhij', q, k) * scale
            attn = jax.nn.softmax(attn, axis=-1)
            out = jnp.einsum('bhij,bjhd->bihd', attn, v).reshape(B, S, D_ATTN)
            return out @ wo + bo
        key = jax.random.key(seed)
        ks = jax.random.split(key, 16)
        B, S, T = (8, 128, 32)
        n = jax.random.normal
        inp = {'x': n(ks[0], (B, S, D_MODEL), jnp.float32), 'cond_emb': n(ks[1], (B, T, D_COND), jnp.float32), 'ln1_g': jnp.ones((D_MODEL,), jnp.float32), 'ln1_b': jnp.zeros((D_MODEL,), jnp.float32), 'ln2_g': jnp.ones((D_MODEL,), jnp.float32), 'ln2_b': jnp.zeros((D_MODEL,), jnp.float32), 'ln3_g': jnp.ones((D_MODEL,), jnp.float32), 'ln3_b': jnp.zeros((D_MODEL,), jnp.float32), 'sa_wq': n(ks[2], (D_MODEL, D_ATTN), jnp.float32) * D_MODEL ** (-0.5), 'sa_wk': n(ks[3], (D_MODEL, D_ATTN), jnp.float32) * D_MODEL ** (-0.5), 'sa_wv': n(ks[4], (D_MODEL, D_ATTN), jnp.float32) * D_MODEL ** (-0.5), 'sa_wo': n(ks[5], (D_ATTN, D_MODEL), jnp.float32) * D_ATTN ** (-0.5), 'sa_bo': jnp.zeros((D_MODEL,), jnp.float32), 'ca_wq': n(ks[6], (D_MODEL, D_ATTN), jnp.float32) * D_MODEL ** (-0.5), 'ca_wk': n(ks[7], (D_COND, D_ATTN), jnp.float32) * D_COND ** (-0.5), 'ca_wv': n(ks[8], (D_COND, D_ATTN), jnp.float32) * D_COND ** (-0.5), 'ca_wo': n(ks[9], (D_ATTN, D_MODEL), jnp.float32) * D_ATTN ** (-0.5), 'ca_bo': jnp.zeros((D_MODEL,), jnp.float32), 'ff_w1': n(ks[10], (D_MODEL, 2 * D_FF), jnp.float32) * D_MODEL ** (-0.5), 'ff_b1': jnp.zeros((2 * D_FF,), jnp.float32), 'ff_w2': n(ks[11], (D_FF, D_MODEL), jnp.float32) * D_FF ** (-0.5), 'ff_b2': jnp.zeros((D_MODEL,), jnp.float32)}
        return inp
    _L2_xattn_all = _L2_xattn_setup()
    _L2_xattn_in = {k: v for k, v in _L2_xattn_all.items() if k in ('ln1_g', 'ln1_b', 'ln2_g', 'ln2_b', 'ln3_g', 'ln3_b', 'sa_wq', 'sa_wk', 'sa_wv', 'sa_wo', 'sa_bo', 'ca_wq', 'ca_wk', 'ca_wv', 'ca_wo', 'ca_bo', 'ff_w1', 'ff_b1', 'ff_w2', 'ff_b2')}
    del _L2_xattn_all

    def _L3_xattn_setup():
        import jax, jax.numpy as jnp
        import numpy as np
        B, S, D = (4, 256, 128)
        CTX_LEN, CTX_DIM = (77, 96)
        H, DH = (16, 64)
        INNER = H * DH
        MULT = 4
        EPS = 1e-05

        def _layernorm(x, g, b):
            mu = jnp.mean(x, axis=-1, keepdims=True)
            var = jnp.var(x, axis=-1, keepdims=True)
            return (x - mu) * jax.lax.rsqrt(var + EPS) * g + b

        def _attn(xq, xkv, wq, wk, wv, wo, bo):
            b, sq, _ = xq.shape
            sk = xkv.shape[1]
            q = (xq @ wq).reshape(b, sq, H, DH)
            k = (xkv @ wk).reshape(b, sk, H, DH)
            v = (xkv @ wv).reshape(b, sk, H, DH)
            score = jnp.einsum('bqhd,bkhd->bhqk', q, k) * DH ** (-0.5)
            w = jax.nn.softmax(score, axis=-1)
            o = jnp.einsum('bhqk,bkhd->bqhd', w, v).reshape(b, sq, INNER)
            return o @ wo + bo

        def _block(x, context, ln1_g, ln1_b, ln2_g, ln2_b, ln3_g, ln3_b, a1_wq, a1_wk, a1_wv, a1_wo, a1_bo, a2_wq, a2_wk, a2_wv, a2_wo, a2_bo, ff_w1, ff_b1, ff_w2, ff_b2):
            x = _attn(_layernorm(x, ln1_g, ln1_b), _layernorm(x, ln1_g, ln1_b), a1_wq, a1_wk, a1_wv, a1_wo, a1_bo) + x
            x = _attn(_layernorm(x, ln2_g, ln2_b), context, a2_wq, a2_wk, a2_wv, a2_wo, a2_bo) + x
            h = _layernorm(x, ln3_g, ln3_b) @ ff_w1 + ff_b1
            u, gate = jnp.split(h, 2, axis=-1)
            x = u * jax.nn.gelu(gate, approximate=False) @ ff_w2 + ff_b2 + x
            return x
        key = jax.random.key(seed)
        ks = jax.random.split(key, 14)
        nrm = lambda k, shape: jax.random.normal(k, shape, dtype=jnp.float32) * 0.02
        return {'x': jax.random.normal(ks[0], (B, S, D), dtype=jnp.float32), 'context': jax.random.normal(ks[1], (B, CTX_LEN, CTX_DIM), dtype=jnp.float32), 'ln1_g': jnp.ones((D,), jnp.float32), 'ln1_b': jnp.zeros((D,), jnp.float32), 'ln2_g': jnp.ones((D,), jnp.float32), 'ln2_b': jnp.zeros((D,), jnp.float32), 'ln3_g': jnp.ones((D,), jnp.float32), 'ln3_b': jnp.zeros((D,), jnp.float32), 'a1_wq': nrm(ks[2], (D, INNER)), 'a1_wk': nrm(ks[3], (D, INNER)), 'a1_wv': nrm(ks[4], (D, INNER)), 'a1_wo': nrm(ks[5], (INNER, D)), 'a1_bo': jnp.zeros((D,), jnp.float32), 'a2_wq': nrm(ks[6], (D, INNER)), 'a2_wk': nrm(ks[7], (CTX_DIM, INNER)), 'a2_wv': nrm(ks[8], (CTX_DIM, INNER)), 'a2_wo': nrm(ks[9], (INNER, D)), 'a2_bo': jnp.zeros((D,), jnp.float32), 'ff_w1': nrm(ks[10], (D, D * MULT * 2)), 'ff_b1': jnp.zeros((D * MULT * 2,), jnp.float32), 'ff_w2': nrm(ks[11], (D * MULT, D)), 'ff_b2': jnp.zeros((D,), jnp.float32)}
    _L3_xattn_all = _L3_xattn_setup()
    _L3_xattn_in = {k: v for k, v in _L3_xattn_all.items() if k in ('ln1_g', 'ln1_b', 'ln2_g', 'ln2_b', 'ln3_g', 'ln3_b', 'a1_wq', 'a1_wk', 'a1_wv', 'a1_wo', 'a1_bo', 'a2_wq', 'a2_wk', 'a2_wv', 'a2_wo', 'a2_bo', 'ff_w1', 'ff_b1', 'ff_w2', 'ff_b2')}
    del _L3_xattn_all
    return {'x': x, 'ctx_768': ctx_768, 'mask_BxS_bf0': mask_BxS_bf0, 'mask_BxS2_bf0': mask_BxS2_bf0, 'L0_xattn_ln1_w': _L0_xattn_in['ln1_w'], 'L0_xattn_ln1_b': _L0_xattn_in['ln1_b'], 'L0_xattn_qkv_w': _L0_xattn_in['qkv_w'], 'L0_xattn_qkv_b': _L0_xattn_in['qkv_b'], 'L0_xattn_proj_w': _L0_xattn_in['proj_w'], 'L0_xattn_proj_b': _L0_xattn_in['proj_b'], 'L0_xattn_ln2_w': _L0_xattn_in['ln2_w'], 'L0_xattn_ln2_b': _L0_xattn_in['ln2_b'], 'L0_xattn_q_w': _L0_xattn_in['q_w'], 'L0_xattn_q_b': _L0_xattn_in['q_b'], 'L0_xattn_k_w': _L0_xattn_in['k_w'], 'L0_xattn_k_b': _L0_xattn_in['k_b'], 'L0_xattn_v_w': _L0_xattn_in['v_w'], 'L0_xattn_v_b': _L0_xattn_in['v_b'], 'L0_xattn_out_w': _L0_xattn_in['out_w'], 'L0_xattn_out_b': _L0_xattn_in['out_b'], 'L0_xattn_ln3_w': _L0_xattn_in['ln3_w'], 'L0_xattn_ln3_b': _L0_xattn_in['ln3_b'], 'L0_xattn_mlp1_w': _L0_xattn_in['mlp1_w'], 'L0_xattn_mlp1_b': _L0_xattn_in['mlp1_b'], 'L0_xattn_mlp2_w': _L0_xattn_in['mlp2_w'], 'L0_xattn_mlp2_b': _L0_xattn_in['mlp2_b'], 'L1_xattn_Wq': _L1_xattn_in['Wq'], 'L1_xattn_bq': _L1_xattn_in['bq'], 'L1_xattn_Wk': _L1_xattn_in['Wk'], 'L1_xattn_bk': _L1_xattn_in['bk'], 'L1_xattn_Wv': _L1_xattn_in['Wv'], 'L1_xattn_bv': _L1_xattn_in['bv'], 'L1_xattn_Wo': _L1_xattn_in['Wo'], 'L1_xattn_bo': _L1_xattn_in['bo'], 'L1_xattn_ln_g': _L1_xattn_in['ln_g'], 'L1_xattn_ln_b': _L1_xattn_in['ln_b'], 'L1_xattn_W1': _L1_xattn_in['W1'], 'L1_xattn_b1': _L1_xattn_in['b1'], 'L1_xattn_W2': _L1_xattn_in['W2'], 'L1_xattn_b2': _L1_xattn_in['b2'], 'L2_xattn_ln1_g': _L2_xattn_in['ln1_g'], 'L2_xattn_ln1_b': _L2_xattn_in['ln1_b'], 'L2_xattn_ln2_g': _L2_xattn_in['ln2_g'], 'L2_xattn_ln2_b': _L2_xattn_in['ln2_b'], 'L2_xattn_ln3_g': _L2_xattn_in['ln3_g'], 'L2_xattn_ln3_b': _L2_xattn_in['ln3_b'], 'L2_xattn_sa_wq': _L2_xattn_in['sa_wq'], 'L2_xattn_sa_wk': _L2_xattn_in['sa_wk'], 'L2_xattn_sa_wv': _L2_xattn_in['sa_wv'], 'L2_xattn_sa_wo': _L2_xattn_in['sa_wo'], 'L2_xattn_sa_bo': _L2_xattn_in['sa_bo'], 'L2_xattn_ca_wq': _L2_xattn_in['ca_wq'], 'L2_xattn_ca_wk': _L2_xattn_in['ca_wk'], 'L2_xattn_ca_wv': _L2_xattn_in['ca_wv'], 'L2_xattn_ca_wo': _L2_xattn_in['ca_wo'], 'L2_xattn_ca_bo': _L2_xattn_in['ca_bo'], 'L2_xattn_ff_w1': _L2_xattn_in['ff_w1'], 'L2_xattn_ff_b1': _L2_xattn_in['ff_b1'], 'L2_xattn_ff_w2': _L2_xattn_in['ff_w2'], 'L2_xattn_ff_b2': _L2_xattn_in['ff_b2'], 'L3_xattn_ln1_g': _L3_xattn_in['ln1_g'], 'L3_xattn_ln1_b': _L3_xattn_in['ln1_b'], 'L3_xattn_ln2_g': _L3_xattn_in['ln2_g'], 'L3_xattn_ln2_b': _L3_xattn_in['ln2_b'], 'L3_xattn_ln3_g': _L3_xattn_in['ln3_g'], 'L3_xattn_ln3_b': _L3_xattn_in['ln3_b'], 'L3_xattn_a1_wq': _L3_xattn_in['a1_wq'], 'L3_xattn_a1_wk': _L3_xattn_in['a1_wk'], 'L3_xattn_a1_wv': _L3_xattn_in['a1_wv'], 'L3_xattn_a1_wo': _L3_xattn_in['a1_wo'], 'L3_xattn_a1_bo': _L3_xattn_in['a1_bo'], 'L3_xattn_a2_wq': _L3_xattn_in['a2_wq'], 'L3_xattn_a2_wk': _L3_xattn_in['a2_wk'], 'L3_xattn_a2_wv': _L3_xattn_in['a2_wv'], 'L3_xattn_a2_wo': _L3_xattn_in['a2_wo'], 'L3_xattn_a2_bo': _L3_xattn_in['a2_bo'], 'L3_xattn_ff_w1': _L3_xattn_in['ff_w1'], 'L3_xattn_ff_b1': _L3_xattn_in['ff_b1'], 'L3_xattn_ff_w2': _L3_xattn_in['ff_w2'], 'L3_xattn_ff_b2': _L3_xattn_in['ff_b2']}

def reference(x, ctx_768, mask_BxS_bf0, mask_BxS2_bf0, L0_xattn_ln1_w, L0_xattn_ln1_b, L0_xattn_qkv_w, L0_xattn_qkv_b, L0_xattn_proj_w, L0_xattn_proj_b, L0_xattn_ln2_w, L0_xattn_ln2_b, L0_xattn_q_w, L0_xattn_q_b, L0_xattn_k_w, L0_xattn_k_b, L0_xattn_v_w, L0_xattn_v_b, L0_xattn_out_w, L0_xattn_out_b, L0_xattn_ln3_w, L0_xattn_ln3_b, L0_xattn_mlp1_w, L0_xattn_mlp1_b, L0_xattn_mlp2_w, L0_xattn_mlp2_b, L1_xattn_Wq, L1_xattn_bq, L1_xattn_Wk, L1_xattn_bk, L1_xattn_Wv, L1_xattn_bv, L1_xattn_Wo, L1_xattn_bo, L1_xattn_ln_g, L1_xattn_ln_b, L1_xattn_W1, L1_xattn_b1, L1_xattn_W2, L1_xattn_b2, L2_xattn_ln1_g, L2_xattn_ln1_b, L2_xattn_ln2_g, L2_xattn_ln2_b, L2_xattn_ln3_g, L2_xattn_ln3_b, L2_xattn_sa_wq, L2_xattn_sa_wk, L2_xattn_sa_wv, L2_xattn_sa_wo, L2_xattn_sa_bo, L2_xattn_ca_wq, L2_xattn_ca_wk, L2_xattn_ca_wv, L2_xattn_ca_wo, L2_xattn_ca_bo, L2_xattn_ff_w1, L2_xattn_ff_b1, L2_xattn_ff_w2, L2_xattn_ff_b2, L3_xattn_ln1_g, L3_xattn_ln1_b, L3_xattn_ln2_g, L3_xattn_ln2_b, L3_xattn_ln3_g, L3_xattn_ln3_b, L3_xattn_a1_wq, L3_xattn_a1_wk, L3_xattn_a1_wv, L3_xattn_a1_wo, L3_xattn_a1_bo, L3_xattn_a2_wq, L3_xattn_a2_wk, L3_xattn_a2_wv, L3_xattn_a2_wo, L3_xattn_a2_bo, L3_xattn_ff_w1, L3_xattn_ff_b1, L3_xattn_ff_w2, L3_xattn_ff_b2):
    import jax
    import jax.numpy as jnp

    def _L0_xattn_ref(x, enc, tgt_key_padding_mask, enc_padding_mask, ln1_w, ln1_b, qkv_w, qkv_b, proj_w, proj_b, ln2_w, ln2_b, q_w, q_b, k_w, k_b, v_w, v_b, out_w, out_b, ln3_w, ln3_b, mlp1_w, mlp1_b, mlp2_w, mlp2_b):
        import jax, jax.numpy as jnp
        import numpy as np
        D_DEC, D_ENC, H, D_MLP = (128, 96, 16, 512)
        HD = D_DEC // H

        def _layernorm(x, w, b, eps=1e-05):
            m = x.mean(-1, keepdims=True)
            v = ((x - m) ** 2).mean(-1, keepdims=True)
            return (x - m) / jnp.sqrt(v + eps) * w + b

        def _decoder_block(x, enc, tgt_mask, enc_mask, ln1_w, ln1_b, qkv_w, qkv_b, proj_w, proj_b, ln2_w, ln2_b, q_w, q_b, k_w, k_b, v_w, v_b, out_w, out_b, ln3_w, ln3_b, mlp1_w, mlp1_b, mlp2_w, mlp2_b):
            B, T, C = x.shape
            S = enc.shape[1]
            scale = HD ** (-0.5)
            neg = jnp.asarray(-jnp.inf, x.dtype)
            h = _layernorm(x, ln1_w, ln1_b)
            qkv = (h @ qkv_w + qkv_b).reshape(B, T, 3, H, HD)
            q, k, v = [qkv[:, :, i].transpose(0, 2, 1, 3) for i in range(3)]
            attn = jnp.einsum('bhtd,bhsd->bhts', q, k) * scale
            causal = jnp.triu(jnp.ones((T, T), bool), 1)
            attn = jnp.where(causal[None, None], neg, attn)
            attn = jnp.where(tgt_mask[:, None, None, :], neg, attn)
            attn = jax.nn.softmax(attn, axis=-1)
            sa = jnp.einsum('bhts,bhsd->bhtd', attn, v).transpose(0, 2, 1, 3).reshape(B, T, C)
            x = x + sa @ proj_w + proj_b
            h = _layernorm(x, ln2_w, ln2_b)
            q = (h @ q_w + q_b).reshape(B, T, H, HD).transpose(0, 2, 1, 3)
            k = (enc @ k_w + k_b).reshape(B, S, H, HD).transpose(0, 2, 1, 3)
            v = (enc @ v_w + v_b).reshape(B, S, H, HD).transpose(0, 2, 1, 3)
            attn = jnp.einsum('bhtd,bhsd->bhts', q, k) * scale
            attn = jnp.where(enc_mask[:, None, None, :], neg, attn)
            attn = jax.nn.softmax(attn, axis=-1)
            ca = jnp.einsum('bhts,bhsd->bhtd', attn, v).transpose(0, 2, 1, 3).reshape(B, T, C)
            x = x + ca @ out_w + out_b
            h = _layernorm(x, ln3_w, ln3_b)
            h = jax.nn.gelu(h @ mlp1_w + mlp1_b, approximate=False)
            x = x + h @ mlp2_w + mlp2_b
            return x
        return _decoder_block(x, enc, tgt_key_padding_mask, enc_padding_mask, ln1_w, ln1_b, qkv_w, qkv_b, proj_w, proj_b, ln2_w, ln2_b, q_w, q_b, k_w, k_b, v_w, v_b, out_w, out_b, ln3_w, ln3_b, mlp1_w, mlp1_b, mlp2_w, mlp2_b)

    def _L1_xattn_ref(x, xf, Wq, bq, Wk, bk, Wv, bv, Wo, bo, ln_g, ln_b, W1, b1, W2, b2):
        import jax, jax.numpy as jnp
        import numpy as np
        LATENT = 128
        TEXT = 96
        HEADS = 16
        HEAD_DIM = LATENT // HEADS
        SCALE = HEAD_DIM ** (-0.5)
        LN_EPS = 1e-05
        B, Tx, D = x.shape
        Txf = xf.shape[1]
        q = (x @ Wq + bq).reshape(B, Tx, HEADS, HEAD_DIM).transpose(0, 2, 1, 3)
        k = (xf @ Wk + bk).reshape(B, Txf, HEADS, HEAD_DIM).transpose(0, 2, 1, 3)
        v = (xf @ Wv + bv).reshape(B, Txf, HEADS, HEAD_DIM).transpose(0, 2, 1, 3)
        scores = jnp.einsum('bhqd,bhkd->bhqk', q * SCALE, k)
        probs = jax.nn.softmax(scores, axis=-1)
        attn = jnp.einsum('bhqk,bhkd->bhqd', probs, v)
        out = attn.transpose(0, 2, 1, 3).reshape(B, Tx, D)
        out = out @ Wo + bo
        mu = jnp.mean(out, axis=-1, keepdims=True)
        var = jnp.var(out, axis=-1, keepdims=True)
        h = (out - mu) * jax.lax.rsqrt(var + LN_EPS) * ln_g + ln_b
        h = jax.nn.gelu(h @ W1 + b1, approximate=False)
        ffn = h @ W2 + b2
        out = out + ffn
        return x + out

    def _L2_xattn_ref(x, cond_emb, ln1_g, ln1_b, ln2_g, ln2_b, ln3_g, ln3_b, sa_wq, sa_wk, sa_wv, sa_wo, sa_bo, ca_wq, ca_wk, ca_wv, ca_wo, ca_bo, ff_w1, ff_b1, ff_w2, ff_b2):
        import jax, jax.numpy as jnp
        import numpy as np
        D_MODEL = 128
        D_COND = 96
        N_HEADS = 16
        D_HEAD = 64
        D_ATTN = N_HEADS * D_HEAD
        D_FF = 4 * D_MODEL

        def _layernorm(x, g, b, eps=1e-05):
            mu = jnp.mean(x, axis=-1, keepdims=True)
            var = jnp.var(x, axis=-1, keepdims=True)
            return (x - mu) * jax.lax.rsqrt(var + eps) * g + b

        def _attention(xq, xkv, wq, wk, wv, wo, bo):
            B, S, _ = xq.shape
            T = xkv.shape[1]
            q = (xq @ wq).reshape(B, S, N_HEADS, D_HEAD)
            k = (xkv @ wk).reshape(B, T, N_HEADS, D_HEAD)
            v = (xkv @ wv).reshape(B, T, N_HEADS, D_HEAD)
            scale = D_HEAD ** (-0.5)
            attn = jnp.einsum('bihd,bjhd->bhij', q, k) * scale
            attn = jax.nn.softmax(attn, axis=-1)
            out = jnp.einsum('bhij,bjhd->bihd', attn, v).reshape(B, S, D_ATTN)
            return out @ wo + bo
        h = _layernorm(x, ln1_g, ln1_b)
        x = _attention(h, h, sa_wq, sa_wk, sa_wv, sa_wo, sa_bo) + x
        h = _layernorm(x, ln2_g, ln2_b)
        x = _attention(h, cond_emb, ca_wq, ca_wk, ca_wv, ca_wo, ca_bo) + x
        h = _layernorm(x, ln3_g, ln3_b)
        p = h @ ff_w1 + ff_b1
        a, gate = (p[..., :D_FF], p[..., D_FF:])
        h = a * jax.nn.gelu(gate, approximate=False) @ ff_w2 + ff_b2
        return h + x

    def _L3_xattn_ref(x, context, ln1_g, ln1_b, ln2_g, ln2_b, ln3_g, ln3_b, a1_wq, a1_wk, a1_wv, a1_wo, a1_bo, a2_wq, a2_wk, a2_wv, a2_wo, a2_bo, ff_w1, ff_b1, ff_w2, ff_b2):
        import jax, jax.numpy as jnp
        import numpy as np
        B, S, D = (4, 256, 128)
        CTX_LEN, CTX_DIM = (77, 96)
        H, DH = (16, 64)
        INNER = H * DH
        MULT = 4
        EPS = 1e-05

        def _layernorm(x, g, b):
            mu = jnp.mean(x, axis=-1, keepdims=True)
            var = jnp.var(x, axis=-1, keepdims=True)
            return (x - mu) * jax.lax.rsqrt(var + EPS) * g + b

        def _attn(xq, xkv, wq, wk, wv, wo, bo):
            b, sq, _ = xq.shape
            sk = xkv.shape[1]
            q = (xq @ wq).reshape(b, sq, H, DH)
            k = (xkv @ wk).reshape(b, sk, H, DH)
            v = (xkv @ wv).reshape(b, sk, H, DH)
            score = jnp.einsum('bqhd,bkhd->bhqk', q, k) * DH ** (-0.5)
            w = jax.nn.softmax(score, axis=-1)
            o = jnp.einsum('bhqk,bkhd->bqhd', w, v).reshape(b, sq, INNER)
            return o @ wo + bo

        def _block(x, context, ln1_g, ln1_b, ln2_g, ln2_b, ln3_g, ln3_b, a1_wq, a1_wk, a1_wv, a1_wo, a1_bo, a2_wq, a2_wk, a2_wv, a2_wo, a2_bo, ff_w1, ff_b1, ff_w2, ff_b2):
            x = _attn(_layernorm(x, ln1_g, ln1_b), _layernorm(x, ln1_g, ln1_b), a1_wq, a1_wk, a1_wv, a1_wo, a1_bo) + x
            x = _attn(_layernorm(x, ln2_g, ln2_b), context, a2_wq, a2_wk, a2_wv, a2_wo, a2_bo) + x
            h = _layernorm(x, ln3_g, ln3_b) @ ff_w1 + ff_b1
            u, gate = jnp.split(h, 2, axis=-1)
            x = u * jax.nn.gelu(gate, approximate=False) @ ff_w2 + ff_b2 + x
            return x
        return _block(x, context, ln1_g, ln1_b, ln2_g, ln2_b, ln3_g, ln3_b, a1_wq, a1_wk, a1_wv, a1_wo, a1_bo, a2_wq, a2_wk, a2_wv, a2_wo, a2_bo, ff_w1, ff_b1, ff_w2, ff_b2)
    x = _L0_xattn_ref(x, ctx_768, mask_BxS_bf0, mask_BxS2_bf0, L0_xattn_ln1_w, L0_xattn_ln1_b, L0_xattn_qkv_w, L0_xattn_qkv_b, L0_xattn_proj_w, L0_xattn_proj_b, L0_xattn_ln2_w, L0_xattn_ln2_b, L0_xattn_q_w, L0_xattn_q_b, L0_xattn_k_w, L0_xattn_k_b, L0_xattn_v_w, L0_xattn_v_b, L0_xattn_out_w, L0_xattn_out_b, L0_xattn_ln3_w, L0_xattn_ln3_b, L0_xattn_mlp1_w, L0_xattn_mlp1_b, L0_xattn_mlp2_w, L0_xattn_mlp2_b)
    x = _L1_xattn_ref(x, ctx_768, L1_xattn_Wq, L1_xattn_bq, L1_xattn_Wk, L1_xattn_bk, L1_xattn_Wv, L1_xattn_bv, L1_xattn_Wo, L1_xattn_bo, L1_xattn_ln_g, L1_xattn_ln_b, L1_xattn_W1, L1_xattn_b1, L1_xattn_W2, L1_xattn_b2)
    x = _L2_xattn_ref(x, ctx_768, L2_xattn_ln1_g, L2_xattn_ln1_b, L2_xattn_ln2_g, L2_xattn_ln2_b, L2_xattn_ln3_g, L2_xattn_ln3_b, L2_xattn_sa_wq, L2_xattn_sa_wk, L2_xattn_sa_wv, L2_xattn_sa_wo, L2_xattn_sa_bo, L2_xattn_ca_wq, L2_xattn_ca_wk, L2_xattn_ca_wv, L2_xattn_ca_wo, L2_xattn_ca_bo, L2_xattn_ff_w1, L2_xattn_ff_b1, L2_xattn_ff_w2, L2_xattn_ff_b2)
    x = _L3_xattn_ref(x, ctx_768, L3_xattn_ln1_g, L3_xattn_ln1_b, L3_xattn_ln2_g, L3_xattn_ln2_b, L3_xattn_ln3_g, L3_xattn_ln3_b, L3_xattn_a1_wq, L3_xattn_a1_wk, L3_xattn_a1_wv, L3_xattn_a1_wo, L3_xattn_a1_bo, L3_xattn_a2_wq, L3_xattn_a2_wk, L3_xattn_a2_wv, L3_xattn_a2_wo, L3_xattn_a2_bo, L3_xattn_ff_w1, L3_xattn_ff_b1, L3_xattn_ff_w2, L3_xattn_ff_b2)
    return x

_drawn_inputs = setup_inputs


def setup_inputs(seed=0):
    import zlib

    import numpy as np

    out = dict(_drawn_inputs(seed))
    spreads = {'L0_xattn_ln1_w': (1.0, 0.6),
     'L0_xattn_ln1_b': (0.0, 0.1),
     'L0_xattn_ln2_w': (1.0, 0.6),
     'L0_xattn_ln2_b': (0.0, 0.8),
     'L0_xattn_ln3_w': (1.0, 0.2),
     'L0_xattn_ln3_b': (0.0, 0.327),
     'L1_xattn_ln_g': (1.0, 0.2),
     'L1_xattn_ln_b': (0.0, 0.272),
     'L2_xattn_ln1_g': (1.0, 0.2),
     'L2_xattn_ln1_b': (0.0, 0.1),
     'L2_xattn_ln2_g': (1.0, 0.2),
     'L2_xattn_ln2_b': (0.0, 0.394),
     'L2_xattn_ln3_g': (1.0, 0.2),
     'L2_xattn_ln3_b': (0.0, 0.1),
     'L2_xattn_sa_bo': (0.0, 0.1),
     'L2_xattn_ca_bo': (0.0, 0.1),
     'L2_xattn_ff_b1': (0.0, 0.1),
     'L2_xattn_ff_b2': (0.0, 0.1),
     'L3_xattn_ln1_g': (1.0, 0.6),
     'L3_xattn_ln1_b': (0.0, 0.8),
     'L3_xattn_ln2_g': (1.0, 0.6),
     'L3_xattn_ln2_b': (0.0, 0.8),
     'L3_xattn_ln3_g': (1.0, 0.6),
     'L3_xattn_ln3_b': (0.0, 0.8),
     'L3_xattn_a1_bo': (0.0, 0.1),
     'L3_xattn_a2_bo': (0.0, 0.1),
     'L3_xattn_ff_b1': (0.0, 0.8),
     'L3_xattn_ff_b2': (0.0, 0.8)}
    factors = {'L0_xattn_q_w': 2.825,
     'L0_xattn_q_b': 8.0,
     'L0_xattn_k_w': 2.843,
     'L0_xattn_k_b': 64.0,
     'L0_xattn_mlp1_b': 2.762,
     'L1_xattn_bq': 8.0,
     'L1_xattn_bk': 64.0,
     'L1_xattn_b1': 2.69,
     'L3_xattn_a1_wq': 8.0,
     'L3_xattn_a1_wk': 8.0,
     'L3_xattn_a2_wq': 8.0,
     'L3_xattn_a2_wk': 8.0,
     'L3_xattn_ff_w1': 5.761,
     'L3_xattn_ff_w2': 5.63}
    for name, (base, spread) in spreads.items():
        noise = np.random.default_rng([zlib.crc32(name.encode()), seed]).standard_normal(out[name].shape)
        drawn = base * np.exp(spread * noise) if base else spread * noise
        out[name] = jnp.asarray(drawn.astype(out[name].dtype))
    for name, factor in factors.items():
        out[name] = (out[name] * factor).astype(out[name].dtype)
    return out
```

```python
from contextlib import ExitStack

import concourse.bass as bass
from concourse import mybir

F32 = mybir.dt.float32
F32R = mybir.dt.float32r
BF16 = mybir.dt.bfloat16
U8 = mybir.dt.uint8
ALU = mybir.AluOpType
ACT = mybir.ActivationFunctionType
AX = mybir.AxisListType

P = 128
B = 2
T = 512
D = 128
N = B * T
TILES = N // P
QT = T // P
S = 77
SP_ = 78
DC = 96
H = 16
HS = 8
HB = 64
F = 512
FT = F // P
QUADS = H // 4
PAIRS = H // 2
ROWS = 32
ROW_MAX = 24
ROW_MASK = 25
BIG = 1e30
EPS = 1e-5

LN_NAMES = ["l0n1", "l0n2", "l0n3", "l1n", "l2n1", "l2n2", "l2n3", "l3n1", "l3n2", "l3n3"]
COLS = {}
for _n in LN_NAMES:
    COLS[_n + "g"] = len(COLS)
    COLS[_n + "b"] = len(COLS)
_c = len(COLS)
for _n, _k in (("l0m", FT), ("l1m", FT), ("l2m", 2 * FT), ("l3m", 2 * FT),
               ("l0saq", QUADS), ("l0sak", QUADS), ("l0caq", QUADS), ("l0cak", QUADS),
               ("l1caq", QUADS), ("l1cak", QUADS), ("nselq", 1), ("nselk", 1)):
    COLS[_n] = _c
    _c += _k
NCOLS = _c
ROW_NAMES = ["l0sao", "l0cao", "l1cao", "l2sao", "l2cao", "l3sao", "l3cao",
             "l0b2", "l1b2", "l2b2", "l3b2", "l0sav", "l0cav", "l1cav"]
ROWV = {n: i for i, n in enumerate(ROW_NAMES)}
WTS = {}
_c = 0
LOADS = [("l0sa",), ("l0ca", "l0m"), ("l1ca", "l1m"), ("l2m",), ("l3m",)]
LOAD_AT = []
for _g in LOADS:
    LOAD_AT.append(_c)
    for _n in _g:
        if _n.endswith("a"):
            for _p, _k in (("q", QUADS * P), ("k", QUADS * P), ("v", D), ("o", D)):
                WTS[_n + _p] = _c
                _c += _k
        else:
            WTS[_n + "1"] = _c
            _c += F if _n in ("l0m", "l1m") else 2 * F
            WTS[_n + "2"] = _c
            _c += F
LOAD_AT.append(_c)
NWTS = _c


class Item:

    def __init__(self, c, n=None, per=0):
        a, m, self.i = n if n is not None else (0, 0, None)
        self.c, self.step = c + per * a, per * m
        assert self.step % 2 == 0

    def _value(self, c, step):
        return c if self.i is None else self.i * step + c

    @property
    def slot(self):
        return self.c % 2

    def full(self):
        return self._value(self.c + 1, self.step)

    def free(self):
        return self._value(self.c // 2 + 1, self.step // 2)

    def vacant(self):
        return self._value(self.c // 2, self.step // 2)

    def first(self):
        return self.i is None and self.c < 2


def count(c, n, per):
    a, m, i = n
    return c + per * a if i is None else i * (per * m) + (c + per * a)


class Small:

    def __init__(self, name, causal, ctx, masked, into, base):
        self.name, self.causal, self.ctx, self.masked, self.into = name, causal, ctx, masked, into
        self.kt = 1 if ctx else QT
        self.kw = S if ctx else P
        order = [("V", 0, 0)]
        ms = 4 if ctx else 4 * QT
        for n in range(QUADS):
            order += [("Q", n, 0), ("K", n, 0)] + [("M", n, k) for k in range(ms)] + [("T", n, 0)]
        order += [("A", 0, 0), ("O", 0, 0)]
        self.items = {k: Item(base["item"] + i) for i, k in enumerate(order)}
        self.unit0, self.o0, self.qk0, self.mrow0 = base["unit"], base["o"], base["qk"], base["mrow"]
        self.units = [(b, hp, kt) for b in range(B) for hp in range(2) for kt in range(self.kt)]
        self.sqk, self.sv, self.sw = self.qk0, None, None
        base["item"] += len(order)
        base["unit"] += QUADS * len(self.units)
        base["o"] += QUADS * 4
        base["qk"] += QUADS * 2
        base["mrow"] += QUADS

    def m_list(self):
        if self.ctx:
            return [(b, hp, None) for b in range(B) for hp in range(2)]
        return [(b, hp, qt) for b in range(B) for hp in range(2) for qt in range(QT)]


class Big:

    def __init__(self, name, ctx, base):
        self.name, self.ctx = name, ctx
        self.kt = 1 if ctx else QT
        self.kw = S if ctx else P
        self.kn = SP_ if ctx else T
        self.g = B * self.kt
        self.ms = 2 if ctx else B * QT
        self.np = 3 + self.ms + 1
        self.item0, self.unit0, self.o0 = base["item"], base["unit"], base["o"]
        self.hi0, self.wqkv0, self.wo0 = base["hi"], base["wqkv"], base["wo"]
        base["item"] += 2 * self.np + (self.np + 2) * (PAIRS - 2) + 4
        base["unit"] += PAIRS * self.g
        base["o"] += PAIRS * 2
        base["hi"] += PAIRS * 2
        base["wqkv"] += PAIRS
        base["wo"] += PAIRS

    def prep(self, n, k):
        if n == (0, 0, None):
            return Item(self.item0 + k)
        return Item(self.item0 - 2 + k, n, self.np + 2)

    def fin(self, n, k):
        if n == (PAIRS - 1, 0, None):
            return Item(self.item0 + 2 * self.np + (self.np + 2) * (PAIRS - 2) + 2 + k)
        return Item(self.item0 + 2 * self.np + k, n, self.np + 2)


class Norm:

    def __init__(self, name, src, base):
        self.name, self.src = name, src
        self.item0 = base["item"]
        base["item"] += 2


class Mlp:
    def __init__(self, name, gated, base):
        self.name, self.gated = name, gated
        self.item0 = base["item"]
        self.per = 2 if gated else 1
        base["item"] += FT * self.per + 1

    def gate(self, f):
        return Item(self.item0 + f * self.per)

    def up(self, f):
        return Item(self.item0 + f * self.per + 1)

    def out(self):
        return Item(self.item0 + FT * self.per)


def plan():
    base = dict(item=0, unit=0, o=0, qk=0, mrow=0, hi=0, wqkv=0, wo=0)
    return [
        Norm("l0n1", "x", base), Small("l0sa", True, False, True, "x", base),
        Norm("l0n2", "x", base), Small("l0ca", False, True, True, "x", base),
        Norm("l0n3", "x", base), Mlp("l0m", False, base),
        Norm(None, "x", base), Small("l1ca", False, True, False, "att", base),
        Norm("l1n", "att", base), Mlp("l1m", False, base),
        Norm("l2n1", "x", base), Big("l2sa", False, base),
        Norm("l2n2", "x", base), Big("l2ca", True, base),
        Norm("l2n3", "x", base), Mlp("l2m", True, base),
        Norm("l3n1", "x", base), Big("l3sa", False, base),
        Norm("l3n2", "x", base), Big("l3ca", True, base),
        Norm("l3n3", "x", base), Mlp("l3m", True, base),
    ]


def pair_steps(eng, body):
    body((0, 0, None), 0, True, False)
    with eng.Fori(0, (PAIRS - 2) // 2) as i:
        body((1, 2, i), 1, False, False)
        body((2, 2, i), 0, False, False)
    body((PAIRS - 1, 0, None), (PAIRS - 1) % 2, False, True)


def shift(n, by):
    return (n[0] + by, n[1], n[2])


def program(nc, x_in, ctx_in, tmask_row, tmask_col, cmask_row, cmask_col, cols_in, rows_in, wts_in, big_in, out):
    sections = plan()
    with ExitStack() as ctx:
        def sb(name, shape, dt=F32):
            return ctx.enter_context(nc.sbuf_tensor(name, shape, dt))

        def sem(name):
            return ctx.enter_context(nc.semaphore(name))

        x_res = sb("x_res", [P, TILES, D])
        att = sb("att", [P, TILES, D])
        z = sb("z", [P, TILES, D])
        hT = sb("hT", [P, N])
        ctxT = sb("ctxT", [DC, B * SP_])
        cols = sb("cols", [P, NCOLS])
        rows = sb("rows", [P, len(ROW_NAMES), D])
        wts = sb("wts", [P, NWTS])
        ident = sb("ident", [P, P])
        ident_bf = sb("ident_bf", [P, P], BF16)
        after_q = sb("after_q", [P, P], BF16)
        after_k = sb("after_k", [P, P], BF16)
        mask_sel = sb("mask_sel", [1, P], BF16)
        tm8 = sb("tm8", [1, N], U8)
        tc8 = sb("tc8", [P, TILES], U8)
        cm8 = sb("cm8", [1, B * SP_], U8)
        cc8 = sb("cc8", [P, B], U8)
        tmask = sb("tmask", [1, N], BF16)
        cmask = sb("cmask", [1, B * SP_], BF16)
        tkeep = sb("tkeep", [P, TILES])
        ckeep = sb("ckeep", [P, B])
        stats = sb("stats", [P, TILES, 6])
        mv = sb("mv", [P, TILES, 2])
        std = sb("std", [P, TILES])
        rstd = sb("rstd", [P, TILES])
        q1 = sb("q1", [P, 2, 2, N], F32R)
        q2 = sb("q2", [P, 2, 2, N], F32R)
        k1 = sb("k1", [P, 2, 2, N], F32R)
        k2 = sb("k2", [P, 2, 2, N], F32R)
        vb = sb("vb", [P, 2, TILES, 2, HB + 1])
        bigw = sb("bigw", [P, 4, P])
        full = sb("full", [P, 2, N])
        qs = sb("qs", [P, 2, N], F32R)
        ks = sb("ks", [P, 2, N], F32R)
        vs = sb("vs", [P, TILES, H, HS + 1])
        mT = sb("mT", [4, N], F32R)
        mneg = sb("mneg", [P, TILES, HB + 2])
        prob = sb("prob", [P, 2, 2, T])
        recip = sb("recip", [P, 2, QT, 2])
        on = sb("on", [P, TILES, D])
        onT = sb("onT", [P, N])
        gbuf = full
        actT = sb("actT", [P, FT, N])
        half = actT

        st = ctx.enter_context(nc.psum_tensor("st", [P, 2, 512], F32))
        oacc = ctx.enter_context(nc.psum_tensor("oacc", [P, 2, 512], F32))
        work = [ctx.enter_context(nc.psum_tensor(f"work{i}", [P, 2, 512], F32)) for i in range(2)]

        x_loaded = sem("x_loaded")
        consts_loaded = sem("consts_loaded")
        wts_loaded = [sem(f"wts_loaded{i}") for i in range(len(LOADS))]
        wqkv_loaded = sem("wqkv_loaded")
        wo_loaded = sem("wo_loaded")
        made = sem("made")
        masks_made = sem("masks_made")
        work_full = sem("work_full")
        work_free = [sem("work_free0"), sem("work_free1")]
        st_full = sem("st_full")
        exp_done = sem("exp_done")
        o_full = sem("o_full")
        o_normed = sem("o_normed")
        hi_done = sem("hi_done")
        qk_done = sem("qk_done")
        v_masked = sem("v_masked")
        mrow_done = sem("mrow_done")
        var_done = sem("var_done")
        std_done = sem("std_done")
        z_done = sem("z_done")
        vec = sem("vec")
        stored = sem("stored")

        block = ctx.enter_context(nc.Block())

        @block.sync
        def _(sp):
            sp.dma_start(x_res[:], x_in.rearrange("(t p) d -> p t d", p=P)).then_inc(x_loaded, 16)
            for dst, src in ((cols[:], cols_in), (rows[:], rows_in), (ctxT[:], ctx_in), (tm8[:], tmask_row),
                             (tc8[:], tmask_col), (cm8[:], cmask_row), (cc8[0:S, :], cmask_col)):
                sp.dma_start(dst, src).then_inc(consts_loaded, 16)
            for i in range(len(LOADS)):
                sp.dma_start(wts[:, LOAD_AT[i]:LOAD_AT[i + 1]],
                             wts_in[:, LOAD_AT[i]:LOAD_AT[i + 1]]).then_inc(wts_loaded[i], 16)

            def move_max_rows(s):
                for n in range(QUADS):
                    it = s.items["T", n, 0]
                    sp.wait_ge(work_free[it.slot], it.free())
                    sp.dma_start(qs[ROW_MAX:P:ROWS, n % 2, :].bitcast(F32), mT[:, :].bitcast(F32)).then_inc(mrow_done, 16)

            def load_pairs(s):
                wq, wk, wv, wo = big_in[s.name]
                kr = DC if s.ctx else D

                def load(n, first, v_before, o_before):
                    at = n[0] * P if n[2] is None else n[2] * (n[1] * P) + n[0] * P
                    if not first:
                        sp.wait_ge(work_full, v_before.full())
                    sp.dma_start(bigw[:, 0, :], wq[:, bass.ds(at, P)]).then_inc(wqkv_loaded, 16)
                    sp.dma_start(bigw[0:kr, 1, :], wk[:, bass.ds(at, P)]).then_inc(wqkv_loaded, 16)
                    sp.dma_start(bigw[0:kr, 2, :], wv[:, bass.ds(at, P)]).then_inc(wqkv_loaded, 16)
                    if o_before is not None:
                        sp.wait_ge(work_full, o_before.full())
                    sp.dma_start(bigw[:, 3, :], wo[bass.ds(at, P), :]).then_inc(wo_loaded, 16)

                load((0, 0, None), s.item0 == 0, Item(s.item0 - 1), None)
                load((1, 0, None), False, s.prep((0, 0, None), 2), s.fin((0, 0, None), 1))
                with sp.Fori(0, (PAIRS - 2) // 2) as i:
                    load((2, 2, i), False, s.prep((1, 2, i), 2), s.fin((1, 2, i), 1))
                    load((3, 2, i), False, s.prep((2, 2, i), 2), s.fin((2, 2, i), 1))

            for s in sections:
                if isinstance(s, Small):
                    move_max_rows(s)
                if isinstance(s, Big):
                    load_pairs(s)
            last = sections[-1].out()
            sp.wait_ge(work_free[last.slot], last.free())
            sp.dma_start(out.rearrange("(t p) d -> p t d", p=P), x_res[:]).then_inc(stored, 16)
            sp.wait_ge(stored, 16)

        @block.gpsimd
        def _(pool):
            pool.memset(ident[:], 0.0).then_inc(made, 1)
            pool.memset(ident_bf[:], 0.0).then_inc(made, 1)
            pool.memset(after_q[:], 0.0).then_inc(made, 1)
            pool.memset(after_k[:], 0.0).then_inc(made, 1)
            pool.memset(mask_sel[:], 0.0).then_inc(made, 1)
            pool.wait_ge(made, 5)
            for m in (ident, ident_bf):
                pool.affine_select(out=m[:], in_=m[:], compare_op=ALU.not_equal, fill=1.0, base=0,
                                   pattern=[[-1, P]], channel_multiplier=1).then_inc(made, 1)
            pool.affine_select(out=after_q[:], in_=after_q[:], compare_op=ALU.is_ge, fill=-BIG, base=0,
                               pattern=[[-1, P]], channel_multiplier=1).then_inc(made, 1)
            pool.affine_select(out=after_k[:], in_=after_k[:], compare_op=ALU.is_ge, fill=-BIG, base=0,
                               pattern=[[1, P]], channel_multiplier=-1).then_inc(made, 1)
            for j in range(4):
                pool.memset(mask_sel[0:1, ROWS * j + ROW_MASK:ROWS * j + ROW_MASK + 1], 1.0).then_inc(made, 1)
            pool.memset(q2[:].bitcast(F32), 0.0).then_inc(made, 1)
            pool.memset(k2[:].bitcast(F32), 0.0).then_inc(made, 1)
            pool.memset(mneg[:], 0.0).then_inc(made, 1)
            pool.memset(vb[:], 1.0).then_inc(made, 1)
            pool.wait_ge(made, 17)
            pool.memset(k2[HB:HB + 1, :, 0, :].bitcast(F32), 1.0).then_inc(made, 1)
            pool.memset(k2[0:1, :, 1, :].bitcast(F32), 1.0).then_inc(made, 1)

        @block.tensor
        def _(pe):
            def open_item(it):
                if not it.first():
                    pe.wait_ge(work_free[it.slot], it.vacant())
                return work[it.slot]

            def taken(it):
                pe.wait_ge(work_free[it.slot], it.free())

            def norm(s):
                for k in range(2):
                    if s.name:
                        pe.wait_ge(z_done, z_count[s.name] + k + 1)
                        src = z
                    else:
                        if k == 0:
                            taken(x_item[0])
                        src = x_res
                    it = Item(s.item0 + k)
                    w = open_item(it)
                    for t in range(QT):
                        mm = pe.transpose(w[:, 0, t * P:(t + 1) * P], src[:, k * QT + t, :], ident[:])
                    mm.then_inc(work_full, 1)

            def both_halves(w, lhsT, rhs, then=None):
                for b in range(B):
                    mm = pe.matmul(w[:, b, :], lhsT, rhs[:, b * T:(b + 1) * T], start=True, stop=then is None)
                    if then is not None:
                        mm = then(b)
                return mm

            def transpose_out(it):
                w = open_item(it)
                for t in range(TILES):
                    mm = pe.transpose(w[:, t // QT, (t % QT) * P:(t % QT + 1) * P], on[:, t, :], ident[:])
                mm.then_inc(work_full, 1)

            def project_out(it, before, wo):
                w = open_item(it)
                taken(before)
                for t in range(TILES):
                    mm = pe.matmul(w[:, t // QT, (t % QT) * P:(t % QT + 1) * P], onT[:, t * P:(t + 1) * P],
                                   wo, start=True, stop=True)
                mm.then_inc(work_full, 1)

            def values(it, wv, ctx_side):
                w = open_item(it)
                if ctx_side:
                    for b in range(B):
                        mm = pe.matmul(w[0:S, b, 0:D], ctxT[:, b * SP_:b * SP_ + S], wv, start=True, stop=True)
                else:
                    for t in range(TILES):
                        mm = pe.matmul(w[:, t // QT, (t % QT) * P:(t % QT + 1) * P], hT[:, t * P:(t + 1) * P],
                                       wv, start=True, stop=True)
                mm.then_inc(work_full, 1)

            def small(s):
                kr = DC if s.ctx else D
                wv = wts[0:kr, WTS[s.name + "v"]:WTS[s.name + "v"] + D]
                wo = wts[:, WTS[s.name + "o"]:WTS[s.name + "o"] + D]

                def prepare(n):
                    wq = wts[:, WTS[s.name + "q"] + n * P:WTS[s.name + "q"] + (n + 1) * P]
                    wk = wts[0:kr, WTS[s.name + "k"] + n * P:WTS[s.name + "k"] + (n + 1) * P]
                    w = open_item(s.items["Q", n, 0])
                    both_halves(w, wq, hT).then_inc(work_full, 1)
                    yield
                    w = open_item(s.items["K", n, 0])
                    if s.ctx:
                        mm = pe.matmul(w[:, 0, 0:B * SP_], wk, ctxT[:], start=True, stop=not s.masked)
                        if s.masked:
                            mm = pe.matmul(w[:, 0, 0:B * SP_], mask_sel[:], cmask[:], start=False, stop=True)
                    else:
                        mm = both_halves(w, wk, hT, lambda b: pe.matmul(
                            w[:, b, :], mask_sel[:], tmask[:, b * T:(b + 1) * T], start=False, stop=True))
                    mm.then_inc(work_full, 1)
                    yield
                    pe.wait_ge(qk_done, s.qk0 + 2 * n + 2)
                    buf = n % 2
                    for k, (b, hp, qt) in enumerate(s.m_list()):
                        w = open_item(s.items["M", n, k])
                        for hh in range(2):
                            r = ROWS * (2 * hp + hh)
                            if s.ctx:
                                for t in range(QT):
                                    mm = pe.matmul(w[:, hh, t * SP_:(t + 1) * SP_],
                                                   qs[r:r + ROWS, buf, b * T + t * P:b * T + (t + 1) * P],
                                                   ks[r:r + ROWS, buf, b * SP_:(b + 1) * SP_], start=True, stop=True,
                                                   tile_position=(r, 0))
                            else:
                                keys = (qt + 1) * P
                                pe.matmul(w[:, hh, 0:keys], qs[r:r + ROWS, buf, b * T + qt * P:b * T + (qt + 1) * P],
                                          ks[r:r + ROWS, buf, b * T:b * T + keys], start=True, stop=False,
                                          skip_group_check=True, tile_position=(r, 0))
                                mm = pe.matmul(w[:, hh, qt * P:keys], ident_bf[:], after_q[:], start=False, stop=True,
                                               skip_group_check=True)
                        mm.then_inc(work_full, 1)
                        yield
                    it = s.items["M", n, len(s.m_list()) - 1]
                    taken(it)
                    before = s.items["M", n, len(s.m_list()) - 2]
                    taken(before)
                    w = open_item(s.items["T", n, 0])
                    for t in range(TILES):
                        mm = pe.transpose(w[0:4, t // QT, (t % QT) * P:(t % QT + 1) * P], mneg[:, t, 0:4], ident[:])
                    mm.then_inc(work_full, 1)
                    yield

                values_it = s.items["V", 0, 0]
                values(values_it, wv, s.ctx)
                for _ in prepare(0):
                    pass
                taken(values_it)
                if s.masked:
                    pe.wait_ge(v_masked, v_count[s.name])

                def scores(n, u):
                    b, hp, kt = s.units[u]
                    buf, g = n % 2, s.unit0 + n * len(s.units) + u
                    if u == 0:
                        pe.wait_ge(mrow_done, 16 * (s.mrow0 + n + 1))
                    if g:
                        pe.wait_ge(exp_done, g)
                    q0 = kt * P if s.causal else 0
                    kc = (b * T + kt * P) if not s.ctx else b * SP_
                    for hh in range(2):
                        r = ROWS * (2 * hp + hh)
                        mm = pe.matmul(st[0:s.kw, hh, q0:T], ks[r:r + ROWS, buf, kc:kc + s.kw],
                                       qs[r:r + ROWS, buf, b * T + q0:(b + 1) * T], start=True, stop=not s.causal,
                                       skip_group_check=True, tile_position=(r, 0))
                        if s.causal:
                            mm = pe.matmul(st[:, hh, q0:q0 + P], ident_bf[:], after_k[:], start=False, stop=True,
                                           skip_group_check=True)
                    mm.then_inc(st_full, 1)

                def weigh(n, u):
                    b, hp, kt = s.units[u]
                    g = s.unit0 + n * len(s.units) + u
                    o = s.o0 + 4 * n + 2 * b + hp
                    pe.wait_ge(exp_done, g + 1)
                    if kt == 0 and o:
                        pe.wait_ge(o_normed, max(o - 1, s.o0))
                    for t in range(kt if s.causal else 0, QT):
                        for hh in range(2):
                            c = (2 * t + hh) * (HS + 1)
                            mm = pe.matmul(oacc[:, hp, c:c + HS + 1], prob[0:s.kw, g % 2, hh, t * P:(t + 1) * P],
                                           vs[0:s.kw, (b * QT + kt) if not s.ctx else b, 4 * n + 2 * hp + hh, :],
                                           start=(kt == 0 and t == 0 and hh == 0),
                                           stop=(kt == (t if s.causal else s.kt - 1)), skip_group_check=True)
                    if kt == s.kt - 1:
                        mm.then_inc(o_full, 1)

                for n in range(QUADS):
                    ahead = prepare(n + 1) if n + 1 < QUADS else iter(())
                    per = 2
                    for u in range(len(s.units)):
                        scores(n, u)
                        if u:
                            weigh(n, u - 1)
                        for _ in range(per):
                            next(ahead, None)
                    weigh(n, len(s.units) - 1)
                    for _ in ahead:
                        pass
                o_all = s.o0 + 4 * QUADS
                pe.wait_ge(o_normed, o_all)
                transpose_out(s.items["A", 0, 0])
                project_out(s.items["O", 0, 0], s.items["A", 0, 0], wo)

            def big(s):
                kr = DC if s.ctx else D
                wq, wk, wv, wo = bigw[:, 0, :], bigw[0:kr, 1, :], bigw[0:kr, 2, :], bigw[:, 3, :]

                def prepare(n, buf, k):
                    it = s.prep(n, k)
                    if k == 0:
                        pe.wait_ge(wqkv_loaded, count(48 * (s.wqkv0 + 1), n, 48))
                        w = open_item(it)
                        both_halves(w, wq, hT).then_inc(work_full, 1)
                    elif k == 1:
                        w = open_item(it)
                        if s.ctx:
                            mm = pe.matmul(w[:, 0, 0:B * SP_], wk, ctxT[:], start=True, stop=True)
                        else:
                            mm = both_halves(w, wk, hT)
                        mm.then_inc(work_full, 1)
                    elif k == 2:
                        values(it, wv, s.ctx)
                    elif k < 3 + s.ms:
                        w = open_item(it)
                        if k == 3:
                            taken(s.prep(n, 0))
                            taken(s.prep(n, 1))
                        if s.ctx:
                            b = k - 3
                            for h in range(2):
                                for t in range(QT):
                                    q0 = b * T + t * P
                                    mm = pe.matmul(w[:, h, t * SP_:(t + 1) * SP_], q1[:, buf, h, q0:q0 + P],
                                                   k1[:, buf, h, b * SP_:(b + 1) * SP_], start=True, stop=True)
                        else:
                            b, t = divmod(k - 3, QT)
                            q0 = b * T + t * P
                            for h in range(2):
                                mm = pe.matmul(w[:, h, :], q1[:, buf, h, q0:q0 + P],
                                               k1[:, buf, h, b * T:(b + 1) * T], start=True, stop=True)
                        mm.then_inc(work_full, 1)
                    else:
                        taken(s.prep(n, 2 + s.ms))
                        taken(s.prep(n, 1 + s.ms))
                        w = open_item(it)
                        for t in range(TILES):
                            mm = pe.transpose(w[0:HB + 1, t // QT, (t % QT) * P:(t % QT + 1) * P], mneg[:, t, 0:HB + 1], ident[:])
                        mm.then_inc(work_full, 1)

                def scores(n, buf, g):
                    b, kt = divmod(g, s.kt)
                    if g == 0:
                        taken(s.prep(n, s.np - 1))
                    pe.wait_ge(exp_done, count(s.unit0 + g, n, s.g))
                    kc = (b * T + kt * P) if not s.ctx else b * SP_
                    for h in range(2):
                        pe.matmul(st[0:s.kw, h, :], k1[:, buf, h, kc:kc + s.kw], q1[:, buf, h, b * T:(b + 1) * T],
                                  start=True, stop=False)
                        mm = pe.matmul(st[0:s.kw, h, :], k2[:, buf, h, kc:kc + s.kw], q2[:, buf, h, b * T:(b + 1) * T],
                                       start=False, stop=True)
                    mm.then_inc(st_full, 1)

                def weigh(n, buf, g):
                    b, kt = divmod(g, s.kt)
                    pe.wait_ge(exp_done, count(s.unit0 + g + 1, n, s.g))
                    if g == 0:
                        taken(s.prep(n, 2))
                    if kt == 0:
                        pe.wait_ge(o_normed, count(s.o0 + b, n, 2))
                    slot = (s.unit0 + g) % 2
                    for h in range(2):
                        for t in range(QT):
                            mm = pe.matmul(oacc[:, h, t * (HB + 1):(t + 1) * (HB + 1)],
                                           prob[0:s.kw, slot, h, t * P:(t + 1) * P],
                                           vb[0:s.kw, buf, (b * QT + kt) if not s.ctx else b, h, :],
                                           start=(kt == 0 and t == 0), stop=(kt == s.kt - 1), skip_group_check=True)
                    if kt == s.kt - 1:
                        mm.then_inc(o_full, 1)

                def finish(n, k):
                    if k == 0:
                        pe.wait_ge(o_normed, count(s.o0 + 2, n, 2))
                        transpose_out(s.fin(n, 0))
                    else:
                        pe.wait_ge(wo_loaded, count(16 * (s.wo0 + 1), n, 16))
                        project_out(s.fin(n, 1), s.fin(n, 0), wo)

                ms = list(range(3, 3 + s.ms))
                if s.ctx:
                    with_unit = [[0, 1], [2] + ms]
                    tail = [s.np - 1]
                    finish_with = {0: 0, 1: 1}
                else:
                    with_unit = [[], [0], [1], [2], ms[0:2], ms[2:4], ms[4:6], ms[6:8]]
                    tail = [s.np - 1]
                    finish_with = {0: 0, 1: 1}

                def body(n, buf, first, last):
                    nxt = shift(n, 1)
                    for g in range(s.g):
                        scores(n, buf, g)
                        if s.ctx:
                            if g == 0 and not first:
                                finish(shift(n, -1), 0)
                                finish(shift(n, -1), 1)
                        elif g in finish_with and not first:
                            finish(shift(n, -1), finish_with[g])
                        if g:
                            weigh(n, buf, g - 1)
                        if not last:
                            for k in with_unit[g]:
                                prepare(nxt, 1 - buf, k)
                    weigh(n, buf, s.g - 1)
                    if not last:
                        for k in tail:
                            prepare(nxt, 1 - buf, k)

                for k in range(s.np):
                    prepare((0, 0, None), 0, k)
                pair_steps(pe, body)
                finish((PAIRS - 1, 0, None), 0)
                finish((PAIRS - 1, 0, None), 1)

            def mlp(s):
                w1, w2 = WTS[s.name + "1"], WTS[s.name + "2"]
                for f in range(FT):
                    if s.gated:
                        w = open_item(s.gate(f))
                        both_halves(w, wts[:, w1 + F + f * P:w1 + F + (f + 1) * P], hT).then_inc(work_full, 1)
                        w = open_item(s.up(f))
                        both_halves(w, wts[:, w1 + f * P:w1 + (f + 1) * P], hT).then_inc(work_full, 1)
                    else:
                        w = open_item(s.gate(f))
                        both_halves(w, wts[:, w1 + f * P:w1 + (f + 1) * P], hT).then_inc(work_full, 1)
                w = open_item(s.out())
                for f in range(FT):
                    taken(s.up(f) if s.gated else s.gate(f))
                for t in range(TILES):
                    for f in range(FT):
                        mm = pe.matmul(w[:, t // QT, (t % QT) * P:(t % QT + 1) * P], actT[:, f, t * P:(t + 1) * P],
                                       wts[:, w2 + f * P:w2 + (f + 1) * P], start=(f == 0), stop=(f == FT - 1))
                mm.then_inc(work_full, 1)

            pe.wait_ge(made, 19)
            pe.wait_ge(masks_made, 4)
            pe.wait_ge(consts_loaded, 16 * 7)
            z_count, v_count = counts(sections)
            x_item = [None]
            for s in sections:
                for i, g in enumerate(LOADS):
                    if s.name in g:
                        pe.wait_ge(wts_loaded[i], 16)
                if isinstance(s, Norm):
                    norm(s)
                    taken(Item(s.item0))
                    taken(Item(s.item0 + 1))
                if isinstance(s, Small):
                    small(s)
                if isinstance(s, Big):
                    big(s)
                if isinstance(s, Mlp):
                    mlp(s)
                    x_item[0] = s.out()

        @block.scalar
        def _(act):
            def filled(it):
                act.wait_ge(work_full, it.full())
                return work[it.slot]

            def norm(s):
                if s.name:
                    act.wait_ge(var_done, norm_no[s.name] + 1)
                    act.activation(std[:], mv[:, :, 1], ACT.Sqrt, bias=EPS).then_inc(std_done, 1)
                for k in range(2):
                    it = Item(s.item0 + k)
                    w = filled(it)
                    dst = hT[:, k * T:(k + 1) * T]
                    if s.name:
                        g, b = COLS[s.name + "g"], COLS[s.name + "b"]
                        ins = act.activation(dst, w[:, 0, :], ACT.Identity, bias=cols[:, b:b + 1], scale=cols[:, g:g + 1])
                    else:
                        ins = act.activation(dst, w[:, 0, :], ACT.Copy)
                    ins.then_inc(work_free[it.slot], 1)

            def take_out(it):
                w = filled(it)
                act.activation(onT[:], w[:, :, :], ACT.Copy).then_inc(work_free[it.slot], 1)

            def small(s):
                def prepare(n):
                    for k, what in enumerate("QK"):
                        j = s.qk0 + 2 * n + k
                        it = s.items[what, n, 0]
                        w = filled(it)
                        if j >= 2:
                            act.wait_ge(qk_done, j - 1)
                        c = COLS[s.name + what.lower()] + n
                        if k == 1 and s.ctx:
                            dst, src = full[:, j % 2, 0:B * SP_], w[:, 0, 0:B * SP_]
                        else:
                            dst, src = full[:, j % 2, :], w[:, :, :]
                        act.activation(dst, src, ACT.Identity, bias=cols[:, c:c + 1])
                        rounded = half[:, j % 2, 0:dst.shape[-1]].bitcast(F32R)
                        act.activation(rounded, src, ACT.Identity, bias=cols[:, c:c + 1]).then_inc(work_free[it.slot], 1)
                        yield
                    it = s.items["T", n, 0]
                    w = filled(it)
                    if n or s.mrow0:
                        act.wait_ge(mrow_done, 16 * (s.mrow0 + n))
                    act.activation(mT[:, :], w[0:4, :, :], ACT.Copy).then_inc(work_free[it.slot], 1)
                    yield

                for _ in prepare(0):
                    pass
                for n in range(QUADS):
                    ahead = prepare(n + 1) if n + 1 < QUADS else iter(())
                    for u, (b, hp, kt) in enumerate(s.units):
                        g = s.unit0 + n * len(s.units) + u
                        q0 = kt * P if s.causal else 0
                        act.wait_ge(st_full, g + 1)
                        act.activation(prob[0:s.kw, g % 2, :, q0:T], st[0:s.kw, :, q0:T], ACT.Exp,
                                       scale=HS ** -0.5).then_inc(exp_done, 1)
                        if u < 2 and not s.ctx or u == 0:
                            next(ahead, None)
                            if s.ctx:
                                next(ahead, None)
                    for _ in ahead:
                        pass
                take_out(s.items["A", 0, 0])

            def big(s):
                def prepare(n, buf, k):
                    it = s.prep(n, k)
                    w = filled(it)
                    if k < 2:
                        dst = q2 if k == 0 else k1
                        if k == 1 and s.ctx:
                            act.activation(dst[0:HB, buf, 0, 0:B * SP_], w[0:HB, 0, 0:B * SP_], ACT.Copy).then_inc(hi_done, 1)
                            act.activation(dst[HB:P, buf, 1, 0:B * SP_], w[HB:P, 0, 0:B * SP_], ACT.Copy).then_inc(hi_done, 1)
                        else:
                            act.activation(dst[0:HB, buf, 0, :], w[0:HB, :, :], ACT.Copy).then_inc(hi_done, 1)
                            act.activation(dst[HB:P, buf, 1, :], w[HB:P, :, :], ACT.Copy).then_inc(hi_done, 1)
                    elif k == 2:
                        if s.ctx:
                            act.activation(vb[0:S, buf, 0:B, :, 0:HB], w[0:S, :, 0:D].rearrange("p b (h d) -> p b h d", h=2),
                                           ACT.Copy).then_inc(work_free[it.slot], 1)
                        else:
                            act.activation(vb[:, buf, :, :, 0:HB], w[:, :, :].rearrange("p b (t h d) -> p (b t) h d", h=2, d=HB),
                                           ACT.Copy).then_inc(work_free[it.slot], 1)
                    else:
                        act.activation(q2[HB:HB + 1, buf, 0, :], w[0:1, :, :], ACT.Copy)
                        act.activation(q2[0:1, buf, 1, :], w[HB:HB + 1, :, :], ACT.Copy).then_inc(work_free[it.slot], 1)

                for k in (0, 1, 2, s.np - 1):
                    prepare((0, 0, None), 0, k)

                def body(n, buf, first, last):
                    nxt = shift(n, 1)
                    after = [[0], [1, 2]] if s.ctx else [[], [0], [1], [2], [], [], [], []]
                    for g in range(s.g):
                        act.wait_ge(st_full, count(s.unit0 + g + 1, n, s.g))
                        act.activation(prob[0:s.kw, (s.unit0 + g) % 2, :, :], st[0:s.kw, :, :], ACT.Exp,
                                       scale=HB ** -0.5).then_inc(exp_done, 1)
                        if g == 0 and not first:
                            take_out(s.fin(shift(n, -1), 0))
                        if not last:
                            for k in after[g]:
                                prepare(nxt, 1 - buf, k)
                    if not last:
                        prepare(nxt, 1 - buf, s.np - 1)
                pair_steps(act, body)
                take_out(s.fin((PAIRS - 1, 0, None), 0))

            def mlp(s):
                c = COLS[s.name]
                for f in range(FT):
                    it = s.gate(f)
                    w = filled(it)
                    if s.gated:
                        if f >= 2:
                            before = s.up(f - 2)
                            act.wait_ge(work_free[before.slot], before.free())
                        dst, b = gbuf[:, f % 2, :], c + FT + f
                    else:
                        dst, b = actT[:, f, :], c + f
                    act.activation(dst, w[:, :, :], ACT.Gelu, bias=cols[:, b:b + 1]).then_inc(work_free[it.slot], 1)

            norm_no = {s.name: i for i, s in enumerate([s for s in sections if isinstance(s, Norm) and s.name])}
            act.wait_ge(consts_loaded, 16 * 7)
            act.wait_ge(made, 19)
            for s in sections:
                if isinstance(s, Norm):
                    norm(s)
                if isinstance(s, Small):
                    small(s)
                if isinstance(s, Big):
                    big(s)
                if isinstance(s, Mlp):
                    mlp(s)

        @block.vector
        def _(dve):
            steps = [0]

            def link(ins):
                steps[0] += 1
                ins.then_inc(vec, 1)
                dve.wait_ge(vec, steps[0])

            def filled(it):
                dve.wait_ge(work_full, it.full())
                return work[it.slot]

            def row(name, k=TILES):
                return rows[:, ROWV[name], :].unsqueeze(1).to_broadcast([P, k, D])

            def tiles(ap):
                return ap.rearrange("p b (t d) -> p (b t) d", d=D)

            def norm(s, add):
                if s.name:
                    src = x_res if s.src == "x" else att
                    for t in range(TILES):
                        ins = dve.bn_stats(stats[:, t, :], src[:, t, :])
                    link(ins)
                    for t in range(TILES):
                        ins = dve.bn_aggr(mv[:, t, :], stats[:, t, :])
                    ins.then_inc(var_done, 1)
                    dve.wait_ge(std_done, norm_no[s.name] + 1)
                    link(dve.reciprocal(rstd[:], std[:]))
                    for t in range(TILES):
                        ins = dve.tensor_scalar(z[:, t, :], src[:, t, :], mv[:, t, 0:1], rstd[:, t:t + 1],
                                                ALU.subtract, ALU.mult)
                        if t % QT == QT - 1:
                            ins.then_inc(z_done, 1)
                    dve.wait_ge(z_done, z_count[s.name] + 2)
                for what in add:
                    link(dve.tensor_tensor(x_res[:], x_res[:], att[:] if what == "att" else row(what), ALU.add))

            def add_out(it, into, name=None):
                w = filled(it)
                if into == "x":
                    ins = dve.tensor_tensor(x_res[:], x_res[:], tiles(w[:, :, :]), ALU.add)
                else:
                    ins = dve.tensor_tensor(att[:], tiles(w[:, :, :]), row(name), ALU.add)
                ins.then_inc(work_free[it.slot], 1)
                dve.wait_ge(work_free[it.slot], it.free())

            def small(s):
                link(dve.memset(vs[:], 1.0))
                it = s.items["V", 0, 0]
                w = filled(it)
                if s.ctx:
                    src = w[0:S, :, 0:D].rearrange("p b (h d) -> p b h d", d=HS)
                    for b in range(B):
                        ins = dve.tensor_tensor(vs[0:S, b, :, 0:HS], src[:, b], rows[0:S, ROWV[s.name + "v"], :].rearrange(
                            "p (h d) -> p h d", d=HS), ALU.add)
                else:
                    src = tiles(w[:, :, :])
                    for t in range(TILES):
                        ins = dve.tensor_tensor(vs[:, t, :, 0:HS], src[:, t, :].rearrange("p (h d) -> p h d", d=HS),
                                                rows[:, ROWV[s.name + "v"], :].rearrange("p (h d) -> p h d", d=HS), ALU.add)
                ins.then_inc(work_free[it.slot], 1)
                dve.wait_ge(work_free[it.slot], it.free())
                if s.masked:
                    kw = S if s.ctx else P
                    for t in range(B if s.ctx else TILES):
                        keep = ckeep if s.ctx else tkeep
                        ins = dve.tensor_scalar(vs[0:kw, t, :, :], vs[0:kw, t, :, :], keep[0:kw, t:t + 1], None, ALU.mult)
                    ins.then_inc(v_masked, 1)

                def prepare(n):
                    for k in range(2):
                        j = s.qk0 + 2 * n + k
                        w_ = N if k == 0 or not s.ctx else B * SP_
                        c = COLS["nselq" if k == 0 else "nselk"]
                        dst = (qs if k == 0 else ks)[:, n % 2, 0:w_]
                        it = s.items["QK"[k], n, 0]
                        dve.wait_ge(work_free[it.slot], it.free())
                        dve.scalar_tensor_tensor(dst, half[:, j % 2, 0:w_], cols[:, c:c + 1],
                                                 full[:, j % 2, 0:w_], ALU.mult, ALU.add).then_inc(qk_done, 1)
                        yield
                    for k, (b, hp, qt) in enumerate(s.m_list()):
                        it = s.items["M", n, k]
                        w = filled(it)
                        if s.ctx:
                            src = w[:, :, 0:QT * SP_].rearrange("p h (t c) -> p h t c", c=SP_)[:, :, :, 0:S]
                            dst = mneg[:, b * QT:(b + 1) * QT, 2 * hp:2 * hp + 2].rearrange("p t h -> p h t")
                        else:
                            src = w[:, :, 0:(qt + 1) * P]
                            dst = mneg[:, b * QT + qt, 2 * hp:2 * hp + 2]
                        dve.tensor_reduce(dst, src, AX.X, ALU.max, negate=True).then_inc(work_free[it.slot], 1)
                        yield

                def divide(n, b, hp):
                    dve.wait_ge(o_full, s.o0 + 4 * n + 2 * b + hp + 1)
                    o = oacc[:, hp, 0:2 * QT * (HS + 1)].rearrange("p (t h c) -> p t h c", t=QT, h=2)
                    link(dve.reciprocal(recip[:, hp, :, :], o[:, :, :, HS]))
                    c = (4 * n + 2 * hp) * HS
                    dst = on[:, b * QT:(b + 1) * QT, c:c + 2 * HS].rearrange("p t (h d) -> p t h d", h=2)
                    dve.tensor_tensor(dst, o[:, :, :, 0:HS], recip[:, hp, :, :].unsqueeze(3).to_broadcast([P, QT, 2, HS]),
                                      ALU.mult).then_inc(o_normed, 1)

                for _ in prepare(0):
                    pass
                for n in range(QUADS):
                    ahead = prepare(n + 1) if n + 1 < QUADS else iter(())
                    for u, (b, hp, kt) in enumerate(s.units):
                        if u and s.units[u - 1][2] == s.kt - 1:
                            divide(n, *s.units[u - 1][0:2])
                        for _ in range(2):
                            next(ahead, None)
                    divide(n, *s.units[-1][0:2])
                    for _ in ahead:
                        pass
                add_out(s.items["O", 0, 0], s.into, s.name + "o")

            def big(s):
                steps0 = steps[0]

                def prepare(n, buf, k):
                    it = s.prep(n, k)
                    if k < 2:
                        w_ = N if k == 0 or not s.ctx else B * SP_
                        dve.wait_ge(hi_done, count(2 * (s.hi0 + k + 1), n, 4))
                        w = work[it.slot]
                        for h, r in ((0, slice(0, HB)), (1, slice(HB, P))):
                            other = slice(HB, P) if h == 0 else slice(0, HB)
                            src = w[r, :, :] if w_ == N else w[r, 0, 0:w_]
                            if k == 0:
                                hi, lo = q2[r, buf, h, 0:w_], q1[other, buf, h, 0:w_]
                            else:
                                hi, lo = k1[r, buf, h, 0:w_], k2[r, buf, h, 0:w_]
                            if w_ == N:
                                hi, lo = hi.rearrange("p (b c) -> p b c", b=2), lo.rearrange("p (b c) -> p b c", b=2)
                            dve.tensor_tensor(lo, src, hi.bitcast(F32), ALU.subtract)
                            ins = dve.tensor_copy(q1[r, buf, h, 0:w_] if k == 0 else k1[other, buf, h, 0:w_],
                                                  q2[r, buf, h, 0:w_] if k == 0 else k1[r, buf, h, 0:w_])
                        ins.then_inc(work_free[it.slot], 1)
                    elif 3 <= k < 3 + s.ms:
                        w = filled(it)
                        if s.ctx:
                            b = k - 3
                            src = w[:, :, 0:QT * SP_].rearrange("p h (t c) -> p h t c", c=SP_)[:, :, :, 0:S]
                            dst = mneg[:, b * QT:(b + 1) * QT, 0:HB + 1:HB].rearrange("p t h -> p h t")
                        else:
                            src = w[:, :, :]
                            dst = mneg[:, k - 3, 0:HB + 1:HB]
                        dve.tensor_reduce(dst, src, AX.X, ALU.max, negate=True).then_inc(work_free[it.slot], 1)

                def divide(n, b):
                    dve.wait_ge(o_full, count(s.o0 + b + 1, n, 2))
                    o = oacc[:, :, 0:QT * (HB + 1)].rearrange("p h (t c) -> p h t c", t=QT)
                    r = recip[:].rearrange("p a t h -> p (a t h)")[:, 0:2 * QT].rearrange("p (h t) -> p h t", h=2)
                    dve.reciprocal(r, o[:, :, :, HB]).then_inc(vec, 1)
                    dve.wait_ge(vec, count(steps0 + b + 1, n, 2))
                    for h in range(2):
                        ins = dve.tensor_tensor(on[:, b * QT:(b + 1) * QT, h * HB:(h + 1) * HB], o[:, h, :, 0:HB],
                                                r[:, h, :].unsqueeze(2).to_broadcast([P, QT, HB]), ALU.mult)
                    ins.then_inc(o_normed, 1)

                def sum_out(n):
                    it = s.fin(n, 1)
                    w = filled(it)
                    dve.tensor_tensor(x_res[:], x_res[:], tiles(w[:, :, :]), ALU.add).then_inc(work_free[it.slot], 1)
                    dve.wait_ge(work_free[it.slot], it.free())

                for k in [0, 1] + list(range(3, 3 + s.ms)):
                    prepare((0, 0, None), 0, k)
                ms = list(range(3, 3 + s.ms))

                def body(n, buf, first, last):
                    nxt = shift(n, 1)
                    if s.ctx:
                        if not first:
                            sum_out(shift(n, -1))
                        if not last:
                            prepare(nxt, 1 - buf, 0)
                        divide(n, 0)
                        if not last:
                            prepare(nxt, 1 - buf, 1)
                            for k in ms:
                                prepare(nxt, 1 - buf, k)
                        divide(n, 1)
                    else:
                        if not first:
                            sum_out(shift(n, -1))
                        if not last:
                            prepare(nxt, 1 - buf, 0)
                            prepare(nxt, 1 - buf, 1)
                            prepare(nxt, 1 - buf, ms[0])
                        divide(n, 0)
                        if not last:
                            for k in ms[1:]:
                                prepare(nxt, 1 - buf, k)
                        divide(n, 1)
                pair_steps(dve, body)
                steps[0] += 2 * PAIRS
                sum_out((PAIRS - 1, 0, None))

            def mlp(s):
                if s.gated:
                    for f in range(FT):
                        it, g = s.up(f), s.gate(f)
                        w = filled(it)
                        dve.wait_ge(work_free[g.slot], g.free())
                        c = COLS[s.name] + f
                        dve.scalar_tensor_tensor(actT[:, f, :].rearrange("p (b c) -> p b c", b=2), w[:, :, :], cols[:, c:c + 1],
                                                 gbuf[:, f % 2, :].rearrange("p (b c) -> p b c", b=2), ALU.add,
                                                 ALU.mult).then_inc(work_free[it.slot], 1)
                add_out(s.out(), "x")

            norm_no = {s.name: i for i, s in enumerate([s for s in sections if isinstance(s, Norm) and s.name])}
            z_count, _ = counts(sections)
            dve.wait_ge(consts_loaded, 16 * 7)
            dve.tensor_scalar(tmask[:], tm8[:], -BIG, None, ALU.mult).then_inc(masks_made, 1)
            dve.tensor_scalar(cmask[:], cm8[:], -BIG, None, ALU.mult).then_inc(masks_made, 1)
            dve.tensor_scalar(tkeep[:], tc8[:], -1.0, 1.0, ALU.mult, ALU.add).then_inc(masks_made, 1)
            dve.tensor_scalar(ckeep[0:S, :], cc8[0:S, :], -1.0, 1.0, ALU.mult, ALU.add).then_inc(masks_made, 1)
            dve.wait_ge(masks_made, 4)
            dve.wait_ge(made, 19)
            dve.wait_ge(x_loaded, 16)
            adds = {"l0n1": ["l0sao"], "l0n2": ["l0cao"], "l0n3": ["l0b2"], "l1n": ["att", "l1b2"],
                    "l2n1": ["l2sao"], "l2n2": ["l2cao"], "l2n3": ["l2b2"],
                    "l3n1": ["l3sao"], "l3n2": ["l3cao"], "l3n3": ["l3b2"], None: []}
            for s in sections:
                if isinstance(s, Norm):
                    norm(s, adds[s.name])
                if isinstance(s, Small):
                    small(s)
                if isinstance(s, Big):
                    big(s)
                if isinstance(s, Mlp):
                    mlp(s)


def counts(sections):
    z_count, v_count, z, v = {}, {}, 0, 0
    for s in sections:
        if isinstance(s, Norm) and s.name:
            z_count[s.name] = z
            z += 2
        if isinstance(s, Small):
            v += s.masked
            v_count[s.name] = v
    return z_count, v_count


def kernel(**a):
    import numpy as np
    import concourse.bacc as bacc
    from concourse import mybir as mb
    from concourse.bass_utils import run_bass_kernel_spmd as run

    f = {k: np.asarray(v) for k, v in a.items()}

    def norm_names(layer, i):
        return {"l0": ("L0_xattn_ln%d_w" % i, "L0_xattn_ln%d_b" % i), "l1": ("L1_xattn_ln_g", "L1_xattn_ln_b")}.get(
            layer, ("%s_xattn_ln%d_g" % (layer.upper(), i), "%s_xattn_ln%d_b" % (layer.upper(), i)))

    cols = np.zeros((P, NCOLS), np.float32)
    for name in LN_NAMES:
        g, b = norm_names(name[:2], int(name[3:] or 1))
        cols[:, COLS[name + "g"]] = f[g]
        cols[:, COLS[name + "b"]] = f[b]
    for name, src in (("l0m", "L0_xattn_mlp1_b"), ("l1m", "L1_xattn_b1"), ("l2m", "L2_xattn_ff_b1"), ("l3m", "L3_xattn_ff_b1")):
        v = f[src].reshape(-1, P).T
        cols[:, COLS[name]:COLS[name] + v.shape[1]] = v

    def blocks(w):
        out = np.zeros(w.shape[:-1] + (H, ROWS), np.float32)
        for r in range(3):
            out[..., r * HS:(r + 1) * HS] = w.reshape(w.shape[:-1] + (H, HS))
        return out.reshape(w.shape[:-1] + (H * ROWS,))

    def bias_cols(name, b, ones_row):
        v = blocks(b).reshape(H, ROWS)
        v[:, ones_row] = 1.0
        cols[:, COLS[name]:COLS[name] + QUADS] = v.reshape(QUADS, P).T

    l0 = "L0_xattn_"
    l1 = "L1_xattn_"
    qkv_w, qkv_b = f[l0 + "qkv_w"], f[l0 + "qkv_b"]
    small = {
        "l0sa": (qkv_w[:, 0:D], qkv_w[:, D:2 * D], qkv_w[:, 2 * D:], f[l0 + "proj_w"],
                 qkv_b[0:D], qkv_b[D:2 * D], qkv_b[2 * D:], f[l0 + "proj_b"]),
        "l0ca": tuple(f[l0 + n] for n in ("q_w", "k_w", "v_w", "out_w", "q_b", "k_b", "v_b", "out_b")),
        "l1ca": tuple(f[l1 + n] for n in ("Wq", "Wk", "Wv", "Wo", "bq", "bk", "bv", "bo")),
    }
    rows = np.zeros((P, len(ROW_NAMES), D), np.float32)
    wts = np.zeros((P, NWTS), np.float32)
    for name, (wq, wk, wv, wo, bq, bk, bv, bo) in small.items():
        bias_cols(name + "q", bq, ROW_MASK)
        bias_cols(name + "k", bk, ROW_MAX)
        rows[:, ROWV[name + "v"]] = bv
        rows[:, ROWV[name + "o"]] = bo
        for p, w in (("q", blocks(wq)), ("k", blocks(wk)), ("v", wv), ("o", wo)):
            wts[0:w.shape[0], WTS[name + p]:WTS[name + p] + w.shape[1]] = w
    for name, src in (("l2sao", "L2_xattn_sa_bo"), ("l2cao", "L2_xattn_ca_bo"), ("l3sao", "L3_xattn_a1_bo"),
                      ("l3cao", "L3_xattn_a2_bo"), ("l0b2", "L0_xattn_mlp2_b"), ("l1b2", "L1_xattn_b2"),
                      ("l2b2", "L2_xattn_ff_b2"), ("l3b2", "L3_xattn_ff_b2")):
        rows[:, ROWV[name]] = f[src]
    for name, w1, w2 in (("l0m", l0 + "mlp1_w", l0 + "mlp2_w"), ("l1m", l1 + "W1", l1 + "W2"),
                         ("l2m", "L2_xattn_ff_w1", "L2_xattn_ff_w2"), ("l3m", "L3_xattn_ff_w1", "L3_xattn_ff_w2")):
        w = f[w1]
        wts[:, WTS[name + "1"]:WTS[name + "1"] + w.shape[1]] = w
        w = f[w2].reshape(FT, P, D).transpose(1, 0, 2).reshape(P, F)
        wts[:, WTS[name + "2"]:WTS[name + "2"] + F] = w
    nsel = np.zeros((2, 4, ROWS), np.float32)
    nsel[0, :, 2 * HS:3 * HS] = -1.0
    nsel[1, :, HS:2 * HS] = -1.0
    cols[:, COLS["nselq"]] = nsel[0].reshape(-1)
    cols[:, COLS["nselk"]] = nsel[1].reshape(-1)

    ctxT = np.zeros((DC, B, SP_), np.float32)
    ctxT[:, :, 0:S] = f["ctx_768"].transpose(2, 0, 1)
    tm = f["mask_BxS_bf0"]
    cm = f["mask_BxS2_bf0"]
    cm_row = np.zeros((1, B, SP_), bool)
    cm_row[0, :, 0:S] = cm

    arrays = {
        "x_in": f["x"].reshape(N, D), "ctx_in": ctxT.reshape(DC, B * SP_),
        "tmask_row": tm.reshape(1, N), "tmask_col": np.ascontiguousarray(tm.reshape(TILES, P).T),
        "cmask_row": cm_row.reshape(1, B * SP_), "cmask_col": np.ascontiguousarray(cm.T),
        "cols_in": cols, "rows_in": rows, "wts_in": wts,
    }
    big_names = {"l2sa": "L2_xattn_sa_w", "l2ca": "L2_xattn_ca_w", "l3sa": "L3_xattn_a1_w", "l3ca": "L3_xattn_a2_w"}
    for n, src in big_names.items():
        for p in "qkvo":
            arrays[n + p] = f[src + p]
    nc = bacc.Bacc("TRN2", target_bir_lowering=False, num_devices=1)
    ap = {}
    for n, v in arrays.items():
        arrays[n] = np.ascontiguousarray(v)
        ap[n] = nc.dram_tensor(n, v.shape, mb.dt.from_np(v.dtype), kind="ExternalInput").ap()
    out = nc.dram_tensor("out", (N, D), mb.dt.float32, kind="ExternalOutput").ap()
    big = {n: tuple(ap[n + p] for p in "qkvo") for n in big_names}
    program(nc, ap["x_in"], ap["ctx_in"], ap["tmask_row"], ap["tmask_col"], ap["cmask_row"], ap["cmask_col"],
            ap["cols_in"], ap["rows_in"], ap["wts_in"], big, out)
    r = run(nc, [arrays], core_ids=[0])
    return r.results[0]["out"].reshape(B, T, D)
```

```python
from contextlib import ExitStack

import concourse.bass as bass
from concourse import mybir

F32 = mybir.dt.float32
F32R = mybir.dt.float32r
BF16 = mybir.dt.bfloat16
U8 = mybir.dt.uint8
ALU = mybir.AluOpType
ACT = mybir.ActivationFunctionType
AX = mybir.AxisListType

P = 128
B = 2
T = 512
D = 128
N = B * T
TILES = N // P
QT = T // P
S = 77
SP_ = 78
DC = 96
H = 16
HS = 8
HB = 64
F = 512
FT = F // P
QUADS = H // 4
PAIRS = H // 2
ROWS = 32
ROW_MAX = 24
ROW_MASK = 25
BIG = 1e30
EPS = 1e-5

LN_NAMES = ["l0n1", "l0n2", "l0n3", "l1n", "l2n1", "l2n2", "l2n3", "l3n1", "l3n2", "l3n3"]
COLS = {}
for _n in LN_NAMES:
    COLS[_n + "g"] = len(COLS)
    COLS[_n + "b"] = len(COLS)
_c = len(COLS)
for _n, _k in (("l0m", FT), ("l1m", FT), ("l2m", 2 * FT), ("l3m", 2 * FT),
               ("l0saq", QUADS), ("l0sak", QUADS), ("l0caq", QUADS), ("l0cak", QUADS),
               ("l1caq", QUADS), ("l1cak", QUADS), ("nselq", 1), ("nselk", 1)):
    COLS[_n] = _c
    _c += _k
NCOLS = _c
ROW_NAMES = ["l0sao", "l0cao", "l1cao", "l2sao", "l2cao", "l3sao", "l3cao",
             "l0b2", "l1b2", "l2b2", "l3b2", "l0sav", "l0cav", "l1cav"]
ROWV = {n: i for i, n in enumerate(ROW_NAMES)}
WTS = {}
_c = 0
LOADS = [("l0sa",), ("l0ca", "l0m"), ("l1ca", "l1m"), ("l2m",), ("l3m",)]
LOAD_AT = []
for _g in LOADS:
    LOAD_AT.append(_c)
    for _n in _g:
        if _n.endswith("a"):
            for _p, _k in (("q", QUADS * P), ("k", QUADS * P), ("v", D), ("o", D)):
                WTS[_n + _p] = _c
                _c += _k
        else:
            WTS[_n + "1"] = _c
            _c += F if _n in ("l0m", "l1m") else 2 * F
            WTS[_n + "2"] = _c
            _c += F
LOAD_AT.append(_c)
NWTS = _c


class Item:

    def __init__(self, c, n=None, per=0):
        a, m, self.i = n if n is not None else (0, 0, None)
        self.c, self.step = c + per * a, per * m
        assert self.step % 2 == 0

    def _value(self, c, step):
        return c if self.i is None else self.i * step + c

    @property
    def slot(self):
        return self.c % 2

    def full(self):
        return self._value(self.c + 1, self.step)

    def free(self):
        return self._value(self.c // 2 + 1, self.step // 2)

    def vacant(self):
        return self._value(self.c // 2, self.step // 2)

    def first(self):
        return self.i is None and self.c < 2


def count(c, n, per):
    a, m, i = n
    return c + per * a if i is None else i * (per * m) + (c + per * a)


class Small:

    def __init__(self, name, causal, ctx, masked, into, base):
        self.name, self.causal, self.ctx, self.masked, self.into = name, causal, ctx, masked, into
        self.kt = 1 if ctx else QT
        self.kw = S if ctx else P
        order = [("V", 0, 0)]
        ms = 4 if ctx else 4 * QT
        for n in range(QUADS):
            order += [("Q", n, 0), ("K", n, 0)] + [("M", n, k) for k in range(ms)] + [("T", n, 0)]
        order += [("A", 0, 0), ("O", 0, 0)]
        self.items = {k: Item(base["item"] + i) for i, k in enumerate(order)}
        self.unit0, self.o0, self.qk0, self.mrow0 = base["unit"], base["o"], base["qk"], base["mrow"]
        self.units = [(b, hp, kt) for b in range(B) for hp in range(2) for kt in range(self.kt)]
        self.sqk, self.sv, self.sw = self.qk0, None, None
        base["item"] += len(order)
        base["unit"] += QUADS * len(self.units)
        base["o"] += QUADS * 4
        base["qk"] += QUADS * 2
        base["mrow"] += QUADS

    def m_list(self):
        if self.ctx:
            return [(b, hp, None) for b in range(B) for hp in range(2)]
        return [(b, hp, qt) for b in range(B) for hp in range(2) for qt in range(QT)]


class Big:

    ctx, kt, kw, g, ms = False, QT, P, B * QT, B * QT
    np = 3 + ms + 1
    PREP = [0, 2] + list(range(4, np + 2))
    FIN = [1, 3]
    T = np - 1

    def __init__(self, name, base):
        self.name = name
        self.item0, self.unit0, self.o0 = base["item"], base["unit"], base["o"]
        self.hi0, self.w0, self.free_from = base["hi"], base["w"], base["big_end"]
        self.turn = self.np + 2
        self.turns0 = self.item0 + 2 * self.np
        base["item"] = self.turns0 + self.turn * (PAIRS - 2) + 4
        base["big_end"] = base["item"] - 1
        base["unit"] += PAIRS * self.g
        base["o"] += PAIRS * 2
        base["hi"] += PAIRS * (1 if self.ctx else 2)
        base["w"] += PAIRS

    def prep(self, n, k):
        if n in ((0, 0, None), (1, 0, None)):
            return Item(self.item0 + n[0] * self.np + k)
        return Item(self.turns0 - 2 * self.turn + self.PREP[k], n, self.turn)

    def fin(self, n, k):
        if n in ((PAIRS - 2, 0, None), (PAIRS - 1, 0, None)):
            return Item(self.turns0 + self.turn * (PAIRS - 2) + 2 * (n[0] - PAIRS + 2) + k)
        return Item(self.turns0 + self.FIN[k], n, self.turn)

    def loaded(self, n, per):
        a, m, i = n
        c = per * ((self.w0 + a) // 2 + 1)
        return c if i is None else i * (per * m // 2) + c


class Cross(Big):

    ctx, kt, kw, g, ms = True, 1, S, B, B
    np = 6
    PREP = [1, 2, 3, 4, 5, 7]
    FIN = [0, 6]
    T = 5


class Norm:

    def __init__(self, name, src, base, split=False):
        self.name, self.src, self.split = name, src, split
        self.item0 = base["item"]
        base["item"] += 2


class Mlp:
    def __init__(self, name, gated, base):
        self.name, self.gated = name, gated
        self.item0 = base["item"]
        self.per = 2 if gated else 1
        base["item"] += FT * self.per + 1

    def gate(self, f):
        return Item(self.item0 + f * self.per)

    def up(self, f):
        return Item(self.item0 + f * self.per + 1)

    def out(self):
        return Item(self.item0 + FT * self.per)


def plan():
    base = dict(item=0, unit=0, o=0, qk=0, mrow=0, hi=0, w=0, big_end=None)
    return [
        Norm("l0n1", "x", base), Small("l0sa", True, False, True, "x", base),
        Norm("l0n2", "x", base), Small("l0ca", False, True, True, "x", base),
        Norm("l0n3", "x", base), Mlp("l0m", False, base),
        Norm(None, "x", base), Small("l1ca", False, True, False, "att", base),
        Norm("l1n", "att", base), Mlp("l1m", False, base),
        Norm("l2n1", "x", base), Big("l2sa", base),
        Norm("l2n2", "x", base, True), Cross("l2ca", base),
        Norm("l2n3", "x", base), Mlp("l2m", True, base),
        Norm("l3n1", "x", base), Big("l3sa", base),
        Norm("l3n2", "x", base, True), Cross("l3ca", base),
        Norm("l3n3", "x", base), Mlp("l3m", True, base),
    ]


def pair_steps(eng, body):
    body((0, 0, None), 0, True, False)
    with eng.Fori(0, (PAIRS - 2) // 2) as i:
        body((1, 2, i), 1, False, False)
        body((2, 2, i), 0, False, False)
    body((PAIRS - 1, 0, None), (PAIRS - 1) % 2, False, True)


def shift(n, by):
    return (n[0] + by, n[1], n[2])


def program(nc, x_in, ctx_in, tmask_row, tmask_col, cmask_row, cmask_col, cols_in, rows_in, wts_in, big_in, out):
    sections = plan()
    with ExitStack() as ctx:
        def sb(name, shape, dt=F32):
            return ctx.enter_context(nc.sbuf_tensor(name, shape, dt))

        def sem(name):
            return ctx.enter_context(nc.semaphore(name))

        x_res = sb("x_res", [P, TILES, D])
        att = sb("att", [P, TILES, D])
        z = sb("z", [P, TILES, D])
        hT = sb("hT", [P, N])
        ctxT = sb("ctxT", [DC, B * SP_])
        cols = sb("cols", [P, NCOLS])
        rows = sb("rows", [P, len(ROW_NAMES), D])
        wts = sb("wts", [P, NWTS])
        ident = sb("ident", [P, P])
        ident_bf = sb("ident_bf", [P, P], BF16)
        after_q = sb("after_q", [P, P], BF16)
        after_k = sb("after_k", [P, P], BF16)
        mask_sel = sb("mask_sel", [1, P], BF16)
        tm8 = sb("tm8", [1, N], U8)
        tc8 = sb("tc8", [P, TILES], U8)
        cm8 = sb("cm8", [1, B * SP_], U8)
        cc8 = sb("cc8", [P, B], U8)
        tmask = sb("tmask", [1, N], BF16)
        cmask = sb("cmask", [1, B * SP_], BF16)
        tkeep = sb("tkeep", [P, TILES])
        ckeep = sb("ckeep", [P, B])
        stats = sb("stats", [P, TILES, 6])
        mv = sb("mv", [P, TILES, 2])
        std = sb("std", [P, TILES])
        rstd = sb("rstd", [P, TILES])
        q1 = sb("q1", [P, 2, 2, N], F32R)
        q2 = sb("q2", [P, 2, 2, N], F32R)
        k1 = sb("k1", [P, 2, 2, N], F32R)
        k2 = sb("k2", [P, 2, 2, N], F32R)
        vb = sb("vb", [P, 2, TILES, 2, HB + 1])
        bigw = sb("bigw", [P, 2, 4, P])
        h_hi, h_lo = q1[:, 0, 0, :], q1[:, 0, 1, :]
        g_hi, g_lo = k1[:, 0, 0, 0:2 * B * SP_], k1[:, 0, 1, 0:2 * B * SP_]
        mrow = q1[0:HB + 1, 1, 0, :]
        kz = sb("kz", [P, 2, B * SP_])
        sel = sb("sel", [HB + 1, 2, SP_], F32R)
        full = sb("full", [P, 2, N])
        qs = sb("qs", [P, 2, N], F32R)
        ks = sb("ks", [P, 2, N], F32R)
        vs = sb("vs", [P, TILES, H, HS + 1])
        mT = sb("mT", [4, N], F32R)
        mneg = sb("mneg", [P, TILES, HB + 2])
        prob = sb("prob", [P, 2, 2, T])
        recip = sb("recip", [P, 2, QT, 2])
        on = z
        onT = sb("onT", [P, N])
        gbuf = full
        actT = sb("actT", [P, FT, N])
        half = actT

        st = ctx.enter_context(nc.psum_tensor("st", [P, 2, 512], F32))
        oacc = ctx.enter_context(nc.psum_tensor("oacc", [P, 2, 512], F32))
        work = [ctx.enter_context(nc.psum_tensor(f"work{i}", [P, 2, 512], F32)) for i in range(2)]

        x_loaded = sem("x_loaded")
        consts_loaded = sem("consts_loaded")
        wts_loaded = [sem(f"wts_loaded{i}") for i in range(len(LOADS))]
        wqkv_loaded = [sem("wqkv_loaded0"), sem("wqkv_loaded1")]
        wo_loaded = [sem("wo_loaded0"), sem("wo_loaded1")]
        made = sem("made")
        masks_made = sem("masks_made")
        work_full = sem("work_full")
        work_free = [sem("work_free0"), sem("work_free1")]
        st_full = sem("st_full")
        exp_done = sem("exp_done")
        o_full = sem("o_full")
        o_normed = sem("o_normed")
        hi_done = sem("hi_done")
        h_split = sem("h_split")
        qk_done = sem("qk_done")
        v_masked = sem("v_masked")
        mrow_done = sem("mrow_done")
        var_done = sem("var_done")
        std_done = sem("std_done")
        z_done = sem("z_done")
        vec = sem("vec")
        stored = sem("stored")

        block = ctx.enter_context(nc.Block())

        @block.sync
        def _(sp):
            sp.dma_start(x_res[:], x_in.rearrange("(t p) d -> p t d", p=P)).then_inc(x_loaded, 16)
            for dst, src in ((cols[:], cols_in), (rows[:], rows_in), (ctxT[:], ctx_in), (tm8[:], tmask_row),
                             (tc8[:], tmask_col), (cm8[:], cmask_row), (cc8[0:S, :], cmask_col)):
                sp.dma_start(dst, src).then_inc(consts_loaded, 16)
            for i in range(len(LOADS)):
                sp.dma_start(wts[:, LOAD_AT[i]:LOAD_AT[i + 1]],
                             wts_in[:, LOAD_AT[i]:LOAD_AT[i + 1]]).then_inc(wts_loaded[i], 16)

            def move_max_rows(s):
                for n in range(QUADS):
                    it = s.items["T", n, 0]
                    sp.wait_ge(work_free[it.slot], it.free())
                    sp.dma_start(qs[ROW_MAX:P:ROWS, n % 2, :].bitcast(F32), mT[:, :].bitcast(F32)).then_inc(mrow_done, 16)

            def load_pairs(s):
                wq, wk, wv, wo = big_in[s.name]
                kr = DC if s.ctx else D

                def load(n, buf, before):
                    at = n[0] * P if n[2] is None else n[2] * (n[1] * P) + n[0] * P
                    if before is not None:
                        sp.wait_ge(work_full, s.prep(before, s.T).full())
                    sp.dma_start(bigw[:, buf, 0, :], wq[bass.ds(at, P), :] if s.ctx else
                                 wq[:, bass.ds(at, P)]).then_inc(wqkv_loaded[buf], 16)
                    sp.dma_start(bigw[0:kr, buf, 1, :], wk[:, bass.ds(at, P)]).then_inc(wqkv_loaded[buf], 16)
                    sp.dma_start(bigw[0:kr, buf, 2, :], wv[:, bass.ds(at, P)]).then_inc(wqkv_loaded[buf], 16)
                    if before is not None:
                        sp.wait_ge(work_full, s.fin(before, 1).full())
                    sp.dma_start(bigw[:, buf, 3, :], wo[bass.ds(at, P), :]).then_inc(wo_loaded[buf], 16)

                if s.free_from is not None:
                    sp.wait_ge(work_full, Item(s.free_from).full())
                load((0, 0, None), 0, None)
                load((1, 0, None), 1, None)
                load((2, 0, None), 0, (0, 0, None))
                load((3, 0, None), 1, (1, 0, None))
                with sp.Fori(0, (PAIRS - 4) // 2) as i:
                    load((4, 2, i), 0, (2, 2, i))
                    load((5, 2, i), 1, (3, 2, i))

            for s in sections:
                if isinstance(s, Small):
                    move_max_rows(s)
                if isinstance(s, Big):
                    load_pairs(s)
            last = sections[-1].out()
            sp.wait_ge(work_free[last.slot], last.free())
            sp.dma_start(out.rearrange("(t p) d -> p t d", p=P), x_res[:]).then_inc(stored, 16)
            sp.wait_ge(stored, 16)

        @block.gpsimd
        def _(pool):
            pool.memset(ident[:], 0.0).then_inc(made, 1)
            pool.memset(ident_bf[:], 0.0).then_inc(made, 1)
            pool.memset(after_q[:], 0.0).then_inc(made, 1)
            pool.memset(after_k[:], 0.0).then_inc(made, 1)
            pool.memset(mask_sel[:], 0.0).then_inc(made, 1)
            pool.wait_ge(made, 5)
            for m in (ident, ident_bf):
                pool.affine_select(out=m[:], in_=m[:], compare_op=ALU.not_equal, fill=1.0, base=0,
                                   pattern=[[-1, P]], channel_multiplier=1).then_inc(made, 1)
            pool.affine_select(out=after_q[:], in_=after_q[:], compare_op=ALU.is_ge, fill=-BIG, base=0,
                               pattern=[[-1, P]], channel_multiplier=1).then_inc(made, 1)
            pool.affine_select(out=after_k[:], in_=after_k[:], compare_op=ALU.is_ge, fill=-BIG, base=0,
                               pattern=[[1, P]], channel_multiplier=-1).then_inc(made, 1)
            for j in range(4):
                pool.memset(mask_sel[0:1, ROWS * j + ROW_MASK:ROWS * j + ROW_MASK + 1], 1.0).then_inc(made, 1)
            pool.memset(q2[:].bitcast(F32), 0.0).then_inc(made, 1)
            pool.memset(k2[:].bitcast(F32), 0.0).then_inc(made, 1)
            pool.memset(mneg[:], 0.0).then_inc(made, 1)
            pool.memset(vb[:], 1.0).then_inc(made, 1)
            pool.memset(kz[:], 0.0).then_inc(made, 1)
            pool.memset(sel[:].bitcast(F32), 0.0).then_inc(made, 1)
            pool.wait_ge(made, 19)
            pool.memset(k2[HB:HB + 1, :, 0, :].bitcast(F32), 1.0).then_inc(made, 1)
            pool.memset(k2[0:1, :, 1, :].bitcast(F32), 1.0).then_inc(made, 1)
            pool.memset(sel[0:1, 0, :].bitcast(F32), 1.0).then_inc(made, 1)
            pool.memset(sel[HB:HB + 1, 1, :].bitcast(F32), 1.0).then_inc(made, 1)

        @block.tensor
        def _(pe):
            def open_item(it):
                if not it.first():
                    pe.wait_ge(work_free[it.slot], it.vacant())
                return work[it.slot]

            def taken(it):
                pe.wait_ge(work_free[it.slot], it.free())

            def norm(s):
                for k in range(2):
                    if s.name:
                        pe.wait_ge(z_done, z_count[s.name] + k + 1)
                        src = z
                    else:
                        if k == 0:
                            taken(x_item[0])
                        src = x_res
                    it = Item(s.item0 + k)
                    w = open_item(it)
                    for t in range(QT):
                        mm = pe.transpose(w[:, 0, t * P:(t + 1) * P], src[:, k * QT + t, :], ident[:])
                    mm.then_inc(work_full, 1)

            def both_halves(w, lhsT, rhs, then=None):
                for b in range(B):
                    mm = pe.matmul(w[:, b, :], lhsT, rhs[:, b * T:(b + 1) * T], start=True, stop=then is None)
                    if then is not None:
                        mm = then(b)
                return mm

            def transpose_out(it):
                w = open_item(it)
                for t in range(TILES):
                    mm = pe.transpose(w[:, t // QT, (t % QT) * P:(t % QT + 1) * P], on[:, t, :], ident[:])
                mm.then_inc(work_full, 1)

            def project_out(it, before, wo):
                w = open_item(it)
                if before.slot != it.slot:
                    taken(before)
                for t in range(TILES):
                    mm = pe.matmul(w[:, t // QT, (t % QT) * P:(t % QT + 1) * P], onT[:, t * P:(t + 1) * P],
                                   wo, start=True, stop=True)
                mm.then_inc(work_full, 1)

            def values(it, wv, ctx_side):
                w = open_item(it)
                if ctx_side:
                    for b in range(B):
                        mm = pe.matmul(w[0:S, b, 0:D], ctxT[:, b * SP_:b * SP_ + S], wv, start=True, stop=True)
                else:
                    for t in range(TILES):
                        mm = pe.matmul(w[:, t // QT, (t % QT) * P:(t % QT + 1) * P], hT[:, t * P:(t + 1) * P],
                                       wv, start=True, stop=True)
                mm.then_inc(work_full, 1)

            def small(s):
                kr = DC if s.ctx else D
                wv = wts[0:kr, WTS[s.name + "v"]:WTS[s.name + "v"] + D]
                wo = wts[:, WTS[s.name + "o"]:WTS[s.name + "o"] + D]

                def prepare(n):
                    wq = wts[:, WTS[s.name + "q"] + n * P:WTS[s.name + "q"] + (n + 1) * P]
                    wk = wts[0:kr, WTS[s.name + "k"] + n * P:WTS[s.name + "k"] + (n + 1) * P]
                    w = open_item(s.items["Q", n, 0])
                    both_halves(w, wq, hT).then_inc(work_full, 1)
                    yield
                    w = open_item(s.items["K", n, 0])
                    if s.ctx:
                        mm = pe.matmul(w[:, 0, 0:B * SP_], wk, ctxT[:], start=True, stop=not s.masked)
                        if s.masked:
                            mm = pe.matmul(w[:, 0, 0:B * SP_], mask_sel[:], cmask[:], start=False, stop=True)
                    else:
                        mm = both_halves(w, wk, hT, lambda b: pe.matmul(
                            w[:, b, :], mask_sel[:], tmask[:, b * T:(b + 1) * T], start=False, stop=True))
                    mm.then_inc(work_full, 1)
                    yield
                    pe.wait_ge(qk_done, s.qk0 + 2 * n + 2)
                    buf = n % 2
                    for k, (b, hp, qt) in enumerate(s.m_list()):
                        w = open_item(s.items["M", n, k])
                        for hh in range(2):
                            r = ROWS * (2 * hp + hh)
                            if s.ctx:
                                for t in range(QT):
                                    mm = pe.matmul(w[:, hh, t * SP_:(t + 1) * SP_],
                                                   qs[r:r + ROWS, buf, b * T + t * P:b * T + (t + 1) * P],
                                                   ks[r:r + ROWS, buf, b * SP_:(b + 1) * SP_], start=True, stop=True,
                                                   tile_position=(r, 0))
                            else:
                                keys = (qt + 1) * P
                                pe.matmul(w[:, hh, 0:keys], qs[r:r + ROWS, buf, b * T + qt * P:b * T + (qt + 1) * P],
                                          ks[r:r + ROWS, buf, b * T:b * T + keys], start=True, stop=False,
                                          skip_group_check=True, tile_position=(r, 0))
                                mm = pe.matmul(w[:, hh, qt * P:keys], ident_bf[:], after_q[:], start=False, stop=True,
                                               skip_group_check=True)
                        mm.then_inc(work_full, 1)
                        yield
                    it = s.items["M", n, len(s.m_list()) - 1]
                    taken(it)
                    before = s.items["M", n, len(s.m_list()) - 2]
                    taken(before)
                    w = open_item(s.items["T", n, 0])
                    for t in range(TILES):
                        mm = pe.transpose(w[0:4, t // QT, (t % QT) * P:(t % QT + 1) * P], mneg[:, t, 0:4], ident[:])
                    mm.then_inc(work_full, 1)
                    yield

                values_it = s.items["V", 0, 0]
                values(values_it, wv, s.ctx)
                for _ in prepare(0):
                    pass
                taken(values_it)
                if s.masked:
                    pe.wait_ge(v_masked, v_count[s.name])

                def scores(n, u):
                    b, hp, kt = s.units[u]
                    buf, g = n % 2, s.unit0 + n * len(s.units) + u
                    if u == 0:
                        pe.wait_ge(mrow_done, 16 * (s.mrow0 + n + 1))
                    if g:
                        pe.wait_ge(exp_done, g)
                    q0 = kt * P if s.causal else 0
                    kc = (b * T + kt * P) if not s.ctx else b * SP_
                    for hh in range(2):
                        r = ROWS * (2 * hp + hh)
                        mm = pe.matmul(st[0:s.kw, hh, q0:T], ks[r:r + ROWS, buf, kc:kc + s.kw],
                                       qs[r:r + ROWS, buf, b * T + q0:(b + 1) * T], start=True, stop=not s.causal,
                                       skip_group_check=True, tile_position=(r, 0))
                        if s.causal:
                            mm = pe.matmul(st[:, hh, q0:q0 + P], ident_bf[:], after_k[:], start=False, stop=True,
                                           skip_group_check=True)
                    mm.then_inc(st_full, 1)

                def weigh(n, u):
                    b, hp, kt = s.units[u]
                    g = s.unit0 + n * len(s.units) + u
                    o = s.o0 + 4 * n + 2 * b + hp
                    pe.wait_ge(exp_done, g + 1)
                    if kt == 0 and o:
                        pe.wait_ge(o_normed, max(o - 1, s.o0))
                    for t in range(kt if s.causal else 0, QT):
                        for hh in range(2):
                            c = (2 * t + hh) * (HS + 1)
                            mm = pe.matmul(oacc[:, hp, c:c + HS + 1], prob[0:s.kw, g % 2, hh, t * P:(t + 1) * P],
                                           vs[0:s.kw, (b * QT + kt) if not s.ctx else b, 4 * n + 2 * hp + hh, :],
                                           start=(kt == 0 and t == 0 and hh == 0),
                                           stop=(kt == (t if s.causal else s.kt - 1)), skip_group_check=True)
                    if kt == s.kt - 1:
                        mm.then_inc(o_full, 1)

                for n in range(QUADS):
                    ahead = prepare(n + 1) if n + 1 < QUADS else iter(())
                    per = 2
                    for u in range(len(s.units)):
                        scores(n, u)
                        if u:
                            weigh(n, u - 1)
                        for _ in range(per):
                            next(ahead, None)
                    weigh(n, len(s.units) - 1)
                    for _ in ahead:
                        pass
                o_all = s.o0 + 4 * QUADS
                pe.wait_ge(o_normed, o_all)
                transpose_out(s.items["A", 0, 0])
                project_out(s.items["O", 0, 0], s.items["A", 0, 0], wo)

            def weigh(s, n, buf, g):
                b, kt = divmod(g, s.kt)
                pe.wait_ge(exp_done, count(s.unit0 + g + 1, n, s.g))
                if kt == 0:
                    pe.wait_ge(o_normed, count(s.o0 + b, n, 2))
                slot = (s.unit0 + g) % 2
                for h in range(2):
                    for t in range(QT):
                        mm = pe.matmul(oacc[:, h, t * (HB + 1):(t + 1) * (HB + 1)],
                                       prob[0:s.kw, slot, h, t * P:(t + 1) * P],
                                       vb[0:s.kw, buf, (b * QT + kt) if not s.ctx else b, h, :],
                                       start=(kt == 0 and t == 0), stop=(kt == s.kt - 1), skip_group_check=True)
                if kt == s.kt - 1:
                    mm.then_inc(o_full, 1)

            def finish(s, n, buf, k):
                if k == 0:
                    pe.wait_ge(o_normed, count(s.o0 + 2, n, 2))
                    transpose_out(s.fin(n, 0))
                else:
                    pe.wait_ge(wo_loaded[buf], s.loaded(n, 16))
                    project_out(s.fin(n, 1), s.fin(n, 0), bigw[:, buf, 3, :])

            def max_rows(s, n):
                taken(s.prep(n, s.T - 1))
                taken(s.prep(n, s.T - 2))
                w = open_item(s.prep(n, s.T))
                for t in range(TILES):
                    mm = pe.transpose(w[0:HB + 1, t // QT, (t % QT) * P:(t % QT + 1) * P], mneg[:, t, 0:HB + 1], ident[:])
                mm.then_inc(work_full, 1)

            def big(s):
                def prepare(n, buf, k):
                    wq, wk, wv = bigw[:, buf, 0, :], bigw[:, buf, 1, :], bigw[:, buf, 2, :]
                    it = s.prep(n, k)
                    if k == s.T:
                        max_rows(s, n)
                        return
                    if k == 0:
                        pe.wait_ge(wqkv_loaded[buf], s.loaded(n, 48))
                    if k == 2:
                        values(it, wv, False)
                        return
                    w = open_item(it)
                    if k < 2:
                        mm = both_halves(w, wq if k == 0 else wk, hT)
                    else:
                        if k == 3:
                            taken(s.prep(n, 1))
                            if s.prep(n, 0).slot != s.prep(n, 1).slot:
                                taken(s.prep(n, 0))
                        b, t = divmod(k - 3, QT)
                        q0 = b * T + t * P
                        for h in range(2):
                            mm = pe.matmul(w[:, h, :], q1[:, buf, h, q0:q0 + P],
                                           k1[:, buf, h, b * T:(b + 1) * T], start=True, stop=True)
                    mm.then_inc(work_full, 1)

                def scores(n, buf, g):
                    b, kt = divmod(g, s.kt)
                    if g == 0:
                        taken(s.prep(n, s.T))
                    pe.wait_ge(exp_done, count(s.unit0 + g, n, s.g))
                    kc = b * T + kt * P
                    for h in range(2):
                        pe.matmul(st[:, h, :], k1[:, buf, h, kc:kc + P], q1[:, buf, h, b * T:(b + 1) * T],
                                  start=True, stop=False)
                        mm = pe.matmul(st[:, h, :], k2[:, buf, h, kc:kc + P], q2[:, buf, h, b * T:(b + 1) * T],
                                       start=False, stop=True)
                    mm.then_inc(st_full, 1)

                def body(n, buf, first, last):
                    nxt, prev, other = shift(n, 1), shift(n, -1), 1 - buf
                    with_unit = [[0, "A"], [], [1], ["O"], [2, 3], [4, 5], [6, 7, 8], [9, 10]]
                    for g in range(s.g):
                        scores(n, buf, g)
                        if g and g < s.g - 1:
                            weigh(s, n, buf, g - 1)
                        for k in with_unit[g]:
                            if k in ("A", "O"):
                                if not first:
                                    finish(s, prev, other, "AO".index(k))
                            elif not last:
                                prepare(nxt, other, k)
                    weigh(s, n, buf, s.g - 2)
                    if not last:
                        prepare(nxt, other, s.T)
                    weigh(s, n, buf, s.g - 1)

                for k in range(s.np):
                    prepare((0, 0, None), 0, k)
                pair_steps(pe, body)
                finish(s, (PAIRS - 1, 0, None), 1, 0)
                finish(s, (PAIRS - 1, 0, None), 1, 1)

            def cross(s):
                def prepare(n, buf, k):
                    it = s.prep(n, k)
                    if k == 0:
                        pe.wait_ge(wqkv_loaded[buf], s.loaded(n, 48))
                        w = open_item(it)
                        mm = pe.matmul(w[:, 0, 0:B * SP_], bigw[0:DC, buf, 1, :], ctxT[:], start=True, stop=True)
                    elif k == 1:
                        values(it, bigw[0:DC, buf, 2, :], True)
                        return
                    elif k == 2:
                        taken(s.prep(n, 0))
                        w = open_item(it)
                        mm = pe.matmul(w[:, 0, 0:2 * B * SP_], bigw[:, buf, 0, :], kz[:].rearrange("p h c -> p (h c)"),
                                       start=True, stop=True)
                    elif k < s.T:
                        b = k - 3
                        w = open_item(it)
                        if b == 0:
                            taken(s.prep(n, 2))
                        for t in range(QT):
                            q0 = b * T + t * P
                            mm = pe.matmul(w[:, t // 2, (t % 2) * 2 * SP_:(t % 2 + 1) * 2 * SP_], h_hi[:, q0:q0 + P],
                                           g_hi.rearrange("p (h b c) -> p b h c", h=2, b=B)[:, b], start=True, stop=True)
                    else:
                        max_rows(s, n)
                        return
                    mm.then_inc(work_full, 1)

                def scores(n, b):
                    if b == 0:
                        taken(s.prep(n, s.T))
                    pe.wait_ge(exp_done, count(s.unit0 + b, n, s.g))
                    q = slice(b * T, (b + 1) * T)
                    for h in range(2):
                        c = slice((h * B + b) * SP_, (h * B + b) * SP_ + S)
                        passes = [(g_hi[:, c], h_hi[:, q]), (g_hi[:, c], h_lo[:, q]), (g_lo[:, c], h_hi[:, q]),
                                  (sel[:, h, 0:S], mrow[:, q])]
                        for i, (keys, queries) in enumerate(passes):
                            mm = pe.matmul(st[0:S, h, :], keys, queries, start=(i == 0), stop=(i == len(passes) - 1))
                    mm.then_inc(st_full, 1)

                def body(n, buf, first, last):
                    nxt, prev, other = shift(n, 1), shift(n, -1), 1 - buf
                    scores(n, 0)
                    if not first:
                        finish(s, prev, other, 0)
                    if not last:
                        prepare(nxt, other, 0)
                    scores(n, 1)
                    if not last:
                        prepare(nxt, other, 1)
                        prepare(nxt, other, 2)
                    weigh(s, n, buf, 0)
                    if not last:
                        prepare(nxt, other, 3)
                        prepare(nxt, other, 4)
                    if not first:
                        finish(s, prev, other, 1)
                    if not last:
                        prepare(nxt, other, s.T)
                    weigh(s, n, buf, 1)

                for k in range(s.np):
                    prepare((0, 0, None), 0, k)
                pe.wait_ge(h_split, 1 if s.name == "l2ca" else 2)
                pair_steps(pe, body)
                finish(s, (PAIRS - 1, 0, None), 1, 0)
                finish(s, (PAIRS - 1, 0, None), 1, 1)

            def mlp(s):
                w1, w2 = WTS[s.name + "1"], WTS[s.name + "2"]
                for f in range(FT):
                    if s.gated:
                        w = open_item(s.gate(f))
                        both_halves(w, wts[:, w1 + F + f * P:w1 + F + (f + 1) * P], hT).then_inc(work_full, 1)
                        w = open_item(s.up(f))
                        both_halves(w, wts[:, w1 + f * P:w1 + (f + 1) * P], hT).then_inc(work_full, 1)
                    else:
                        w = open_item(s.gate(f))
                        both_halves(w, wts[:, w1 + f * P:w1 + (f + 1) * P], hT).then_inc(work_full, 1)
                w = open_item(s.out())
                for f in range(FT):
                    taken(s.up(f) if s.gated else s.gate(f))
                for t in range(TILES):
                    for f in range(FT):
                        mm = pe.matmul(w[:, t // QT, (t % QT) * P:(t % QT + 1) * P], actT[:, f, t * P:(t + 1) * P],
                                       wts[:, w2 + f * P:w2 + (f + 1) * P], start=(f == 0), stop=(f == FT - 1))
                mm.then_inc(work_full, 1)

            pe.wait_ge(made, 23)
            pe.wait_ge(masks_made, 4)
            pe.wait_ge(consts_loaded, 16 * 7)
            z_count, v_count = counts(sections)
            x_item = [None]
            for s in sections:
                for i, g in enumerate(LOADS):
                    if s.name in g:
                        pe.wait_ge(wts_loaded[i], 16)
                if isinstance(s, Norm):
                    norm(s)
                    taken(Item(s.item0))
                    taken(Item(s.item0 + 1))
                if isinstance(s, Small):
                    small(s)
                if isinstance(s, Cross):
                    cross(s)
                elif isinstance(s, Big):
                    big(s)
                if isinstance(s, Mlp):
                    mlp(s)
                    x_item[0] = s.out()

        @block.scalar
        def _(act):
            def filled(it):
                act.wait_ge(work_full, it.full())
                return work[it.slot]

            def norm(s):
                if s.name:
                    act.wait_ge(var_done, norm_no[s.name] + 1)
                    act.activation(std[:], mv[:, :, 1], ACT.Sqrt, bias=EPS).then_inc(std_done, 1)
                for k in range(2):
                    it = Item(s.item0 + k)
                    w = filled(it)
                    dst = hT[:, k * T:(k + 1) * T]
                    if s.name:
                        g, b = COLS[s.name + "g"], COLS[s.name + "b"]
                        ins = act.activation(dst, w[:, 0, :], ACT.Identity, bias=cols[:, b:b + 1], scale=cols[:, g:g + 1])
                        if s.split:
                            ins = act.activation(h_hi[:, k * T:(k + 1) * T], w[:, 0, :], ACT.Identity,
                                                 bias=cols[:, b:b + 1], scale=cols[:, g:g + 1])
                    else:
                        ins = act.activation(dst, w[:, 0, :], ACT.Copy)
                    ins.then_inc(work_free[it.slot], 1)

            def take_out(it):
                w = filled(it)
                act.activation(onT[:], w[:, :, :], ACT.Copy).then_inc(work_free[it.slot], 1)

            def small(s):
                def prepare(n):
                    for k, what in enumerate("QK"):
                        j = s.qk0 + 2 * n + k
                        it = s.items[what, n, 0]
                        w = filled(it)
                        if j >= 2:
                            act.wait_ge(qk_done, j - 1)
                        c = COLS[s.name + what.lower()] + n
                        if k == 1 and s.ctx:
                            dst, src = full[:, j % 2, 0:B * SP_], w[:, 0, 0:B * SP_]
                        else:
                            dst, src = full[:, j % 2, :], w[:, :, :]
                        act.activation(dst, src, ACT.Identity, bias=cols[:, c:c + 1])
                        rounded = half[:, j % 2, 0:dst.shape[-1]].bitcast(F32R)
                        act.activation(rounded, src, ACT.Identity, bias=cols[:, c:c + 1]).then_inc(work_free[it.slot], 1)
                        yield
                    it = s.items["T", n, 0]
                    w = filled(it)
                    if n or s.mrow0:
                        act.wait_ge(mrow_done, 16 * (s.mrow0 + n))
                    act.activation(mT[:, :], w[0:4, :, :], ACT.Copy).then_inc(work_free[it.slot], 1)
                    yield

                for _ in prepare(0):
                    pass
                for n in range(QUADS):
                    ahead = prepare(n + 1) if n + 1 < QUADS else iter(())
                    for u, (b, hp, kt) in enumerate(s.units):
                        g = s.unit0 + n * len(s.units) + u
                        q0 = kt * P if s.causal else 0
                        act.wait_ge(st_full, g + 1)
                        act.activation(prob[0:s.kw, g % 2, :, q0:T], st[0:s.kw, :, q0:T], ACT.Exp,
                                       scale=HS ** -0.5).then_inc(exp_done, 1)
                        if u < 2 and not s.ctx or u == 0:
                            next(ahead, None)
                            if s.ctx:
                                next(ahead, None)
                    for _ in ahead:
                        pass
                take_out(s.items["A", 0, 0])

            def exp_unit(s, n, g):
                act.wait_ge(st_full, count(s.unit0 + g + 1, n, s.g))
                act.activation(prob[0:s.kw, (s.unit0 + g) % 2, :, :], st[0:s.kw, :, :], ACT.Exp,
                               scale=HB ** -0.5).then_inc(exp_done, 1)

            def big(s):
                def prepare(n, buf, k):
                    it = s.prep(n, k)
                    w = filled(it)
                    if k < 2:
                        dst = q2 if k == 0 else k1
                        act.activation(dst[0:HB, buf, 0, :], w[0:HB, :, :], ACT.Copy).then_inc(hi_done, 1)
                        act.activation(dst[HB:P, buf, 1, :], w[HB:P, :, :], ACT.Copy).then_inc(hi_done, 1)
                    elif k == 2:
                        act.activation(vb[:, buf, :, :, 0:HB], w[:, :, :].rearrange("p b (t h d) -> p (b t) h d", h=2, d=HB),
                                       ACT.Copy).then_inc(work_free[it.slot], 1)
                    else:
                        act.activation(q2[HB:HB + 1, buf, 0, :], w[0:1, :, :], ACT.Copy)
                        act.activation(q2[0:1, buf, 1, :], w[HB:HB + 1, :, :], ACT.Copy).then_inc(work_free[it.slot], 1)

                for k in (0, 1, 2, s.T):
                    prepare((0, 0, None), 0, k)

                def body(n, buf, first, last):
                    nxt, prev, other = shift(n, 1), shift(n, -1), 1 - buf
                    with_unit = {0: 0, 2: 1, 4: 2}
                    for g in range(s.g):
                        exp_unit(s, n, g)
                        if g == 1 and not first:
                            take_out(s.fin(prev, 0))
                        if g in with_unit and not last:
                            prepare(nxt, other, with_unit[g])
                    if not last:
                        prepare(nxt, other, s.T)
                pair_steps(act, body)
                take_out(s.fin((PAIRS - 1, 0, None), 0))

            def cross(s):
                def prepare(n, buf, k):
                    it = s.prep(n, k)
                    w = filled(it)
                    if k == 0:
                        act.activation(kz[0:HB, 0, :], w[0:HB, 0, 0:B * SP_], ACT.Copy)
                        act.activation(kz[HB:P, 1, :], w[HB:P, 0, 0:B * SP_], ACT.Copy).then_inc(work_free[it.slot], 1)
                    elif k == 1:
                        act.activation(vb[0:S, buf, 0:B, :, 0:HB], w[0:S, :, 0:D].rearrange("p b (h d) -> p b h d", h=2),
                                       ACT.Copy).then_inc(work_free[it.slot], 1)
                    elif k == 2:
                        act.activation(g_hi, w[:, 0, 0:2 * B * SP_], ACT.Copy).then_inc(hi_done, 2)
                    else:
                        act.activation(mrow, w[0:HB + 1, :, :], ACT.Copy).then_inc(work_free[it.slot], 1)

                for k in (0, 1, 2, s.T):
                    prepare((0, 0, None), 0, k)

                def body(n, buf, first, last):
                    nxt, prev, other = shift(n, 1), shift(n, -1), 1 - buf
                    exp_unit(s, n, 0)
                    if not first:
                        take_out(s.fin(prev, 0))
                    if not last:
                        prepare(nxt, other, 0)
                    exp_unit(s, n, 1)
                    if not last:
                        prepare(nxt, other, 1)
                        prepare(nxt, other, 2)
                        prepare(nxt, other, s.T)
                pair_steps(act, body)
                take_out(s.fin((PAIRS - 1, 0, None), 0))

            def mlp(s):
                c = COLS[s.name]
                for f in range(FT):
                    it = s.gate(f)
                    w = filled(it)
                    if s.gated:
                        if f >= 2:
                            before = s.up(f - 2)
                            act.wait_ge(work_free[before.slot], before.free())
                        dst, b = gbuf[:, f % 2, :], c + FT + f
                    else:
                        dst, b = actT[:, f, :], c + f
                    act.activation(dst, w[:, :, :], ACT.Gelu, bias=cols[:, b:b + 1]).then_inc(work_free[it.slot], 1)

            norm_no = {s.name: i for i, s in enumerate([s for s in sections if isinstance(s, Norm) and s.name])}
            act.wait_ge(consts_loaded, 16 * 7)
            act.wait_ge(made, 23)
            for s in sections:
                if isinstance(s, Norm):
                    norm(s)
                if isinstance(s, Small):
                    small(s)
                if isinstance(s, Cross):
                    cross(s)
                elif isinstance(s, Big):
                    big(s)
                if isinstance(s, Mlp):
                    mlp(s)

        @block.vector
        def _(dve):
            steps = [0]

            def link(ins):
                steps[0] += 1
                ins.then_inc(vec, 1)
                dve.wait_ge(vec, steps[0])

            def filled(it):
                dve.wait_ge(work_full, it.full())
                return work[it.slot]

            def row(name, k=TILES):
                return rows[:, ROWV[name], :].unsqueeze(1).to_broadcast([P, k, D])

            def tiles(ap):
                return ap.rearrange("p b (t d) -> p (b t) d", d=D)

            def norm(s, add):
                if s.name:
                    src = x_res if s.src == "x" else att
                    for t in range(TILES):
                        ins = dve.bn_stats(stats[:, t, :], src[:, t, :])
                    link(ins)
                    for t in range(TILES):
                        ins = dve.bn_aggr(mv[:, t, :], stats[:, t, :])
                    ins.then_inc(var_done, 1)
                    dve.wait_ge(std_done, norm_no[s.name] + 1)
                    link(dve.reciprocal(rstd[:], std[:]))
                    for t in range(TILES):
                        ins = dve.tensor_scalar(z[:, t, :], src[:, t, :], mv[:, t, 0:1], rstd[:, t:t + 1],
                                                ALU.subtract, ALU.mult)
                        if t % QT == QT - 1:
                            ins.then_inc(z_done, 1)
                    dve.wait_ge(z_done, z_count[s.name] + 2)
                for what in add:
                    link(dve.tensor_tensor(x_res[:], x_res[:], att[:] if what == "att" else row(what), ALU.add))

            def add_out(it, into, name=None):
                w = filled(it)
                if into == "x":
                    ins = dve.tensor_tensor(x_res[:], x_res[:], tiles(w[:, :, :]), ALU.add)
                else:
                    ins = dve.tensor_tensor(att[:], tiles(w[:, :, :]), row(name), ALU.add)
                ins.then_inc(work_free[it.slot], 1)
                dve.wait_ge(work_free[it.slot], it.free())

            def small(s):
                link(dve.memset(vs[:], 1.0))
                it = s.items["V", 0, 0]
                w = filled(it)
                if s.ctx:
                    src = w[0:S, :, 0:D].rearrange("p b (h d) -> p b h d", d=HS)
                    for b in range(B):
                        ins = dve.tensor_tensor(vs[0:S, b, :, 0:HS], src[:, b], rows[0:S, ROWV[s.name + "v"], :].rearrange(
                            "p (h d) -> p h d", d=HS), ALU.add)
                else:
                    src = tiles(w[:, :, :])
                    for t in range(TILES):
                        ins = dve.tensor_tensor(vs[:, t, :, 0:HS], src[:, t, :].rearrange("p (h d) -> p h d", d=HS),
                                                rows[:, ROWV[s.name + "v"], :].rearrange("p (h d) -> p h d", d=HS), ALU.add)
                ins.then_inc(work_free[it.slot], 1)
                dve.wait_ge(work_free[it.slot], it.free())
                if s.masked:
                    kw = S if s.ctx else P
                    for t in range(B if s.ctx else TILES):
                        keep = ckeep if s.ctx else tkeep
                        ins = dve.tensor_scalar(vs[0:kw, t, :, :], vs[0:kw, t, :, :], keep[0:kw, t:t + 1], None, ALU.mult)
                    ins.then_inc(v_masked, 1)

                def prepare(n):
                    for k in range(2):
                        j = s.qk0 + 2 * n + k
                        w_ = N if k == 0 or not s.ctx else B * SP_
                        c = COLS["nselq" if k == 0 else "nselk"]
                        dst = (qs if k == 0 else ks)[:, n % 2, 0:w_]
                        it = s.items["QK"[k], n, 0]
                        dve.wait_ge(work_free[it.slot], it.free())
                        dve.scalar_tensor_tensor(dst, half[:, j % 2, 0:w_], cols[:, c:c + 1],
                                                 full[:, j % 2, 0:w_], ALU.mult, ALU.add).then_inc(qk_done, 1)
                        yield
                    for k, (b, hp, qt) in enumerate(s.m_list()):
                        it = s.items["M", n, k]
                        w = filled(it)
                        if s.ctx:
                            src = w[:, :, 0:QT * SP_].rearrange("p h (t c) -> p h t c", c=SP_)[:, :, :, 0:S]
                            dst = mneg[:, b * QT:(b + 1) * QT, 2 * hp:2 * hp + 2].rearrange("p t h -> p h t")
                        else:
                            src = w[:, :, 0:(qt + 1) * P]
                            dst = mneg[:, b * QT + qt, 2 * hp:2 * hp + 2]
                        dve.tensor_reduce(dst, src, AX.X, ALU.max, negate=True).then_inc(work_free[it.slot], 1)
                        yield

                def divide(n, b, hp):
                    dve.wait_ge(o_full, s.o0 + 4 * n + 2 * b + hp + 1)
                    o = oacc[:, hp, 0:2 * QT * (HS + 1)].rearrange("p (t h c) -> p t h c", t=QT, h=2)
                    link(dve.reciprocal(recip[:, hp, :, :], o[:, :, :, HS]))
                    c = (4 * n + 2 * hp) * HS
                    dst = on[:, b * QT:(b + 1) * QT, c:c + 2 * HS].rearrange("p t (h d) -> p t h d", h=2)
                    dve.tensor_tensor(dst, o[:, :, :, 0:HS], recip[:, hp, :, :].unsqueeze(3).to_broadcast([P, QT, 2, HS]),
                                      ALU.mult).then_inc(o_normed, 1)

                for _ in prepare(0):
                    pass
                for n in range(QUADS):
                    ahead = prepare(n + 1) if n + 1 < QUADS else iter(())
                    for u, (b, hp, kt) in enumerate(s.units):
                        if u and s.units[u - 1][2] == s.kt - 1:
                            divide(n, *s.units[u - 1][0:2])
                        for _ in range(2):
                            next(ahead, None)
                    divide(n, *s.units[-1][0:2])
                    for _ in ahead:
                        pass
                add_out(s.items["O", 0, 0], s.into, s.name + "o")

            def divide(s, steps0, n, b):
                dve.wait_ge(o_full, count(s.o0 + b + 1, n, 2))
                o = oacc[:, :, 0:QT * (HB + 1)].rearrange("p h (t c) -> p h t c", t=QT)
                r = recip[:].rearrange("p a t h -> p (a t h)")[:, 0:2 * QT].rearrange("p (h t) -> p h t", h=2)
                dve.reciprocal(r, o[:, :, :, HB]).then_inc(vec, 1)
                dve.wait_ge(vec, count(steps0 + b + 1, n, 2))
                for h in range(2):
                    ins = dve.tensor_tensor(on[:, b * QT:(b + 1) * QT, h * HB:(h + 1) * HB], o[:, h, :, 0:HB],
                                            r[:, h, :].unsqueeze(2).to_broadcast([P, QT, HB]), ALU.mult)
                ins.then_inc(o_normed, 1)

            def sum_out(s, n):
                it = s.fin(n, 1)
                w = filled(it)
                dve.tensor_tensor(x_res[:], x_res[:], tiles(w[:, :, :]), ALU.add).then_inc(work_free[it.slot], 1)
                dve.wait_ge(work_free[it.slot], it.free())

            def big(s):
                steps0 = steps[0]

                def prepare(n, buf, k):
                    it = s.prep(n, k)
                    if k < 2:
                        dve.wait_ge(hi_done, count(2 * (s.hi0 + k + 1), n, 4))
                        w = work[it.slot]
                        for h, r in ((0, slice(0, HB)), (1, slice(HB, P))):
                            other = slice(HB, P) if h == 0 else slice(0, HB)
                            if k == 0:
                                hi, lo = q2[r, buf, h, :], q1[other, buf, h, :]
                            else:
                                hi, lo = k1[r, buf, h, :], k2[r, buf, h, :]
                            dve.tensor_tensor(lo.rearrange("p (b c) -> p b c", b=2), w[r, :, :],
                                              hi.rearrange("p (b c) -> p b c", b=2).bitcast(F32), ALU.subtract)
                            ins = dve.tensor_copy(q1[r, buf, h, :] if k == 0 else k1[other, buf, h, :], hi)
                        ins.then_inc(work_free[it.slot], 1)
                    else:
                        w = filled(it)
                        dve.tensor_reduce(mneg[:, k - 3, 0:HB + 1:HB], w[:, :, :], AX.X, ALU.max,
                                          negate=True).then_inc(work_free[it.slot], 1)

                ms = list(range(3, 3 + s.ms))
                for k in [0, 1] + ms:
                    prepare((0, 0, None), 0, k)

                def body(n, buf, first, last):
                    nxt, prev, other = shift(n, 1), shift(n, -1), 1 - buf
                    if not last:
                        prepare(nxt, other, 0)
                        prepare(nxt, other, 1)
                    if not first:
                        sum_out(s, prev)
                    divide(s, steps0, n, 0)
                    if not last:
                        for k in ms:
                            prepare(nxt, other, k)
                    divide(s, steps0, n, 1)
                pair_steps(dve, body)
                steps[0] += 2 * PAIRS
                sum_out(s, (PAIRS - 1, 0, None))

            def cross(s):
                steps0 = steps[0]
                before = Item(s.item0 - 1)
                dve.wait_ge(work_free[before.slot], before.free())
                dve.tensor_tensor(h_lo, hT[:], h_hi.bitcast(F32), ALU.subtract).then_inc(h_split, 1)

                def prepare(n, k):
                    it = s.prep(n, k)
                    if k == 2:
                        dve.wait_ge(hi_done, count(2 * (s.hi0 + 1), n, 2))
                        w = work[it.slot]
                        dve.tensor_tensor(g_lo, w[:, 0, 0:2 * B * SP_], g_hi.bitcast(F32),
                                          ALU.subtract).then_inc(work_free[it.slot], 1)
                    else:
                        w = filled(it)
                        b = k - 3
                        src = w[:, :, 0:4 * SP_].rearrange("p a (t h c) -> p a t h c", t=2, h=2)[..., 0:S]
                        dst = mneg[:, b * QT:(b + 1) * QT, 0:HB + 1:HB].rearrange("p (a t) h -> p a t h", a=2)
                        dve.tensor_reduce(dst, src, AX.X, ALU.max, negate=True).then_inc(work_free[it.slot], 1)

                for k in (2, 3, 4):
                    prepare((0, 0, None), k)

                def body(n, buf, first, last):
                    nxt, prev = shift(n, 1), shift(n, -1)
                    if not last:
                        prepare(nxt, 2)
                    divide(s, steps0, n, 0)
                    if not last:
                        prepare(nxt, 3)
                        prepare(nxt, 4)
                    if not first:
                        sum_out(s, prev)
                    divide(s, steps0, n, 1)
                pair_steps(dve, body)
                steps[0] += 2 * PAIRS
                sum_out(s, (PAIRS - 1, 0, None))

            def mlp(s):
                if s.gated:
                    for f in range(FT):
                        it, g = s.up(f), s.gate(f)
                        w = filled(it)
                        dve.wait_ge(work_free[g.slot], g.free())
                        c = COLS[s.name] + f
                        dve.scalar_tensor_tensor(actT[:, f, :].rearrange("p (b c) -> p b c", b=2), w[:, :, :], cols[:, c:c + 1],
                                                 gbuf[:, f % 2, :].rearrange("p (b c) -> p b c", b=2), ALU.add,
                                                 ALU.mult).then_inc(work_free[it.slot], 1)
                add_out(s.out(), "x")

            norm_no = {s.name: i for i, s in enumerate([s for s in sections if isinstance(s, Norm) and s.name])}
            z_count, _ = counts(sections)
            dve.wait_ge(consts_loaded, 16 * 7)
            dve.tensor_scalar(tmask[:], tm8[:], -BIG, None, ALU.mult).then_inc(masks_made, 1)
            dve.tensor_scalar(cmask[:], cm8[:], -BIG, None, ALU.mult).then_inc(masks_made, 1)
            dve.tensor_scalar(tkeep[:], tc8[:], -1.0, 1.0, ALU.mult, ALU.add).then_inc(masks_made, 1)
            dve.tensor_scalar(ckeep[0:S, :], cc8[0:S, :], -1.0, 1.0, ALU.mult, ALU.add).then_inc(masks_made, 1)
            dve.wait_ge(masks_made, 4)
            dve.wait_ge(made, 23)
            dve.wait_ge(x_loaded, 16)
            adds = {"l0n1": ["l0sao"], "l0n2": ["l0cao"], "l0n3": ["l0b2"], "l1n": ["att", "l1b2"],
                    "l2n1": ["l2sao"], "l2n2": ["l2cao"], "l2n3": ["l2b2"],
                    "l3n1": ["l3sao"], "l3n2": ["l3cao"], "l3n3": ["l3b2"], None: []}
            for s in sections:
                if isinstance(s, Norm):
                    norm(s, adds[s.name])
                if isinstance(s, Small):
                    small(s)
                if isinstance(s, Cross):
                    cross(s)
                elif isinstance(s, Big):
                    big(s)
                if isinstance(s, Mlp):
                    mlp(s)


def counts(sections):
    z_count, v_count, z, v = {}, {}, 0, 0
    for s in sections:
        if isinstance(s, Norm) and s.name:
            z_count[s.name] = z
            z += 2
        if isinstance(s, Small):
            v += s.masked
            v_count[s.name] = v
    return z_count, v_count


def kernel(**a):
    import numpy as np
    import concourse.bacc as bacc
    from concourse import mybir as mb
    from concourse.bass_utils import run_bass_kernel_spmd as run

    f = {k: np.asarray(v) for k, v in a.items()}

    def norm_names(layer, i):
        return {"l0": ("L0_xattn_ln%d_w" % i, "L0_xattn_ln%d_b" % i), "l1": ("L1_xattn_ln_g", "L1_xattn_ln_b")}.get(
            layer, ("%s_xattn_ln%d_g" % (layer.upper(), i), "%s_xattn_ln%d_b" % (layer.upper(), i)))

    cols = np.zeros((P, NCOLS), np.float32)
    for name in LN_NAMES:
        g, b = norm_names(name[:2], int(name[3:] or 1))
        cols[:, COLS[name + "g"]] = f[g]
        cols[:, COLS[name + "b"]] = f[b]
    for name, src in (("l0m", "L0_xattn_mlp1_b"), ("l1m", "L1_xattn_b1"), ("l2m", "L2_xattn_ff_b1"), ("l3m", "L3_xattn_ff_b1")):
        v = f[src].reshape(-1, P).T
        cols[:, COLS[name]:COLS[name] + v.shape[1]] = v

    def blocks(w):
        out = np.zeros(w.shape[:-1] + (H, ROWS), np.float32)
        for r in range(3):
            out[..., r * HS:(r + 1) * HS] = w.reshape(w.shape[:-1] + (H, HS))
        return out.reshape(w.shape[:-1] + (H * ROWS,))

    def bias_cols(name, b, ones_row):
        v = blocks(b).reshape(H, ROWS)
        v[:, ones_row] = 1.0
        cols[:, COLS[name]:COLS[name] + QUADS] = v.reshape(QUADS, P).T

    l0 = "L0_xattn_"
    l1 = "L1_xattn_"
    qkv_w, qkv_b = f[l0 + "qkv_w"], f[l0 + "qkv_b"]
    small = {
        "l0sa": (qkv_w[:, 0:D], qkv_w[:, D:2 * D], qkv_w[:, 2 * D:], f[l0 + "proj_w"],
                 qkv_b[0:D], qkv_b[D:2 * D], qkv_b[2 * D:], f[l0 + "proj_b"]),
        "l0ca": tuple(f[l0 + n] for n in ("q_w", "k_w", "v_w", "out_w", "q_b", "k_b", "v_b", "out_b")),
        "l1ca": tuple(f[l1 + n] for n in ("Wq", "Wk", "Wv", "Wo", "bq", "bk", "bv", "bo")),
    }
    rows = np.zeros((P, len(ROW_NAMES), D), np.float32)
    wts = np.zeros((P, NWTS), np.float32)
    for name, (wq, wk, wv, wo, bq, bk, bv, bo) in small.items():
        bias_cols(name + "q", bq, ROW_MASK)
        bias_cols(name + "k", bk, ROW_MAX)
        rows[:, ROWV[name + "v"]] = bv
        rows[:, ROWV[name + "o"]] = bo
        for p, w in (("q", blocks(wq)), ("k", blocks(wk)), ("v", wv), ("o", wo)):
            wts[0:w.shape[0], WTS[name + p]:WTS[name + p] + w.shape[1]] = w
    for name, src in (("l2sao", "L2_xattn_sa_bo"), ("l2cao", "L2_xattn_ca_bo"), ("l3sao", "L3_xattn_a1_bo"),
                      ("l3cao", "L3_xattn_a2_bo"), ("l0b2", "L0_xattn_mlp2_b"), ("l1b2", "L1_xattn_b2"),
                      ("l2b2", "L2_xattn_ff_b2"), ("l3b2", "L3_xattn_ff_b2")):
        rows[:, ROWV[name]] = f[src]
    for name, w1, w2 in (("l0m", l0 + "mlp1_w", l0 + "mlp2_w"), ("l1m", l1 + "W1", l1 + "W2"),
                         ("l2m", "L2_xattn_ff_w1", "L2_xattn_ff_w2"), ("l3m", "L3_xattn_ff_w1", "L3_xattn_ff_w2")):
        w = f[w1]
        wts[:, WTS[name + "1"]:WTS[name + "1"] + w.shape[1]] = w
        w = f[w2].reshape(FT, P, D).transpose(1, 0, 2).reshape(P, F)
        wts[:, WTS[name + "2"]:WTS[name + "2"] + F] = w
    nsel = np.zeros((2, 4, ROWS), np.float32)
    nsel[0, :, 2 * HS:3 * HS] = -1.0
    nsel[1, :, HS:2 * HS] = -1.0
    cols[:, COLS["nselq"]] = nsel[0].reshape(-1)
    cols[:, COLS["nselk"]] = nsel[1].reshape(-1)

    ctxT = np.zeros((DC, B, SP_), np.float32)
    ctxT[:, :, 0:S] = f["ctx_768"].transpose(2, 0, 1)
    tm = f["mask_BxS_bf0"]
    cm = f["mask_BxS2_bf0"]
    cm_row = np.zeros((1, B, SP_), bool)
    cm_row[0, :, 0:S] = cm

    arrays = {
        "x_in": f["x"].reshape(N, D), "ctx_in": ctxT.reshape(DC, B * SP_),
        "tmask_row": tm.reshape(1, N), "tmask_col": np.ascontiguousarray(tm.reshape(TILES, P).T),
        "cmask_row": cm_row.reshape(1, B * SP_), "cmask_col": np.ascontiguousarray(cm.T),
        "cols_in": cols, "rows_in": rows, "wts_in": wts,
    }
    big_names = {"l2sa": "L2_xattn_sa_w", "l2ca": "L2_xattn_ca_w", "l3sa": "L3_xattn_a1_w", "l3ca": "L3_xattn_a2_w"}
    for n, src in big_names.items():
        for p in "qkvo":
            arrays[n + p] = f[src + p].T if n + p in ("l2caq", "l3caq") else f[src + p]
    nc = bacc.Bacc("TRN2", target_bir_lowering=False, num_devices=1)
    ap = {}
    for n, v in arrays.items():
        arrays[n] = np.ascontiguousarray(v)
        ap[n] = nc.dram_tensor(n, v.shape, mb.dt.from_np(v.dtype), kind="ExternalInput").ap()
    out = nc.dram_tensor("out", (N, D), mb.dt.float32, kind="ExternalOutput").ap()
    big = {n: tuple(ap[n + p] for p in "qkvo") for n in big_names}
    program(nc, ap["x_in"], ap["ctx_in"], ap["tmask_row"], ap["tmask_col"], ap["cmask_row"], ap["cmask_col"],
            ap["cols_in"], ap["rows_in"], ap["wts_in"], big, out)
    r = run(nc, [arrays], core_ids=[0])
    return r.results[0]["out"].reshape(B, T, D)
```

```python
from contextlib import ExitStack

import concourse.bass as bass
from concourse import mybir

F32 = mybir.dt.float32
F32R = mybir.dt.float32r
BF16 = mybir.dt.bfloat16
U8 = mybir.dt.uint8
ALU = mybir.AluOpType
ACT = mybir.ActivationFunctionType
AX = mybir.AxisListType

P = 128
B = 2
T = 512
D = 128
N = B * T
TILES = N // P
QT = T // P
S = 77
SP_ = 78
DC = 96
H = 16
HS = 8
HB = 64
F = 512
FT = F // P
QUADS = H // 4
PAIRS = H // 2
ROWS = 32
ROW_MAX = 24
ROW_MASK = 25
BIG = 1e30
EPS = 1e-5

LN_NAMES = ["l0n1", "l0n2", "l0n3", "l1n", "l2n1", "l2n2", "l2n3", "l3n1", "l3n2", "l3n3"]
COLS = {}
for _n in LN_NAMES:
    COLS[_n + "g"] = len(COLS)
    COLS[_n + "b"] = len(COLS)
_c = len(COLS)
for _n, _k in (("l0m", FT), ("l1m", FT), ("l2m", 2 * FT), ("l3m", 2 * FT),
               ("l0saq", QUADS), ("l0sak", QUADS), ("l0caq", QUADS), ("l0cak", QUADS),
               ("l1caq", QUADS), ("l1cak", QUADS), ("nselq", 1), ("nselk", 1)):
    COLS[_n] = _c
    _c += _k
NCOLS = _c
ROW_NAMES = ["l0sao", "l0cao", "l1cao", "l2sao", "l2cao", "l3sao", "l3cao",
             "l0b2", "l1b2", "l2b2", "l3b2", "l0sav", "l0cav", "l1cav"]
ROWV = {n: i for i, n in enumerate(ROW_NAMES)}
WTS = {}
_c = 0
LOADS = [("l0sa",), ("l0ca", "l0m"), ("l1ca", "l1m"), ("l2m",), ("l3m",)]
LOAD_AT = []
for _g in LOADS:
    LOAD_AT.append(_c)
    for _n in _g:
        if _n.endswith("a"):
            for _p, _k in (("q", QUADS * P), ("k", QUADS * P), ("v", D), ("o", D)):
                WTS[_n + _p] = _c
                _c += _k
        else:
            WTS[_n + "1"] = _c
            _c += F if _n in ("l0m", "l1m") else 2 * F
            WTS[_n + "2"] = _c
            _c += F
LOAD_AT.append(_c)
NWTS = _c


class Item:

    def __init__(self, c, n=None, per=0):
        a, m, self.i = n if n is not None else (0, 0, None)
        self.c, self.step = c + per * a, per * m
        assert self.step % 2 == 0

    def _value(self, c, step):
        return c if self.i is None else self.i * step + c

    @property
    def slot(self):
        return self.c % 2

    def full(self):
        return self._value(self.c + 1, self.step)

    def free(self):
        return self._value(self.c // 2 + 1, self.step // 2)

    def vacant(self):
        return self._value(self.c // 2, self.step // 2)

    def first(self):
        return self.i is None and self.c < 2


def count(c, n, per):
    a, m, i = n
    return c + per * a if i is None else i * (per * m) + (c + per * a)


class Small:

    def __init__(self, name, causal, ctx, masked, into, base):
        self.name, self.causal, self.ctx, self.masked, self.into = name, causal, ctx, masked, into
        self.kt = 1 if ctx else QT
        self.kw = S if ctx else P
        self.m_list = ([(b, tp, None) for b in range(B) for tp in range(2)] if ctx else
                       [(b, hp, qt) for b in range(B) for hp in range(2) for qt in range(QT)])
        self.units = [(b, kt, hp) for b in range(B) for kt in range(self.kt) for hp in range(2)]
        self.first = [("V", 0, 0), ("Q", 0, 0), ("K", 0, 0)] + [("M", 0, k) for k in range(len(self.m_list))] \
            + [("T", 0, 0), ("Q", 1, 0), ("K", 1, 0)]
        order = list(self.first)
        for n in range(QUADS):
            order += sum(self.with_units(n), [])
        order += [("N", QUADS - 1, 0), ("A", 0, 0), ("O", 0, 0)]
        self.items = {k: Item(base["item"] + i) for i, k in enumerate(order)}
        self.unit0, self.o0, self.qk0, self.mrow0 = base["unit"], base["o"], base["qk"], base["mrow"]
        base["item"] += len(order)
        base["unit"] += QUADS * len(self.units)
        base["o"] += QUADS * 2
        base["qk"] += QUADS * 2
        base["mrow"] += QUADS

    def with_units(self, n):
        sched = [[] for _ in self.units]
        m0, m1, t, q, k, o = (0,1,2,2,2,0) if self.ctx else (2,12,13,14,15,1)
        if n + 1 < QUADS:
            ms = len(self.m_list)
            for u in range(m0, m1 + 1):
                sched[u] += [("M", n + 1, i) for i in range(ms * (u - m0) // (m1 + 1 - m0), ms * (u + 1 - m0) // (m1 + 1 - m0))]
            sched[t].append(("T", n + 1, 0))
        if n:
            sched[o].append(("N", n - 1, 0))
        if n + 2 < QUADS:
            sched[q].append(("Q", n + 2, 0))
            sched[k].append(("K", n + 2, 0))
        return sched


class Big:

    ctx, kt, kw, g, ms = False, QT, P, B * QT, B * QT
    np = 3 + ms + 1
    PREP = [0, 1, 2, 3] + list(range(5, np + 1))
    OUT = 4
    LEAD = 1
    T = np - 1
    ADDS = B * (QT - 1)

    def __init__(self, name, base):
        self.name = name
        self.item0, self.unit0, self.o0 = base["item"], base["unit"], base["o"]
        self.hi0, self.w0, self.free_from = base["hi"], base["w"], base["big_end"]
        self.turn = self.np + 2
        self.turns0 = self.item0 + 2 * self.np + self.LEAD
        base["item"] = self.turns0 + self.turn * (PAIRS - 2) + 4 - self.LEAD
        base["big_end"] = base["item"] - 1
        self.add0 = base["add"]
        self.w0s = self.add0 // self.ADDS
        base["add"] += 0 if self.ctx else PAIRS * self.ADDS
        base["unit"] += PAIRS * self.g
        base["o"] += PAIRS * 2
        base["hi"] += PAIRS * (1 if self.ctx else 2)
        base["w"] += PAIRS

    def prep(self, n, k):
        if n in ((0, 0, None), (1, 0, None)):
            return Item(self.item0 + n[0] * self.np + k)
        return Item(self.turns0 - 2 * self.turn + self.PREP[k], n, self.turn)

    def fin(self, n, k):
        end = self.turns0 + self.turn * (PAIRS - 2)
        if n == (PAIRS - 1, 0, None):
            return Item(end + 1 + k)
        if k == 0:
            return Item(self.turns0 - 1, n, self.turn)
        return Item(end) if n == (PAIRS - 2, 0, None) else Item(self.turns0 + self.OUT, n, self.turn)

    def loaded(self, n, per):
        a, m, i = n
        c = per * ((self.w0 + a) // 2 + 1)
        return c if i is None else i * (per * m // 2) + c


class Cross(Big):

    ctx, kt, kw, g, ms = True, 1, S, B, B
    np = 6
    PREP = [1, 2, 3, 4, 5, 7]
    FIN = [0, 6]
    LEAD = 0
    T = 5

    def fin(self, n, k):
        if n in ((PAIRS - 2, 0, None), (PAIRS - 1, 0, None)):
            return Item(self.turns0 + self.turn * (PAIRS - 2) + 2 * (n[0] - PAIRS + 2) + k)
        return Item(self.turns0 + self.FIN[k], n, self.turn)


class Norm:

    def __init__(self, name, src, base, split=False):
        self.name, self.src, self.split = name, src, split
        self.item0 = base["item"]
        base["item"] += 2


class Mlp:
    def __init__(self, name, gated, base):
        self.name, self.gated = name, gated
        self.item0 = base["item"]
        self.per = 2 if gated else 1
        base["item"] += FT * self.per + 1

    def gate(self, f):
        return Item(self.item0 + f * self.per)

    def up(self, f):
        return Item(self.item0 + f * self.per + 1)

    def out(self):
        return Item(self.item0 + FT * self.per)


def plan():
    base = dict(item=0, unit=0, o=0, qk=0, mrow=0, hi=0, w=0, big_end=None, add=0)
    return [
        Norm("l0n1", "x", base), Small("l0sa", True, False, True, "x", base),
        Norm("l0n2", "x", base), Small("l0ca", False, True, True, "x", base),
        Norm("l0n3", "x", base), Mlp("l0m", False, base),
        Norm(None, "x", base), Small("l1ca", False, True, False, "att", base),
        Norm("l1n", "att", base), Mlp("l1m", False, base),
        Norm("l2n1", "x", base), Big("l2sa", base),
        Norm("l2n2", "x", base, True), Cross("l2ca", base),
        Norm("l2n3", "x", base), Mlp("l2m", True, base),
        Norm("l3n1", "x", base), Big("l3sa", base),
        Norm("l3n2", "x", base, True), Cross("l3ca", base),
        Norm("l3n3", "x", base), Mlp("l3m", True, base),
    ]


def pair_steps(eng, body):
    body((0, 0, None), 0, True, False)
    with eng.Fori(0, (PAIRS - 2) // 2) as i:
        body((1, 2, i), 1, False, False)
        body((2, 2, i), 0, False, False)
    body((PAIRS - 1, 0, None), (PAIRS - 1) % 2, False, True)


def shift(n, by):
    return (n[0] + by, n[1], n[2])


def program(nc, x_in, ctx_in, tmask_row, tmask_col, cmask_row, cmask_col, cols_in, rows_in, wts_in, big_in, out):
    sections = plan()
    with ExitStack() as ctx:
        def sb(name, shape, dt=F32):
            return ctx.enter_context(nc.sbuf_tensor(name, shape, dt))

        def sem(name):
            return ctx.enter_context(nc.semaphore(name))

        x_res = sb("x_res", [P, TILES, D])
        att = sb("att", [P, TILES, D])
        z = sb("z", [P, TILES, D])
        hT = sb("hT", [P, N])
        ctxT = sb("ctxT", [DC, B * SP_])
        cols = sb("cols", [P, NCOLS])
        rows = sb("rows", [P, len(ROW_NAMES), D])
        wts = sb("wts", [P, NWTS])
        ident = sb("ident", [P, P])
        ident_bf = sb("ident_bf", [P, P], BF16)
        after_q = sb("after_q", [P, P], BF16)
        after_k = sb("after_k", [P, P], BF16)
        mask_sel = sb("mask_sel", [1, P], BF16)
        tm8 = sb("tm8", [1, N], U8)
        tc8 = sb("tc8", [P, TILES], U8)
        cm8 = sb("cm8", [1, B * SP_], U8)
        cc8 = sb("cc8", [P, B], U8)
        tmask = sb("tmask", [1, N], BF16)
        cmask = sb("cmask", [1, B * SP_], BF16)
        tkeep = sb("tkeep", [P, TILES])
        ckeep = sb("ckeep", [P, B])
        stats = sb("stats", [P, TILES, 6])
        mv = sb("mv", [P, TILES, 2])
        std = sb("std", [P, TILES])
        rstd = sb("rstd", [P, TILES])
        shift_z = sb("shift_z", [P, TILES])
        q1 = sb("q1", [P, 2, 2, N], F32R)
        k1 = sb("k1", [P, 2, 2, N], F32R)
        with nc.sbuf_tensor("vs", [P, TILES, H, ROWS], F32) as vs:
            pass
        q2 = sb("q2", [P, 2, 2, N], F32R)
        k2 = sb("k2", [P, 2, 2, N], F32R)
        vb = sb("vb", [P, 2, TILES, 2, HB + 1])
        bigw = sb("bigw", [P, 2, 4, P])
        h_hi, h_lo = q1[:, 0, 0, :], q1[:, 0, 1, :]
        g_hi, g_lo = k1[:, 0, 0, 0:2 * B * SP_], k1[:, 0, 1, 0:2 * B * SP_]
        mrow = q1[0:HB + 1, 1, 0, :]
        kz = sb("kz", [P, 2, B * SP_])
        sel = sb("sel", [HB + 1, 2, SP_], F32R)
        full = sb("full", [P, 2, N])
        qs = sb("qs", [P, 2, N], F32R)
        ks = [q1[:].rearrange("p a h n -> p (a h) n"), k1[:].rearrange("p a h n -> p (a h) n")]
        mT = sb("mT", [4, N], F32R)
        mneg = sb("mneg", [P, TILES, HB + 2])
        prob = sb("prob", [P, 2, 2, T])
        vb_flat = vb[:].rearrange("p a t h c -> p (a t h c)")
        probs = [prob[:, 0], prob[:, 1]] + [vb_flat[:, i * 2 * T:(i + 1) * 2 * T].rearrange("p (h q) -> p h q", h=2)
                                            for i in range(2)]
        recip4 = sb("recip4", [P, TILES, 4])
        recip = sb("recip", [P, 2, QT, 2])
        on = z
        onT = sb("onT", [P, N])
        psum = full
        ones = sb("ones", [P, HB])
        den_c = sb("den_c", [P, N // 32])
        actT = sb("actT", [P, FT, N])
        half = actT
        gbuf = full
        den_t, den_r = actT[:, 0, :], actT[:, 1, :]
        raw = z[:].rearrange("p t d -> p (t d)")
        big_probs = [prob[:, 0], prob[:, 1]] + [actT[:, i, :].rearrange("p (h q) -> p h q", h=2) for i in (2, 3)]

        st = ctx.enter_context(nc.psum_tensor("st", [P, 2, 512], F32))
        oacc = ctx.enter_context(nc.psum_tensor("oacc", [P, 2, 512], F32))
        work = [ctx.enter_context(nc.psum_tensor(f"work{i}", [P, 2, 512], F32)) for i in range(2)]

        x_loaded = sem("x_loaded")
        consts_loaded = sem("consts_loaded")
        wts_loaded = [sem(f"wts_loaded{i}") for i in range(len(LOADS))]
        wqkv_loaded = [sem("wqkv_loaded0"), sem("wqkv_loaded1")]
        wo_loaded = [sem("wo_loaded0"), sem("wo_loaded1")]
        made = sem("made")
        masks_made = sem("masks_made")
        work_full = sem("work_full")
        work_free = [sem("work_free0"), sem("work_free1")]
        st_full = sem("st_full")
        exp_done = sem("exp_done")
        o_full = sem("o_full")
        o_taken = sem("o_taken")
        hi_done = sem("hi_done")
        big_ready = sem("big_ready")
        added = sem("added")
        scaled = sem("scaled")
        pool_gate = sem("pool_gate")
        act_gate = sem("act_gate")
        h_split = sem("h_split")
        qk_done = sem("qk_done")
        v_done = sem("v_done")
        mrow_done = sem("mrow_done")
        var_done = sem("var_done")
        std_done = sem("std_done")
        rstd_done = sem("rstd_done")
        z_done = sem("z_done")
        z_act = sem("z_act")
        vec = sem("vec")
        stored = sem("stored")

        WARM = 20
        MADE_FIRST, MADE = 13, 22
        ACT_TILES = (2, 3, 6, 7)
        small_end = [s for s in sections if isinstance(s, Small)][-1].items["O", 0, 0]

        block = ctx.enter_context(nc.Block())

        @block.sync
        def _(sp):
            sp.dma_start(x_res[:], x_in.rearrange("(t p) d -> p t d", p=P)).then_inc(x_loaded, 16)
            for dst, src in ((cols[:], cols_in), (rows[:], rows_in), (ctxT[:], ctx_in), (tm8[:], tmask_row),
                             (tc8[:], tmask_col), (cm8[:], cmask_row), (cc8[0:S, :], cmask_col)):
                sp.dma_start(dst, src).then_inc(consts_loaded, 16)
            for i in range(len(LOADS)):
                sp.dma_start(wts[:, LOAD_AT[i]:LOAD_AT[i + 1]],
                             wts_in[:, LOAD_AT[i]:LOAD_AT[i + 1]]).then_inc(wts_loaded[i], 16)

            def move_max_rows(s):
                for n in range(QUADS):
                    it = s.items["T", n, 0]
                    sp.wait_ge(work_free[it.slot], it.free())
                    sp.dma_start(qs[ROW_MAX:P:ROWS, n % 2, :].bitcast(F32), mT[:, :].bitcast(F32)).then_inc(mrow_done, 16)

            def load_pairs(s):
                wq, wk, wv, wo = big_in[s.name]
                kr = DC if s.ctx else D

                def load(n, buf, before):
                    at = n[0] * P if n[2] is None else n[2] * (n[1] * P) + n[0] * P
                    if before is not None:
                        sp.wait_ge(work_full, s.prep(before, s.T).full())
                    sp.dma_start(bigw[:, buf, 0, :], wq[bass.ds(at, P), :] if s.ctx else
                                 wq[:, bass.ds(at, P)]).then_inc(wqkv_loaded[buf], 16)
                    sp.dma_start(bigw[0:kr, buf, 1, :], wk[:, bass.ds(at, P)]).then_inc(wqkv_loaded[buf], 16)
                    sp.dma_start(bigw[0:kr, buf, 2, :], wv[:, bass.ds(at, P)]).then_inc(wqkv_loaded[buf], 16)
                    if before is not None:
                        sp.wait_ge(work_full, s.fin(before, 1).full())
                    sp.dma_start(bigw[:, buf, 3, :], wo[bass.ds(at, P), :]).then_inc(wo_loaded[buf], 16)

                if s.free_from is not None:
                    sp.wait_ge(work_full, Item(s.free_from).full())
                load((0, 0, None), 0, None)
                load((1, 0, None), 1, None)
                load((2, 0, None), 0, (0, 0, None))
                load((3, 0, None), 1, (1, 0, None))
                with sp.Fori(0, (PAIRS - 4) // 2) as i:
                    load((4, 2, i), 0, (2, 2, i))
                    load((5, 2, i), 1, (3, 2, i))

            for s in sections:
                if isinstance(s, Small):
                    move_max_rows(s)
                if isinstance(s, Big):
                    load_pairs(s)
            last = sections[-1].out()
            sp.wait_ge(work_free[last.slot], last.free())
            sp.dma_start(out.rearrange("(t p) d -> p t d", p=P), x_res[:]).then_inc(stored, 16)
            sp.wait_ge(stored, 16)

        @block.gpsimd
        def _(pool):
            pool.memset(ident[:], 0.0).then_inc(made, 1)
            pool.memset(ident_bf[:], 0.0).then_inc(made, 1)
            pool.memset(after_q[:], 0.0).then_inc(made, 1)
            pool.memset(after_k[:], 0.0).then_inc(made, 1)
            pool.memset(mask_sel[:], 0.0).then_inc(made, 1)
            pool.wait_ge(made, 5)
            for m in (ident, ident_bf):
                pool.affine_select(out=m[:], in_=m[:], compare_op=ALU.not_equal, fill=1.0, base=0,
                                   pattern=[[-1, P]], channel_multiplier=1).then_inc(made, 1)
            pool.affine_select(out=after_q[:], in_=after_q[:], compare_op=ALU.is_ge, fill=-BIG, base=0,
                               pattern=[[-1, P]], channel_multiplier=1).then_inc(made, 1)
            pool.affine_select(out=after_k[:], in_=after_k[:], compare_op=ALU.is_ge, fill=-BIG, base=0,
                               pattern=[[1, P]], channel_multiplier=-1).then_inc(made, 1)
            for j in range(4):
                pool.memset(mask_sel[0:1, ROWS * j + ROW_MASK:ROWS * j + ROW_MASK + 1], 1.0).then_inc(made, 1)
            pool.memset(q1[:].bitcast(F32), 0.0).then_inc(made, 1)
            pool.memset(k1[:].bitcast(F32), 0.0).then_inc(made, 1)
            pool.memset(vs[:], 0.0).then_inc(made, 1)
            pool.memset(mneg[:], 0.0).then_inc(made, 1)
            pool.memset(kz[:], 0.0).then_inc(made, 1)
            pool.memset(ones[:], 1.0).then_inc(made, 1)
            pool.memset(sel[:].bitcast(F32), 0.0).then_inc(made, 1)
            pool.wait_ge(made, MADE - 2)
            pool.memset(sel[0:1, 0, :].bitcast(F32), 1.0).then_inc(made, 1)
            pool.memset(sel[HB:HB + 1, 1, :].bitcast(F32), 1.0).then_inc(made, 1)
            pool.wait_ge(work_full, small_end.full())
            pool.memset(q2[:].bitcast(F32), 0.0).then_inc(big_ready, 1)
            pool.memset(k2[:].bitcast(F32), 0.0).then_inc(big_ready, 1)
            pool.memset(vb[:], 1.0).then_inc(big_ready, 1)
            pool.wait_ge(big_ready, 3)
            pool.memset(k2[HB:HB + 1, :, 0, :].bitcast(F32), 1.0).then_inc(big_ready, 1)
            pool.memset(k2[0:1, :, 1, :].bitcast(F32), 1.0).then_inc(big_ready, 1)

            def add_up(s):
                def body(n, buf, first, last):
                    if not first:
                        pool.wait_ge(work_full, s.fin(shift(n, -1), 0).full())
                        pool.sem_inc(pool_gate, 1)
                    for b in range(B):
                        for kt in range(1, QT):
                            g, step = b * QT + kt, b * (QT - 1) + kt
                            pool.wait_ge(exp_done, count(2 * (s.unit0 + g + 1), n, 2 * s.g))
                            pool.sem_inc(pool_gate, 1)
                            total = psum[:, b, :].rearrange("p (h q) -> p h q", h=2)
                            one = big_probs[(g - 1) % 4] if kt == 1 else total
                            if kt > 1:
                                pool.wait_ge(added, count(s.add0 + step - 1, n, s.ADDS))
                                pool.sem_inc(pool_gate, 1)
                            pool.tensor_tensor(total, one, big_probs[g % 4], ALU.add).then_inc(added, 1)
                pair_steps(pool, body)

            for s in sections:
                if isinstance(s, Big) and not s.ctx:
                    add_up(s)

        @block.tensor
        def _(pe):
            def open_item(it):
                if not it.first():
                    pe.wait_ge(work_free[it.slot], it.vacant())
                return work[it.slot]

            def taken(it):
                pe.wait_ge(work_free[it.slot], it.free())

            def stay_warm(w, times):
                for _ in range(times):
                    pe.matmul(w[:, 0, :], ident_bf[:], after_q[:].unsqueeze(1).to_broadcast([P, QT, P]),
                              start=True, stop=True, skip_group_check=True)

            def norm(s):
                for k in range(2):
                    if s.name and k == 0 and s is not sections[0]:
                        stay_warm(open_item(Item(s.item0)), WARM)
                    if s.name:
                        pe.wait_ge(z_done, z_count[s.name] + k + 1)
                        pe.wait_ge(z_act, z_count[s.name] + k + 1)
                        src = z
                    else:
                        if k == 0:
                            taken(x_item[0])
                        src = x_res
                    it = Item(s.item0 + k)
                    w = open_item(it)
                    for t in range(QT):
                        mm = pe.transpose(w[:, 0, t * P:(t + 1) * P], src[:, k * QT + t, :], ident[:])
                    mm.then_inc(work_full, 1)

            def need_h(b):
                if h_item[b] is not None:
                    taken(h_item[b])
                    h_item[b] = None

            def both_halves(w, lhsT, rhs, then=None):
                for b in range(B):
                    need_h(b)
                    mm = pe.matmul(w[:, b, :], lhsT, rhs[:, b * T:(b + 1) * T], start=True, stop=then is None)
                    if then is not None:
                        mm = then(b)
                return mm

            def transpose_out(it):
                w = open_item(it)
                for t in range(TILES):
                    mm = pe.transpose(w[:, t // QT, (t % QT) * P:(t % QT + 1) * P], on[:, t, :], ident[:])
                mm.then_inc(work_full, 1)

            def project_out(it, before, wo):
                w = open_item(it)
                if before.slot != it.slot:
                    taken(before)
                for t in range(TILES):
                    mm = pe.matmul(w[:, t // QT, (t % QT) * P:(t % QT + 1) * P], onT[:, t * P:(t + 1) * P],
                                   wo, start=True, stop=True)
                mm.then_inc(work_full, 1)

            def values(it, wv, ctx_side):
                w = open_item(it)
                if ctx_side:
                    for b in range(B):
                        mm = pe.matmul(w[0:S, b, 0:D], ctxT[:, b * SP_:b * SP_ + S], wv, start=True, stop=True)
                else:
                    for t in range(TILES):
                        need_h(t // QT)
                        mm = pe.matmul(w[:, t // QT, (t % QT) * P:(t % QT + 1) * P], hT[:, t * P:(t + 1) * P],
                                       wv, start=True, stop=True)
                mm.then_inc(work_full, 1)

            def small(s):
                kr = DC if s.ctx else D
                wv = wts[0:kr, WTS[s.name + "v"]:WTS[s.name + "v"] + D]

                def prepare(item):
                    what, n, k = item
                    it, buf = s.items[item], n % 2
                    if what == "Q":
                        w = open_item(it)
                        mm = both_halves(w, wts[:, WTS[s.name + "q"] + n * P:WTS[s.name + "q"] + (n + 1) * P], hT)
                    elif what == "K":
                        w = open_item(it)
                        wk = wts[0:kr, WTS[s.name + "k"] + n * P:WTS[s.name + "k"] + (n + 1) * P]
                        if s.ctx:
                            mm = pe.matmul(w[:, 0, 0:B * SP_], wk, ctxT[:], start=True, stop=not s.masked)
                            if s.masked:
                                mm = pe.matmul(w[:, 0, 0:B * SP_], mask_sel[:], cmask[:], start=False, stop=True)
                        else:
                            mm = both_halves(w, wk, hT, lambda b: pe.matmul(
                                w[:, b, :], mask_sel[:], tmask[:, b * T:(b + 1) * T], start=False, stop=True))
                    elif what == "M":
                        if k == 0:
                            pe.wait_ge(qk_done, s.qk0 + 2 * n + 2)
                        w = open_item(it)
                        b, part, qt = s.m_list[k]
                        if s.ctx:
                            for i in range(2):
                                q0 = b * T + (2 * part + i) * P
                                mm = pe.matmul(w[:, i, 0:4 * SP_], qs[:, buf, q0:q0 + P],
                                               ks[buf][:, :, b * SP_:(b + 1) * SP_], start=True, stop=True)
                        else:
                            keys, q0 = (qt + 1) * P, b * T + qt * P
                            for hh in range(2):
                                pe.matmul(w[:, hh, 0:keys], qs[:, buf, q0:q0 + P],
                                          ks[buf][:, 2 * part + hh, b * T:b * T + keys], start=True, stop=False,
                                          skip_group_check=True)
                                mm = pe.matmul(w[:, hh, qt * P:keys], ident_bf[:], after_q[:], start=False, stop=True,
                                               skip_group_check=True)
                    elif what == "N":
                        w = open_item(it)
                        pe.wait_ge(o_taken, s.o0 + 2 * n + 2)
                        for t in range(TILES):
                            mm = pe.transpose(w[:, t // QT, (t % QT) * P:(t % QT + 1) * P], onT[:, t * P:(t + 1) * P],
                                              ident[:])
                    else:
                        for k in (1, 2):
                            taken(s.items["M", n, len(s.m_list) - k])
                        w = open_item(it)
                        for t in range(TILES):
                            mm = pe.transpose(w[0:4, t // QT, (t % QT) * P:(t % QT + 1) * P], mneg[:, t, 0:4], ident[:])
                    mm.then_inc(work_full, 1)

                def scores(n, u):
                    b, kt, hp = s.units[u]
                    buf, g = n % 2, s.unit0 + n * len(s.units) + u
                    if u == 0:
                        pe.wait_ge(mrow_done, 16 * (s.mrow0 + n + 1))
                    q0 = kt * P if s.causal else 0
                    kc = (b * T + kt * P) if not s.ctx else b * SP_
                    for hh in range(2):
                        if g:
                            pe.wait_ge(exp_done, 2 * g + hh - 1)
                        mm = pe.matmul(st[0:s.kw, hh, q0:T], ks[buf][:, 2 * hp + hh, kc:kc + s.kw],
                                       qs[:, buf, b * T + q0:(b + 1) * T], start=True, stop=not s.causal,
                                       skip_group_check=True)
                        if s.causal:
                            mm = pe.matmul(st[:, hh, q0:q0 + P], ident_bf[:], after_k[:], start=False, stop=True,
                                           skip_group_check=True)
                        mm.then_inc(st_full, 1)

                def weigh_small(n, pair):
                    b, kt, _ = s.units[2 * pair]
                    g = s.unit0 + n * len(s.units) + 2 * pair
                    o = s.o0 + 2 * n + b
                    t = (b * QT + kt) if not s.ctx else b
                    pe.wait_ge(exp_done, 2 * (g + 2))
                    if kt == 0 and o >= 2:
                        pe.wait_ge(o_taken, o - 1)
                    q0 = kt * P if s.causal else 0
                    for j in range(4):
                        mm = pe.matmul(oacc[j * ROWS:(j + 1) * ROWS, b, q0:T], vs[0:s.kw, t, 4 * n + j, :],
                                       probs[(g + j // 2) % 4][0:s.kw, j % 2, q0:T],
                                       start=(kt == 0), stop=(kt == s.kt - 1), skip_group_check=True,
                                       tile_position=(0, j * ROWS))
                    if kt == s.kt - 1:
                        mm.then_inc(o_full, 1)

                values(s.items["V", 0, 0], wv, s.ctx)
                for item in s.first[1:]:
                    prepare(item)
                taken(s.items["V", 0, 0])
                if s.masked:
                    pe.wait_ge(v_done, v_count[s.name])
                for n in range(QUADS):
                    for u, items in enumerate(s.with_units(n)):
                        scores(n, u)
                        for item in items:
                            prepare(item)
                        if u and u % 2 == 0:
                            weigh_small(n, u // 2 - 1)
                    weigh_small(n, len(s.units) // 2 - 1)
                prepare(("N", QUADS - 1, 0))
                taken(s.items["N", QUADS - 1, 0])
                transpose_out(s.items["A", 0, 0])
                project_out(s.items["O", 0, 0], s.items["A", 0, 0], wts[:, WTS[s.name + "o"]:WTS[s.name + "o"] + D])

            def weigh(s, n, buf, g):
                b, kt = divmod(g, s.kt)
                pe.wait_ge(exp_done, count(2 * (s.unit0 + g + 1), n, 2 * s.g))
                if kt == 0:
                    pe.wait_ge(o_taken, count(s.o0 + b, n, 2))
                slot = (s.unit0 + g) % 2
                for h in range(2):
                    for t in range(QT):
                        mm = pe.matmul(oacc[:, h, t * (HB + 1):(t + 1) * (HB + 1)],
                                       prob[0:s.kw, slot, h, t * P:(t + 1) * P],
                                       vb[0:s.kw, buf, (b * QT + kt) if not s.ctx else b, h, :],
                                       start=(kt == 0 and t == 0), stop=(kt == s.kt - 1), skip_group_check=True)
                if kt == s.kt - 1:
                    mm.then_inc(o_full, 1)

            def weigh_self(s, n, buf, g):
                b, kt = divmod(g, s.kt)
                pe.wait_ge(exp_done, count(2 * (s.unit0 + g + 1), n, 2 * s.g))
                if kt == 0:
                    pe.wait_ge(o_taken, count(s.o0 + b - 1, n, 2))
                for h in range(2):
                    mm = pe.matmul(oacc[h * HB:(h + 1) * HB, b, :], vb[:, buf, b * QT + kt, h, 0:HB], big_probs[g % 4][:, h, :],
                                   start=(kt == 0), stop=(kt == s.kt - 1), skip_group_check=True, tile_position=(0, h * HB))
                if kt == s.kt - 1:
                    mm.then_inc(o_full, 1)

            def finish(s, n, buf, k):
                if k == 0 and not s.ctx:
                    pe.wait_ge(added, count(s.add0 + s.ADDS, n, s.ADDS))
                    w = open_item(s.fin(n, 0))
                    for b in range(B):
                        for h in range(2):
                            mm = pe.matmul(w[h * HB:(h + 1) * HB, b, :], ones[:], psum[:, b, h * T:(h + 1) * T],
                                           start=True, stop=True, skip_group_check=True, tile_position=(0, h * HB))
                    mm.then_inc(work_full, 1)
                elif k == 0:
                    pe.wait_ge(o_taken, count(s.o0 + 2, n, 2))
                    transpose_out(s.fin(n, 0))
                else:
                    pe.wait_ge(wo_loaded[buf], s.loaded(n, 16))
                    if not s.ctx:
                        pe.wait_ge(scaled, count(s.w0s + 1, n, 1))
                    project_out(s.fin(n, 1), s.fin(n, 0), bigw[:, buf, 3, :])

            def max_rows(s, n):
                taken(s.prep(n, s.T - 1))
                taken(s.prep(n, s.T - 2))
                w = open_item(s.prep(n, s.T))
                for t in range(TILES):
                    mm = pe.transpose(w[0:HB + 1, t // QT, (t % QT) * P:(t % QT + 1) * P], mneg[:, t, 0:HB + 1], ident[:])
                mm.then_inc(work_full, 1)

            def big(s):
                def prepare(n, buf, k):
                    wq, wk, wv = bigw[:, buf, 0, :], bigw[:, buf, 1, :], bigw[:, buf, 2, :]
                    it = s.prep(n, k)
                    if k == s.T:
                        max_rows(s, n)
                        return
                    if k == 0:
                        pe.wait_ge(wqkv_loaded[buf], s.loaded(n, 48))
                    if k == 2:
                        values(it, wv, False)
                        return
                    w = open_item(it)
                    if k < 2:
                        mm = both_halves(w, wq if k == 0 else wk, hT)
                    else:
                        if k == 3:
                            taken(s.prep(n, 1))
                            if s.prep(n, 0).slot != s.prep(n, 1).slot:
                                taken(s.prep(n, 0))
                        b, t = divmod(k - 3, QT)
                        q0 = b * T + t * P
                        for h in range(2):
                            mm = pe.matmul(w[:, h, :], q1[:, buf, h, q0:q0 + P],
                                           k1[:, buf, h, b * T:(b + 1) * T], start=True, stop=True)
                    mm.then_inc(work_full, 1)

                def scores(n, buf, g):
                    b, kt = divmod(g, s.kt)
                    if g == 0:
                        taken(s.prep(n, s.T))
                    kc = b * T + kt * P
                    for h in range(2):
                        pe.wait_ge(exp_done, count(2 * (s.unit0 + g) + h - 1, n, 2 * s.g))
                        pe.matmul(st[:, h, :], k1[:, buf, h, kc:kc + P], q1[:, buf, h, b * T:(b + 1) * T],
                                  start=True, stop=False)
                        mm = pe.matmul(st[:, h, :], k2[:, buf, h, kc:kc + P], q2[:, buf, h, b * T:(b + 1) * T],
                                       start=False, stop=True)
                        mm.then_inc(st_full, 1)

                def body(n, buf, first, last):
                    nxt, prev, other = shift(n, 1), shift(n, -1), 1 - buf
                    with_unit = [[0], [1], [2], [3, "O"], [4], [5, 6], [7, 8], [9, 10]]
                    for g in range(s.g):
                        scores(n, buf, g)
                        if g and g < s.g - 1:
                            weigh_self(s, n, buf, g - 1)
                        for k in with_unit[g]:
                            if k == "O":
                                if not first:
                                    finish(s, prev, other, 1)
                            elif not last:
                                prepare(nxt, other, k)
                    weigh_self(s, n, buf, s.g - 2)
                    if not last:
                        prepare(nxt, other, s.T)
                    weigh_self(s, n, buf, s.g - 1)
                    finish(s, n, buf, 0)

                pe.wait_ge(big_ready, 5)
                for k in range(s.np):
                    prepare((0, 0, None), 0, k)
                pair_steps(pe, body)
                finish(s, (PAIRS - 1, 0, None), 1, 1)

            def cross(s):
                def prepare(n, buf, k):
                    it = s.prep(n, k)
                    if k == 0:
                        pe.wait_ge(wqkv_loaded[buf], s.loaded(n, 48))
                        w = open_item(it)
                        mm = pe.matmul(w[:, 0, 0:B * SP_], bigw[0:DC, buf, 1, :], ctxT[:], start=True, stop=True)
                    elif k == 1:
                        values(it, bigw[0:DC, buf, 2, :], True)
                        return
                    elif k == 2:
                        taken(s.prep(n, 0))
                        w = open_item(it)
                        mm = pe.matmul(w[:, 0, 0:2 * B * SP_], bigw[:, buf, 0, :], kz[:].rearrange("p h c -> p (h c)"),
                                       start=True, stop=True)
                    elif k < s.T:
                        b = k - 3
                        w = open_item(it)
                        need_h(b)
                        if b == 0:
                            taken(s.prep(n, 2))
                        for t in range(QT):
                            q0 = b * T + t * P
                            mm = pe.matmul(w[:, t // 2, (t % 2) * 2 * SP_:(t % 2 + 1) * 2 * SP_], h_hi[:, q0:q0 + P],
                                           g_hi.rearrange("p (h b c) -> p b h c", h=2, b=B)[:, b], start=True, stop=True)
                    else:
                        max_rows(s, n)
                        return
                    mm.then_inc(work_full, 1)

                def scores(n, b):
                    if b == 0:
                        taken(s.prep(n, s.T))
                    q = slice(b * T, (b + 1) * T)
                    for h in range(2):
                        pe.wait_ge(exp_done, count(2 * (s.unit0 + b) + h - 1, n, 2 * s.g))
                        c = slice((h * B + b) * SP_, (h * B + b) * SP_ + S)
                        passes = [(g_hi[:, c], h_hi[:, q]), (g_hi[:, c], h_lo[:, q]), (g_lo[:, c], h_hi[:, q]),
                                  (sel[:, h, 0:S], mrow[:, q])]
                        for i, (keys, queries) in enumerate(passes):
                            mm = pe.matmul(st[0:S, h, :], keys, queries, start=(i == 0), stop=(i == len(passes) - 1))
                        mm.then_inc(st_full, 1)

                def body(n, buf, first, last):
                    nxt, prev, other = shift(n, 1), shift(n, -1), 1 - buf
                    scores(n, 0)
                    if not first:
                        finish(s, prev, other, 0)
                    if not last:
                        prepare(nxt, other, 0)
                    scores(n, 1)
                    if not last:
                        prepare(nxt, other, 1)
                        prepare(nxt, other, 2)
                    weigh(s, n, buf, 0)
                    if not last:
                        prepare(nxt, other, 3)
                        prepare(nxt, other, 4)
                    if not first:
                        finish(s, prev, other, 1)
                    if not last:
                        prepare(nxt, other, s.T)
                    weigh(s, n, buf, 1)

                for k in range(s.np):
                    prepare((0, 0, None), 0, k)
                pe.wait_ge(h_split, 1 if s.name == "l2ca" else 2)
                pair_steps(pe, body)
                finish(s, (PAIRS - 1, 0, None), 1, 0)
                finish(s, (PAIRS - 1, 0, None), 1, 1)

            def mlp(s):
                w1, w2 = WTS[s.name + "1"], WTS[s.name + "2"]
                for f in range(FT):
                    if s.gated:
                        w = open_item(s.gate(f))
                        both_halves(w, wts[:, w1 + F + f * P:w1 + F + (f + 1) * P], hT).then_inc(work_full, 1)
                        w = open_item(s.up(f))
                        both_halves(w, wts[:, w1 + f * P:w1 + (f + 1) * P], hT).then_inc(work_full, 1)
                    else:
                        w = open_item(s.gate(f))
                        both_halves(w, wts[:, w1 + f * P:w1 + (f + 1) * P], hT).then_inc(work_full, 1)
                w = open_item(s.out())
                for f in range(FT):
                    taken(s.up(f) if s.gated else s.gate(f))
                for t in range(TILES):
                    for f in range(FT):
                        mm = pe.matmul(w[:, t // QT, (t % QT) * P:(t % QT + 1) * P], actT[:, f, t * P:(t + 1) * P],
                                       wts[:, w2 + f * P:w2 + (f + 1) * P], start=(f == 0), stop=(f == FT - 1))
                mm.then_inc(work_full, 1)

            pe.wait_ge(made, MADE_FIRST)
            z_count, v_count = counts(sections)
            x_item, h_item = [None], [None, None]
            for s in sections:
                for i, g in enumerate(LOADS):
                    if s.name in g:
                        pe.wait_ge(wts_loaded[i], 16)
                if isinstance(s, Norm):
                    norm(s)
                    if s is sections[0]:
                        pe.wait_ge(masks_made, 4)
                        pe.wait_ge(consts_loaded, 16 * 7)
                    h_item[0], h_item[1] = Item(s.item0), Item(s.item0 + 1)
                if isinstance(s, Small):
                    small(s)
                if isinstance(s, Cross):
                    cross(s)
                elif isinstance(s, Big):
                    big(s)
                if isinstance(s, Mlp):
                    mlp(s)
                    x_item[0] = s.out()

        @block.scalar
        def _(act):
            def filled(it):
                act.wait_ge(work_full, it.full())
                return work[it.slot]

            def norm(s):
                if s.name:
                    act.wait_ge(var_done, norm_no[s.name] + 1)
                    act.activation(std[:], mv[:, :, 1], ACT.Sqrt, bias=EPS).then_inc(std_done, 1)
                    act.wait_ge(rstd_done, norm_no[s.name] + 1)
                    src = x_res if s.src == "x" else att
                    for t in ACT_TILES:
                        ins = act.activation(z[:, t, :], src[:, t, :], ACT.Identity, bias=shift_z[:, t:t + 1],
                                             scale=rstd[:, t:t + 1])
                        if t % QT == QT - 1:
                            ins.then_inc(z_act, 1)
                if s is sections[0]:
                    act.wait_ge(consts_loaded, 16 * 7)
                for k in range(2):
                    it = Item(s.item0 + k)
                    w = filled(it)
                    dst = hT[:, k * T:(k + 1) * T]
                    if s.name:
                        g, b = COLS[s.name + "g"], COLS[s.name + "b"]
                        ins = act.activation(dst, w[:, 0, :], ACT.Identity, bias=cols[:, b:b + 1], scale=cols[:, g:g + 1])
                        if s.split:
                            ins = act.activation(h_hi[:, k * T:(k + 1) * T], w[:, 0, :], ACT.Identity,
                                                 bias=cols[:, b:b + 1], scale=cols[:, g:g + 1])
                    else:
                        ins = act.activation(dst, w[:, 0, :], ACT.Copy)
                    ins.then_inc(work_free[it.slot], 1)

            def take_out(it):
                w = filled(it)
                act.activation(onT[:], w[:, :, :], ACT.Copy).then_inc(work_free[it.slot], 1)

            def small(s):
                def prepare(item):
                    what, n, _ = item
                    it = s.items[item]
                    if what in "QK":
                        k = "QK".index(what)
                        j = s.qk0 + 2 * n + k
                        w = filled(it)
                        if j >= 2:
                            act.wait_ge(qk_done, j - 1)
                        c = COLS[s.name + what.lower()] + n
                        if k == 1 and s.ctx:
                            dst, src = full[:, j % 2, 0:B * SP_], w[:, 0, 0:B * SP_]
                        else:
                            dst, src = full[:, j % 2, :], w[:, :, :]
                        act.activation(dst, src, ACT.Identity, bias=cols[:, c:c + 1])
                        rounded = half[:, j % 2, 0:dst.shape[-1]].bitcast(F32R)
                        act.activation(rounded, src, ACT.Identity, bias=cols[:, c:c + 1]).then_inc(work_free[it.slot], 1)
                    elif what == "T":
                        w = filled(it)
                        if n or s.mrow0:
                            act.wait_ge(mrow_done, 16 * (s.mrow0 + n))
                        act.activation(mT[:, :], w[0:4, :, :], ACT.Copy).then_inc(work_free[it.slot], 1)

                def take(n, b):
                    act.wait_ge(o_full, s.o0 + 2 * n + b + 1)
                    act.activation(onT[:, b * T:(b + 1) * T], oacc[:, b, :], ACT.Copy).then_inc(o_taken, 1)

                for item in s.first:
                    prepare(item)
                for n in range(QUADS):
                    for u, items in enumerate(s.with_units(n)):
                        b, kt, hp = s.units[u]
                        g = s.unit0 + n * len(s.units) + u
                        q0 = kt * P if s.causal else 0
                        for hh in range(2):
                            act.wait_ge(st_full, 2 * g + hh + 1)
                            act.activation(probs[g % 4][0:s.kw, hh, q0:T], st[0:s.kw, hh, q0:T], ACT.Exp,
                                           scale=HS ** -0.5).then_inc(exp_done, 1)
                        for item in items:
                            prepare(item)
                        if u == s.kt * 2 + (0 if s.ctx else 1):
                            take(n, 0)
                    take(n, 1)
                take_out(s.items["A", 0, 0])

            def exp_unit(s, n, g):
                for h in range(2):
                    act.wait_ge(st_full, count(2 * (s.unit0 + g) + h + 1, n, 2 * s.g))
                    act.activation(big_probs[(s.unit0 + g) % (2 if s.ctx else 4)][0:s.kw, h, :], st[0:s.kw, h, :], ACT.Exp,
                                   scale=HB ** -0.5).then_inc(exp_done, 1)

            def take(s, n, b):
                act.wait_ge(o_full, count(s.o0 + b + 1, n, 2))
                act.activation(raw[:, b * T:(b + 1) * T], oacc[:, b, :], ACT.Copy).then_inc(o_taken, 1)

            def big(s):
                def prepare(n, buf, k):
                    it = s.prep(n, k)
                    w = filled(it)
                    if k < 2:
                        dst = q2 if k == 0 else k1
                        act.activation(dst[0:HB, buf, 0, :], w[0:HB, :, :], ACT.Copy).then_inc(hi_done, 1)
                        act.activation(dst[HB:P, buf, 1, :], w[HB:P, :, :], ACT.Copy).then_inc(hi_done, 1)
                    elif k == 2:
                        act.activation(vb[:, buf, :, :, 0:HB], w[:, :, :].rearrange("p b (t h d) -> p (b t) h d", h=2, d=HB),
                                       ACT.Copy).then_inc(work_free[it.slot], 1)
                    else:
                        act.activation(q2[HB:HB + 1, buf, 0, :], w[0:1, :, :], ACT.Copy)
                        act.activation(q2[0:1, buf, 1, :], w[HB:HB + 1, :, :], ACT.Copy).then_inc(work_free[it.slot], 1)

                act.wait_ge(big_ready, 5)
                for k in (0, 1, 2, s.T):
                    prepare((0, 0, None), 0, k)

                def body(n, buf, first, last):
                    nxt, prev, other = shift(n, 1), shift(n, -1), 1 - buf
                    with_unit = {0: 0, 1: 1, 2: 2}
                    for g in range(s.g):
                        b, kt = divmod(g, QT)
                        if b or not first:
                            step = max(kt, 1) if b else max(kt, 1) + QT - 1 - s.ADDS
                            act.wait_ge(added, count(s.add0 + step, n, s.ADDS))
                            act.sem_inc(act_gate, 1)
                        exp_unit(s, n, g)
                        if g == QT + 1:
                            if not first:
                                act.wait_ge(scaled, count(s.w0s, n, 1))
                                act.sem_inc(act_gate, 1)
                            take(s, n, 0)
                        if g in with_unit and not last:
                            prepare(nxt, other, with_unit[g])
                    if not last:
                        prepare(nxt, other, s.T)
                    take(s, n, 1)
                pair_steps(act, body)

            def cross(s):
                def prepare(n, buf, k):
                    it = s.prep(n, k)
                    w = filled(it)
                    if k == 0:
                        act.activation(kz[0:HB, 0, :], w[0:HB, 0, 0:B * SP_], ACT.Copy)
                        act.activation(kz[HB:P, 1, :], w[HB:P, 0, 0:B * SP_], ACT.Copy).then_inc(work_free[it.slot], 1)
                    elif k == 1:
                        act.activation(vb[0:S, buf, 0:B, :, 0:HB], w[0:S, :, 0:D].rearrange("p b (h d) -> p b h d", h=2),
                                       ACT.Copy).then_inc(work_free[it.slot], 1)
                    elif k == 2:
                        act.activation(g_hi, w[:, 0, 0:2 * B * SP_], ACT.Copy).then_inc(hi_done, 2)
                    else:
                        act.activation(mrow, w[0:HB + 1, :, :], ACT.Copy).then_inc(work_free[it.slot], 1)

                for k in (0, 1, 2, s.T):
                    prepare((0, 0, None), 0, k)

                def body(n, buf, first, last):
                    nxt, prev, other = shift(n, 1), shift(n, -1), 1 - buf
                    exp_unit(s, n, 0)
                    if not first:
                        take_out(s.fin(prev, 0))
                    if not last:
                        prepare(nxt, other, 0)
                    exp_unit(s, n, 1)
                    if not last:
                        prepare(nxt, other, 1)
                        prepare(nxt, other, 2)
                        prepare(nxt, other, s.T)
                pair_steps(act, body)
                take_out(s.fin((PAIRS - 1, 0, None), 0))

            def mlp(s):
                c = COLS[s.name]
                for f in range(FT):
                    it = s.gate(f)
                    w = filled(it)
                    if s.gated:
                        if f >= 2:
                            before = s.up(f - 2)
                            act.wait_ge(work_free[before.slot], before.free())
                        dst, b = gbuf[:, f % 2, :], c + FT + f
                    else:
                        dst, b = actT[:, f, :], c + f
                    act.activation(dst, w[:, :, :], ACT.Gelu, bias=cols[:, b:b + 1]).then_inc(work_free[it.slot], 1)

            norm_no = {s.name: i for i, s in enumerate([s for s in sections if isinstance(s, Norm) and s.name])}
            for s in sections:
                if isinstance(s, Norm):
                    norm(s)
                if isinstance(s, Small):
                    small(s)
                if isinstance(s, Cross):
                    cross(s)
                elif isinstance(s, Big):
                    big(s)
                if isinstance(s, Mlp):
                    mlp(s)

        @block.vector
        def _(dve):
            steps = [0]

            def link(ins):
                steps[0] += 1
                ins.then_inc(vec, 1)
                dve.wait_ge(vec, steps[0])

            def filled(it):
                dve.wait_ge(work_full, it.full())
                return work[it.slot]

            def row(name, k=TILES):
                return rows[:, ROWV[name], :].unsqueeze(1).to_broadcast([P, k, D])

            def tiles(ap):
                return ap.rearrange("p b (t d) -> p (b t) d", d=D)

            def norm(s, add):
                if s.name:
                    src = x_res if s.src == "x" else att
                    for t in range(TILES):
                        ins = dve.bn_stats(stats[:, t, :], src[:, t, :])
                    link(ins)
                    for t in range(TILES):
                        ins = dve.bn_aggr(mv[:, t, :], stats[:, t, :])
                    ins.then_inc(var_done, 1)
                    dve.wait_ge(std_done, norm_no[s.name] + 1)
                    link(dve.reciprocal(rstd[:], std[:]))
                    dve.scalar_tensor_tensor(shift_z[:], mv[:, :, 0], -1.0, rstd[:], ALU.mult, ALU.mult).then_inc(rstd_done, 1)
                    for t in range(TILES):
                        if t not in ACT_TILES:
                            ins = dve.tensor_scalar(z[:, t, :], src[:, t, :], mv[:, t, 0:1], rstd[:, t:t + 1],
                                                    ALU.subtract, ALU.mult)
                        if t % QT == QT - 1:
                            ins.then_inc(z_done, 1)
                    dve.wait_ge(z_done, z_count[s.name] + 2)
                    dve.wait_ge(z_act, z_count[s.name] + 2)
                add_rows(add)

            def add_rows(add):
                for what in add:
                    link(dve.tensor_tensor(x_res[:], x_res[:], att[:] if what == "att" else row(what), ALU.add))

            def add_out(it, into, name=None):
                w = filled(it)
                if into == "x":
                    ins = dve.tensor_tensor(x_res[:], x_res[:], tiles(w[:, :, :]), ALU.add)
                else:
                    ins = dve.tensor_tensor(att[:], tiles(w[:, :, :]), row(name), ALU.add)
                ins.then_inc(work_free[it.slot], 1)
                dve.wait_ge(work_free[it.slot], it.free())

            def small(s):
                it = s.items["V", 0, 0]
                w = filled(it)
                kw, vt = (S, B) if s.ctx else (P, TILES)
                src = (w[0:S, :, 0:D] if s.ctx else tiles(w[:, :, :])).rearrange("p t (h d) -> p t h d", d=HS)
                bias = rows[0:kw, ROWV[s.name + "v"], :].rearrange("p (h d) -> p h d", d=HS)
                dve.memset(vs[0:kw, 0:vt, :, HS:HS + 1], 1.0)
                for t in range(vt):
                    ins = dve.tensor_tensor(vs[0:kw, t, :, 0:HS], src[:, t], bias, ALU.add)
                ins.then_inc(work_free[it.slot], 1)
                dve.wait_ge(work_free[it.slot], it.free())
                if s.masked:
                    keep = ckeep if s.ctx else tkeep
                    for t in range(vt):
                        ins = dve.tensor_scalar(vs[0:kw, t, :, 0:HS + 1], vs[0:kw, t, :, 0:HS + 1], keep[0:kw, t:t + 1],
                                                None, ALU.mult)
                    ins.then_inc(v_done, 1)

                def split(n):
                    for k in range(2):
                        j = s.qk0 + 2 * n + k
                        w_ = N if k == 0 or not s.ctx else B * SP_
                        c = COLS["nselq" if k == 0 else "nselk"]
                        it = s.items["QK"[k], n, 0]
                        dve.wait_ge(work_free[it.slot], it.free())
                        for h in range(4 if k else 1):
                            r = slice(h * ROWS, (h + 1) * ROWS) if k else slice(0, P)
                            dst = ks[n % 2][r, h, 0:w_] if k else qs[:, n % 2, :]
                            ins = dve.scalar_tensor_tensor(dst, half[r, j % 2, 0:w_], cols[r, c:c + 1],
                                                           full[r, j % 2, 0:w_], ALU.mult, ALU.add)
                        ins.then_inc(qk_done, 1)

                def largest(n, k):
                    b, part, qt = s.m_list[k]
                    it = s.items["M", n, k]
                    w = filled(it)
                    if s.ctx:
                        src = w[:, :, 0:4 * SP_].rearrange("p t (h c) -> p t h c", c=SP_)[..., 0:S]
                        dst = mneg[:, b * QT + 2 * part:b * QT + 2 * part + 2, 0:4]
                    else:
                        src = w[:, :, 0:(qt + 1) * P]
                        dst = mneg[:, b * QT + qt, 2 * part:2 * part + 2]
                    dve.tensor_reduce(dst, src, AX.X, ALU.max, negate=True).then_inc(work_free[it.slot], 1)

                def divide_small(n):
                    it = s.items["N", n, 0]
                    w = tiles(filled(it)[:, :, :]).rearrange("p t (h c) -> p t h c", c=ROWS)
                    r = recip4[:]
                    if n:
                        before = s.items["N", n - 1, 0]
                        dve.wait_ge(work_free[before.slot], before.free())
                    link(dve.reciprocal(r, w[..., HS]))
                    dst = on[:, :, n * ROWS:(n + 1) * ROWS].rearrange("p t (h c) -> p t h c", c=HS)
                    dve.tensor_tensor(dst, w[..., 0:HS], r.unsqueeze(3).to_broadcast([P, TILES, 4, HS]),
                                      ALU.mult).then_inc(work_free[it.slot], 1)

                split(0)
                for k in range(len(s.m_list)):
                    largest(0, k)
                for n in range(QUADS):
                    if n + 1 < QUADS:
                        if n:
                            dve.wait_ge(st_full, 2 * (s.unit0 + n * len(s.units)))
                        split(n + 1)
                    for u, items in enumerate(s.with_units(n)):
                        for item in items:
                            if item[0] == "M":
                                largest(n + 1, item[2])
                            elif item[0] == "N":
                                divide_small(n - 1)
                divide_small(QUADS - 1)
                add_out(s.items["O", 0, 0], s.into, s.name + "o")

            def divide(s, steps0, n, b):
                dve.wait_ge(o_full, count(s.o0 + b + 1, n, 2))
                o = oacc[:, :, 0:QT * (HB + 1)].rearrange("p h (t c) -> p h t c", t=QT)
                r = recip[:].rearrange("p a t h -> p (a t h)")[:, 0:2 * QT].rearrange("p (h t) -> p h t", h=2)
                dve.reciprocal(r, o[:, :, :, HB]).then_inc(vec, 1)
                dve.wait_ge(vec, count(steps0 + b + 1, n, 2))
                for h in range(2):
                    ins = dve.tensor_tensor(on[:, b * QT:(b + 1) * QT, h * HB:(h + 1) * HB], o[:, h, :, 0:HB],
                                            r[:, h, :].unsqueeze(2).to_broadcast([P, QT, HB]), ALU.mult)
                ins.then_inc(o_taken, 1)

            def scale(s, steps0, n):
                it = s.fin(n, 0)
                w = filled(it)
                blocks = den_t.rearrange("p (k c) -> p k c", c=32)
                dve.transpose(den_t, w[:, :, :].rearrange("p b c -> p (b c)")).then_inc(work_free[it.slot], 1)
                dve.wait_ge(work_free[it.slot], it.free())
                dve.reciprocal(den_c[:], blocks[:, :, 0]).then_inc(vec, 1)
                dve.wait_ge(vec, count(steps0 + 1, n, 2))
                dve.transpose(den_r, den_c[:].unsqueeze(2).to_broadcast([P, N // 32, 32])).then_inc(vec, 1)
                dve.wait_ge(vec, count(steps0 + 2, n, 2))
                dve.wait_ge(o_taken, count(s.o0 + 2, n, 2))
                dve.tensor_tensor(onT[:], raw, den_r, ALU.mult).then_inc(scaled, 1)

            def sum_out(s, n):
                it = s.fin(n, 1)
                w = filled(it)
                dve.tensor_tensor(x_res[:], x_res[:], tiles(w[:, :, :]), ALU.add).then_inc(work_free[it.slot], 1)
                dve.wait_ge(work_free[it.slot], it.free())

            def big(s):
                steps0 = steps[0]

                def prepare(n, buf, k):
                    it = s.prep(n, k)
                    if k < 2:
                        dve.wait_ge(hi_done, count(2 * (s.hi0 + k + 1), n, 4))
                        w = work[it.slot]
                        for h, r in ((0, slice(0, HB)), (1, slice(HB, P))):
                            other = slice(HB, P) if h == 0 else slice(0, HB)
                            if k == 0:
                                hi, lo = q2[r, buf, h, :], q1[other, buf, h, :]
                            else:
                                hi, lo = k1[r, buf, h, :], k2[r, buf, h, :]
                            dve.tensor_tensor(lo.rearrange("p (b c) -> p b c", b=2), w[r, :, :],
                                              hi.rearrange("p (b c) -> p b c", b=2).bitcast(F32), ALU.subtract)
                            ins = dve.tensor_copy(q1[r, buf, h, :] if k == 0 else k1[other, buf, h, :], hi)
                        ins.then_inc(work_free[it.slot], 1)
                    else:
                        w = filled(it)
                        dve.tensor_reduce(mneg[:, k - 3, 0:HB + 1:HB], w[:, :, :], AX.X, ALU.max,
                                          negate=True).then_inc(work_free[it.slot], 1)

                ms = list(range(3, 3 + s.ms))
                dve.wait_ge(big_ready, 5)
                for k in [0, 1] + ms:
                    prepare((0, 0, None), 0, k)

                def body(n, buf, first, last):
                    nxt, prev, other = shift(n, 1), shift(n, -1), 1 - buf
                    if not last:
                        prepare(nxt, other, 0)
                        prepare(nxt, other, 1)
                        prepare(nxt, other, ms[0])
                    if not first:
                        sum_out(s, prev)
                    if not last:
                        for k in ms[1:]:
                            prepare(nxt, other, k)
                    scale(s, steps0, n)
                pair_steps(dve, body)
                steps[0] += 2 * PAIRS
                sum_out(s, (PAIRS - 1, 0, None))

            def cross(s):
                steps0 = steps[0]
                before = Item(s.item0 - 1)
                dve.wait_ge(work_free[before.slot], before.free())
                dve.tensor_tensor(h_lo, hT[:], h_hi.bitcast(F32), ALU.subtract).then_inc(h_split, 1)

                def prepare(n, k):
                    it = s.prep(n, k)
                    if k == 2:
                        dve.wait_ge(hi_done, count(2 * (s.hi0 + 1), n, 2))
                        w = work[it.slot]
                        dve.tensor_tensor(g_lo, w[:, 0, 0:2 * B * SP_], g_hi.bitcast(F32),
                                          ALU.subtract).then_inc(work_free[it.slot], 1)
                    else:
                        w = filled(it)
                        b = k - 3
                        src = w[:, :, 0:4 * SP_].rearrange("p a (t h c) -> p a t h c", t=2, h=2)[..., 0:S]
                        dst = mneg[:, b * QT:(b + 1) * QT, 0:HB + 1:HB].rearrange("p (a t) h -> p a t h", a=2)
                        dve.tensor_reduce(dst, src, AX.X, ALU.max, negate=True).then_inc(work_free[it.slot], 1)

                for k in (2, 3, 4):
                    prepare((0, 0, None), k)

                def body(n, buf, first, last):
                    nxt, prev = shift(n, 1), shift(n, -1)
                    if not last:
                        for k in (2, 3, 4):
                            prepare(nxt, k)
                    divide(s, steps0, n, 0)
                    if not first:
                        sum_out(s, prev)
                    divide(s, steps0, n, 1)
                pair_steps(dve, body)
                steps[0] += 2 * PAIRS
                sum_out(s, (PAIRS - 1, 0, None))

            def mlp(s):
                if s.gated:
                    for f in range(FT):
                        it, g = s.up(f), s.gate(f)
                        w = filled(it)
                        dve.wait_ge(work_free[g.slot], g.free())
                        c = COLS[s.name] + f
                        dve.scalar_tensor_tensor(actT[:, f, :].rearrange("p (b c) -> p b c", b=2), w[:, :, :], cols[:, c:c + 1],
                                                 gbuf[:, f % 2, :].rearrange("p (b c) -> p b c", b=2), ALU.add,
                                                 ALU.mult).then_inc(work_free[it.slot], 1)
                add_out(s.out(), "x")

            norm_no = {s.name: i for i, s in enumerate([s for s in sections if isinstance(s, Norm) and s.name])}
            z_count, _ = counts(sections)
            dve.wait_ge(x_loaded, 16)
            adds = {"l0n1": ["l0sao"], "l0n2": ["l0cao"], "l0n3": ["l0b2"], "l1n": ["att", "l1b2"],
                    "l2n1": ["l2sao"], "l2n2": ["l2cao"], "l2n3": ["l2b2"],
                    "l3n1": ["l3sao"], "l3n2": ["l3cao"], "l3n3": ["l3b2"], None: []}
            for i, s in enumerate(sections):
                if isinstance(s, Norm):
                    norm(s, adds[s.name] if i else [])
                if i == 0:
                    dve.wait_ge(consts_loaded, 16 * 7)
                    dve.tensor_scalar(tmask[:], tm8[:], -BIG, None, ALU.mult).then_inc(masks_made, 1)
                    dve.tensor_scalar(cmask[:], cm8[:], -BIG, None, ALU.mult).then_inc(masks_made, 1)
                    dve.tensor_scalar(tkeep[:], tc8[:], -1.0, 1.0, ALU.mult, ALU.add).then_inc(masks_made, 1)
                    dve.tensor_scalar(ckeep[0:S, :], cc8[0:S, :], -1.0, 1.0, ALU.mult, ALU.add).then_inc(masks_made, 1)
                    dve.wait_ge(masks_made, 4)
                    add_rows(adds[s.name])
                    dve.wait_ge(made, MADE)
                if isinstance(s, Small):
                    small(s)
                if isinstance(s, Cross):
                    cross(s)
                elif isinstance(s, Big):
                    big(s)
                if isinstance(s, Mlp):
                    mlp(s)


def counts(sections):
    z_count, v_count, z, v = {}, {}, 0, 0
    for s in sections:
        if isinstance(s, Norm) and s.name:
            z_count[s.name] = z
            z += 2
        if isinstance(s, Small):
            v += s.masked
            v_count[s.name] = v
    return z_count, v_count


def kernel(**a):
    import numpy as np
    import concourse.bacc as bacc
    from concourse import mybir as mb
    from concourse.bass_utils import run_bass_kernel_spmd as run

    f = {k: np.asarray(v) for k, v in a.items()}

    def norm_names(layer, i):
        return {"l0": ("L0_xattn_ln%d_w" % i, "L0_xattn_ln%d_b" % i), "l1": ("L1_xattn_ln_g", "L1_xattn_ln_b")}.get(
            layer, ("%s_xattn_ln%d_g" % (layer.upper(), i), "%s_xattn_ln%d_b" % (layer.upper(), i)))

    cols = np.zeros((P, NCOLS), np.float32)
    for name in LN_NAMES:
        g, b = norm_names(name[:2], int(name[3:] or 1))
        cols[:, COLS[name + "g"]] = f[g]
        cols[:, COLS[name + "b"]] = f[b]
    for name, src in (("l0m", "L0_xattn_mlp1_b"), ("l1m", "L1_xattn_b1"), ("l2m", "L2_xattn_ff_b1"), ("l3m", "L3_xattn_ff_b1")):
        v = f[src].reshape(-1, P).T
        cols[:, COLS[name]:COLS[name] + v.shape[1]] = v

    def blocks(w):
        out = np.zeros(w.shape[:-1] + (H, ROWS), np.float32)
        for r in range(3):
            out[..., r * HS:(r + 1) * HS] = w.reshape(w.shape[:-1] + (H, HS))
        return out.reshape(w.shape[:-1] + (H * ROWS,))

    def bias_cols(name, b, ones_row):
        v = blocks(b).reshape(H, ROWS)
        v[:, ones_row] = 1.0
        cols[:, COLS[name]:COLS[name] + QUADS] = v.reshape(QUADS, P).T

    l0 = "L0_xattn_"
    l1 = "L1_xattn_"
    qkv_w, qkv_b = f[l0 + "qkv_w"], f[l0 + "qkv_b"]
    small = {
        "l0sa": (qkv_w[:, 0:D], qkv_w[:, D:2 * D], qkv_w[:, 2 * D:], f[l0 + "proj_w"],
                 qkv_b[0:D], qkv_b[D:2 * D], qkv_b[2 * D:], f[l0 + "proj_b"]),
        "l0ca": tuple(f[l0 + n] for n in ("q_w", "k_w", "v_w", "out_w", "q_b", "k_b", "v_b", "out_b")),
        "l1ca": tuple(f[l1 + n] for n in ("Wq", "Wk", "Wv", "Wo", "bq", "bk", "bv", "bo")),
    }
    rows = np.zeros((P, len(ROW_NAMES), D), np.float32)
    wts = np.zeros((P, NWTS), np.float32)
    for name, (wq, wk, wv, wo, bq, bk, bv, bo) in small.items():
        bias_cols(name + "q", bq, ROW_MASK)
        bias_cols(name + "k", bk, ROW_MAX)
        rows[:, ROWV[name + "v"]] = bv
        rows[:, ROWV[name + "o"]] = bo
        for p, w in (("q", blocks(wq)), ("k", blocks(wk)), ("v", wv), ("o", wo)):
            wts[0:w.shape[0], WTS[name + p]:WTS[name + p] + w.shape[1]] = w
    for name, src in (("l2sao", "L2_xattn_sa_bo"), ("l2cao", "L2_xattn_ca_bo"), ("l3sao", "L3_xattn_a1_bo"),
                      ("l3cao", "L3_xattn_a2_bo"), ("l0b2", "L0_xattn_mlp2_b"), ("l1b2", "L1_xattn_b2"),
                      ("l2b2", "L2_xattn_ff_b2"), ("l3b2", "L3_xattn_ff_b2")):
        rows[:, ROWV[name]] = f[src]
    for name, w1, w2 in (("l0m", l0 + "mlp1_w", l0 + "mlp2_w"), ("l1m", l1 + "W1", l1 + "W2"),
                         ("l2m", "L2_xattn_ff_w1", "L2_xattn_ff_w2"), ("l3m", "L3_xattn_ff_w1", "L3_xattn_ff_w2")):
        w = f[w1]
        wts[:, WTS[name + "1"]:WTS[name + "1"] + w.shape[1]] = w
        w = f[w2].reshape(FT, P, D).transpose(1, 0, 2).reshape(P, F)
        wts[:, WTS[name + "2"]:WTS[name + "2"] + F] = w
    nsel = np.zeros((2, 4, ROWS), np.float32)
    nsel[0, :, 2 * HS:3 * HS] = -1.0
    nsel[1, :, HS:2 * HS] = -1.0
    cols[:, COLS["nselq"]] = nsel[0].reshape(-1)
    cols[:, COLS["nselk"]] = nsel[1].reshape(-1)

    ctxT = np.zeros((DC, B, SP_), np.float32)
    ctxT[:, :, 0:S] = f["ctx_768"].transpose(2, 0, 1)
    tm = f["mask_BxS_bf0"]
    cm = f["mask_BxS2_bf0"]
    cm_row = np.zeros((1, B, SP_), bool)
    cm_row[0, :, 0:S] = cm

    arrays = {
        "x_in": f["x"].reshape(N, D), "ctx_in": ctxT.reshape(DC, B * SP_),
        "tmask_row": tm.reshape(1, N), "tmask_col": np.ascontiguousarray(tm.reshape(TILES, P).T),
        "cmask_row": cm_row.reshape(1, B * SP_), "cmask_col": np.ascontiguousarray(cm.T),
        "cols_in": cols, "rows_in": rows, "wts_in": wts,
    }
    big_names = {"l2sa": "L2_xattn_sa_w", "l2ca": "L2_xattn_ca_w", "l3sa": "L3_xattn_a1_w", "l3ca": "L3_xattn_a2_w"}
    for n, src in big_names.items():
        for p in "qkvo":
            arrays[n + p] = f[src + p].T if n + p in ("l2caq", "l3caq") else f[src + p]
    nc = bacc.Bacc("TRN2", target_bir_lowering=False, num_devices=1)
    ap = {}
    for n, v in arrays.items():
        arrays[n] = np.ascontiguousarray(v)
        ap[n] = nc.dram_tensor(n, v.shape, mb.dt.from_np(v.dtype), kind="ExternalInput").ap()
    out = nc.dram_tensor("out", (N, D), mb.dt.float32, kind="ExternalOutput").ap()
    big = {n: tuple(ap[n + p] for p in "qkvo") for n in big_names}
    program(nc, ap["x_in"], ap["ctx_in"], ap["tmask_row"], ap["tmask_col"], ap["cmask_row"], ap["cmask_col"],
            ap["cols_in"], ap["rows_in"], ap["wts_in"], big, out)
    r = run(nc, [arrays], core_ids=[0])
    return r.results[0]["out"].reshape(B, T, D)
```
